# Optimizing a Trainium2 kernel written in Bass

```python
import numpy as np
import jax
import jax.numpy as jnp

def _softmax(x, axis=-1):
    return jax.nn.softmax(x, axis=axis)

def _gelu(x):
    return jax.nn.gelu(x, approximate=True)

def _silu(x):
    return jax.nn.silu(x)

def _sigmoid(x):
    return jax.nn.sigmoid(x)

def _layernorm(x, axis=-1, eps=1e-05):
    m = jnp.mean(x, axis=axis, keepdims=True)
    v = jnp.var(x, axis=axis, keepdims=True)
    return (x - m) / jnp.sqrt(v + eps)

def _scatter_add(tgt, idx, src, axis=0):
    return tgt.at[idx].add(src)

def _segment_sum(src, seg, n):
    return jax.ops.segment_sum(src, seg, n)
kernel_name = 'mk_perceiver_d2_seqx_r8_de21b9'

def setup_inputs(seed: int=0):
    np.random.seed(seed)
    _w = jnp.asarray

    def _rec_inputs():
        import jax
        import jax.numpy as jnp
        _rk = jax.random.key(seed)
        x = -0.0003929 + 0.9999 * jax.random.normal(jax.random.fold_in(_rk, 1), (4, 128, 128), jnp.float32)
        _lenS = 128 - jax.random.randint(jax.random.fold_in(_rk, 7), (4,), 0, max(1, 128 // 4) + 1, jnp.int32)
        _lenS2 = 2048 - jax.random.randint(jax.random.fold_in(_rk, 8), (4,), 0, max(1, 2048 // 4) + 1, jnp.int32)
        _ctx_2048P = jax.random.normal(jax.random.fold_in(_rk, 11), (4, 16, 256), jnp.float32)
        _ctx_2048c = jax.random.dirichlet(jax.random.fold_in(_rk, 511), 0.3 * jnp.ones((16,), jnp.float32), (4, 2048))
        _ctx_2048t = jnp.einsum('bsk,bkd->bsd', _ctx_2048c, _ctx_2048P)
        _ctx_2048t = _ctx_2048t * jax.lax.rsqrt(jnp.mean(jnp.square(_ctx_2048t)) + 1e-12) * 0.953939
        ctx_2048 = 4.13588e-05 + 0.999923 * (_ctx_2048t + 0.3 * jax.random.normal(jax.random.fold_in(_rk, 611), (4, 2048, 256), jnp.float32))
        _validS = jnp.arange(128)[None, :] < _lenS[:, None]
        _validS2 = jnp.arange(2048)[None, :] < _lenS2[:, None]
        _causal = jnp.tril(jnp.ones((128, 128), dtype=bool))
        mask_BxS2_if0 = jnp.where(jnp.ones((4, 2048), dtype=bool), 4, 0).astype(jnp.int32)
        return (x, ctx_2048, mask_BxS2_if0)
    x, ctx_2048, mask_BxS2_if0 = _rec_inputs()

    def _L0_xattn_setup():
        import jax, jax.numpy as jnp
        import numpy as np
        B, L, P = (4, 512, 128)
        D_MODEL = 128
        D_GLOBAL = 256
        HEADDIM = 32
        EPSILON = 0.001
        RMS_EPS = 1e-05

        def rmsnorm(x, g, eps=RMS_EPS):
            var = jnp.mean(jnp.square(x), axis=-1, keepdims=True)
            return x * jax.lax.rsqrt(var + eps) * g

        def _hnet_depool(h, h_patch_full, patch_lens):
            h_patch = h_patch_full[..., :D_MODEL]
            bsz, plen = (h_patch.shape[0], h_patch.shape[1])
            seqlen = h.shape[1]
            logp = jnp.full((bsz, plen), -EPSILON, dtype=jnp.float32)
            bidx = jnp.cumsum(patch_lens, axis=1) - 1
            boundary_mask = jnp.zeros((bsz, seqlen), dtype=jnp.int32)
            boundary_mask = boundary_mask.at[jnp.arange(bsz)[:, None], bidx].set(1)
            dt = (-jnp.log(-jnp.expm1(logp))).astype(h_patch.dtype)
            x = h_patch / dt[..., None]
            n_heads = D_MODEL // HEADDIM
            A = -jnp.ones((n_heads,), dtype=jnp.float32)
            bcoef = jnp.exp(logp).astype(h_patch.dtype)
            x4 = x.reshape(bsz, plen, n_heads, HEADDIM)
            a = jnp.exp(dt[:, :, None] * A[None, None, :])
            u = (dt * bcoef)[:, :, None, None] * x4
            a_b = jnp.broadcast_to(a[..., None], u.shape)

            def comb(lft, rgt):
                aL, uL = lft
                aR, uR = rgt
                return (aL * aR, uL * aR + uR)
            _, s = jax.lax.associative_scan(comb, (a_b, u), axis=1)
            depool = s.reshape(bsz, plen, D_MODEL)
            plug = jnp.clip(jnp.cumsum(boundary_mask, axis=1) - 1, 0, plen - 1)
            depool_out = depool[jnp.arange(bsz)[:, None], plug]
            return depool_out + h
        key = jax.random.key(seed)
        k1, k2, k3, k4 = jax.random.split(key, 4)
        embeds = jax.random.normal(k1, (B, L, D_MODEL), dtype=jnp.float32)
        patch_embeds = jax.random.normal(k2, (B, P, D_GLOBAL), dtype=jnp.float32)
        patch_lens = jnp.full((B, P), L // P, dtype=jnp.int64)
        W_in = jax.random.normal(k3, (D_MODEL, D_MODEL), dtype=jnp.float32) * 0.02
        b_in = jnp.zeros((D_MODEL,), dtype=jnp.float32)
        g_res = jnp.ones((D_MODEL,), dtype=jnp.float32)
        g_init = jnp.ones((D_GLOBAL,), dtype=jnp.float32)
        return {'embeds': embeds, 'patch_embeds': patch_embeds, 'patch_lens': patch_lens, 'W_in': W_in, 'b_in': b_in, 'g_res': g_res, 'g_init': g_init}
    _L0_xattn_all = _L0_xattn_setup()
    _L0_xattn_in = {k: v for k, v in _L0_xattn_all.items() if k in ('W_in', 'b_in', 'g_res', 'g_init')}
    del _L0_xattn_all

    def _L0_attn_setup():
        import jax, jax.numpy as jnp
        import numpy as np
        B, S, HID = (4, 256, 128)
        E, K, H = (8, 2, 8)
        DK = HID // H
        DV = HID // H
        CAP = int(S * 1.0)
        CHUNK = 64
        EPS = 1e-05

        def chunk_linear_attn(q, k, v):
            Bt, T, Hh, Dk = q.shape
            Dv = v.shape[-1]
            nc = T // CHUNK
            q = q * Dk ** (-0.5)
            qc = q.reshape(Bt, nc, CHUNK, Hh, Dk).transpose(1, 0, 2, 3, 4)
            kc = k.reshape(Bt, nc, CHUNK, Hh, Dk).transpose(1, 0, 2, 3, 4)
            vc = v.reshape(Bt, nc, CHUNK, Hh, Dv).transpose(1, 0, 2, 3, 4)
            causal = jnp.tril(jnp.ones((CHUNK, CHUNK), q.dtype))

            def step(Sst, qkv):
                qb, kb, vb = qkv
                attn = jnp.einsum('bihd,bjhd->bhij', qb, kb) * causal
                intra = jnp.einsum('bhij,bjhe->bihe', attn, vb)
                inter = jnp.einsum('bihd,bhde->bihe', qb, Sst)
                Sst = Sst + jnp.einsum('bjhd,bjhe->bhde', kb, vb)
                return (Sst, intra + inter)
            S0 = jnp.zeros((Bt, Hh, Dk, Dv), q.dtype)
            _, o = jax.lax.scan(step, S0, (qc, kc, vc))
            return o.transpose(1, 0, 2, 3, 4).reshape(Bt, T, Hh, Dv)

        def _forward(x, gate_w, q_w, k_w, v_w, fmq1_w, fmq2_w, fmk1_w, fmk2_w, norm_w, o_w):
            b, s0, d = x.shape
            logits = jnp.einsum('bsd,ed->bse', x, gate_w)
            scores = jax.nn.softmax(logits.astype(jnp.float32), axis=-1)
            rw, sel = jax.lax.top_k(scores, K)
            rw = (rw / rw.sum(-1, keepdims=True)).astype(x.dtype)
            routing_mask = jax.nn.one_hot(sel, E, dtype=jnp.int32).sum(2)
            s = s0 * K
            x_rep = jnp.repeat(x, K, axis=1).reshape(b * s, d)
            sel_flat = sel.reshape(b * s).astype(jnp.int32)
            batch_idx = jnp.repeat(jnp.arange(b, dtype=jnp.int32), s)
            combined = batch_idx * E + sel_flat
            sorted_indices = jnp.argsort(combined)
            x_sorted = x_rep[sorted_indices]
            tokens = routing_mask.sum(axis=1)
            flat_off = (jnp.cumsum(tokens, axis=1) + (jnp.arange(b, dtype=jnp.int32) * s)[:, None]).reshape(-1)
            starts = jnp.concatenate([jnp.zeros((1,), flat_off.dtype), flat_off[:-1]])
            idx = starts[:, None] + jnp.arange(CAP, dtype=flat_off.dtype)[None, :]
            shift = jnp.maximum(tokens.reshape(-1) - CAP, 0)
            tidx = idx + shift[:, None]
            dmask = tidx < flat_off[:, None]
            tidx = jnp.where(dmask, tidx, 0)
            xe = x_sorted[tidx.reshape(-1)].reshape(b * E, CAP, d) * dmask[..., None].astype(x.dtype)
            xe = xe.reshape(b, E, CAP, d).transpose(1, 0, 2, 3)
            q = jnp.einsum('ebtc,kc->ebtk', xe, q_w).reshape(E, b, CAP, H, DK)
            k = jnp.einsum('ebtc,ekc->ebtk', xe, k_w).reshape(E, b, CAP, H, DK)
            v = jnp.einsum('ebtc,ekc->ebtk', xe, v_w).reshape(E, b, CAP, H, DV)
            q = jnp.einsum('...d,kd->...k', q, fmq1_w) * jnp.einsum('...d,kd->...k', q, fmq2_w)
            k = jnp.einsum('...d,kd->...k', k, fmk1_w) * jnp.einsum('...d,kd->...k', k, fmk2_w)
            o = chunk_linear_attn(q.reshape(E * b, CAP, H, DK), k.reshape(E * b, CAP, H, DK), v.reshape(E * b, CAP, H, DV))
            oflat = o.reshape(E, b, CAP, H, DV).transpose(1, 0, 2, 3, 4).reshape(b * E * CAP, H, DV)
            oflat = oflat * dmask.reshape(-1)[:, None, None].astype(o.dtype)
            res = jnp.zeros((b * s, H, DV), o.dtype).at[tidx.reshape(-1)].add(oflat)
            inv = jnp.argsort(sorted_indices)
            restored = res[inv].reshape(b, s0, K, H, DV)
            out = (restored * rw[..., None, None]).sum(axis=2)
            out = out * jax.lax.rsqrt(jnp.mean(out * out, axis=-1, keepdims=True) + EPS) * norm_w
            out = out.reshape(b, s0, H * DV)
            return jnp.einsum('bsv,dv->bsd', out, o_w)
        key = jax.random.key(seed)
        ks = jax.random.split(key, 12)
        std = 0.02
        return {'x': jax.random.normal(ks[0], (B, S, HID), jnp.float32), 'gate_w': jax.random.normal(ks[1], (E, HID), jnp.float32) * std, 'q_w': jax.random.normal(ks[2], (HID, HID), jnp.float32) * std, 'k_w': jax.random.normal(ks[3], (E, HID, HID), jnp.float32) * std, 'v_w': jax.random.normal(ks[4], (E, HID, HID), jnp.float32) * std, 'fmq1_w': jax.random.normal(ks[5], (DK, DK), jnp.float32) * std, 'fmq2_w': jax.random.normal(ks[6], (DK, DK), jnp.float32) * std, 'fmk1_w': jax.random.normal(ks[7], (DK, DK), jnp.float32) * std, 'fmk2_w': jax.random.normal(ks[8], (DK, DK), jnp.float32) * std, 'norm_w': jnp.ones((DV,), jnp.float32), 'o_w': jax.random.normal(ks[9], (HID, HID), jnp.float32) * std}
    _L0_attn_all = _L0_attn_setup()
    _L0_attn_in = {k: v for k, v in _L0_attn_all.items() if k in ('gate_w', 'q_w', 'k_w', 'v_w', 'fmq1_w', 'fmq2_w', 'fmk1_w', 'fmk2_w', 'norm_w', 'o_w')}
    del _L0_attn_all

    def _L0_ffn_setup():
        import jax, jax.numpy as jnp
        import numpy as np
        B, L, D = (4, 64, 128)
        E, TOP_K = (16, 4)
        F = 4 * D
        key = jax.random.key(seed)
        ks = jax.random.split(key, 6)
        scale = 0.02
        return {'x': jax.random.normal(ks[0], (B, L, D), jnp.float32), 'keys': jax.random.normal(ks[1], (E, D), jnp.float32), 'w1': jax.random.normal(ks[2], (E, F, D), jnp.float32) * scale, 'b1': jnp.zeros((E, F), jnp.float32), 'w2': jax.random.normal(ks[3], (E, D, F), jnp.float32) * scale, 'b2': jnp.zeros((E, D), jnp.float32), 'rw': jax.random.normal(ks[4], (E, D), jnp.float32) * scale, 'rb': jnp.zeros((E,), jnp.float32)}
    _L0_ffn_all = _L0_ffn_setup()
    _L0_ffn_in = {k: v for k, v in _L0_ffn_all.items() if k in ('keys', 'w1', 'b1', 'w2', 'b2', 'rw', 'rb')}
    del _L0_ffn_all

    def _L1_xattn_setup():
        import jax, jax.numpy as jnp
        import numpy as np
        B, N, DIM = (8, 512, 128)
        M, CTX = (32, 256)
        HEADS, DH = (16, 64)
        INNER = HEADS * DH
        EPS = 1e-06

        def _split_heads(t):
            b, n, _ = t.shape
            return t.reshape(b, n, HEADS, DH).transpose(0, 2, 1, 3)
        key = jax.random.key(seed)
        ks = jax.random.split(key, 6)
        x = jax.random.normal(ks[0], (B, N, DIM), dtype=jnp.float32)
        context = jax.random.normal(ks[1], (B, M, CTX), dtype=jnp.float32)
        Wq = jax.random.normal(ks[2], (DIM, INNER), dtype=jnp.float32) / np.sqrt(DIM)
        Wkv = jax.random.normal(ks[3], (CTX, 2 * INNER), dtype=jnp.float32) / np.sqrt(CTX)
        null_kv = jax.random.normal(ks[4], (2, DH), dtype=jnp.float32) / np.sqrt(2.0)
        Wout = jax.random.normal(ks[5], (INNER, DIM), dtype=jnp.float32) / np.sqrt(INNER)
        ln_scale = jnp.ones((DIM,), dtype=jnp.float32)
        ln_bias = jnp.zeros((DIM,), dtype=jnp.float32)
        return {'x': x, 'context': context, 'Wq': Wq, 'Wkv': Wkv, 'null_kv': null_kv, 'Wout': Wout, 'ln_scale': ln_scale, 'ln_bias': ln_bias}
    _L1_xattn_all = _L1_xattn_setup()
    _L1_xattn_in = {k: v for k, v in _L1_xattn_all.items() if k in ('Wq', 'Wkv', 'null_kv', 'Wout', 'ln_scale', 'ln_bias')}
    del _L1_xattn_all

    def _L1_attn_setup():
        import jax, jax.numpy as jnp
        import numpy as np
        EMBED_DIM = 128
        NUM_HEADS = 16
        HEAD_DIM = EMBED_DIM // NUM_HEADS
        SCALE = HEAD_DIM ** (-0.5)
        B, N = (2, 256)
        key = jax.random.key(seed)
        k1, k2, k3 = jax.random.split(key, 3)
        x = jax.random.normal(k1, (B, N, EMBED_DIM), dtype=jnp.float32)
        w_qkv = jax.random.normal(k2, (EMBED_DIM, 3 * EMBED_DIM), dtype=jnp.float32) * EMBED_DIM ** (-0.5)
        b_qkv = jnp.zeros((3 * EMBED_DIM,), dtype=jnp.float32)
        w_proj = jax.random.normal(k3, (EMBED_DIM, EMBED_DIM), dtype=jnp.float32) * EMBED_DIM ** (-0.5)
        b_proj = jnp.zeros((EMBED_DIM,), dtype=jnp.float32)
        return {'x': x, 'w_qkv': w_qkv, 'b_qkv': b_qkv, 'w_proj': w_proj, 'b_proj': b_proj}
    _L1_attn_all = _L1_attn_setup()
    _L1_attn_in = {k: v for k, v in _L1_attn_all.items() if k in ('w_qkv', 'b_qkv', 'w_proj', 'b_proj')}
    del _L1_attn_all

    def _L1_ffn_setup():
        import jax, jax.numpy as jnp
        import numpy as np
        TOP_K = 2
        key = jax.random.key(seed)
        ks = jax.random.split(key, 5)
        B, T, D, F, E = (4, 256, 128, 512, 8)
        s = 0.02
        return {'x': jax.random.normal(ks[0], (B, T, D), jnp.float32), 'gate_w': jax.random.normal(ks[1], (D, E), jnp.float32) * s, 'w1': jax.random.normal(ks[2], (E, D, F), jnp.float32) * s, 'w3': jax.random.normal(ks[3], (E, D, F), jnp.float32) * s, 'w2': jax.random.normal(ks[4], (E, F, D), jnp.float32) * s}
    _L1_ffn_all = _L1_ffn_setup()
    _L1_ffn_in = {k: v for k, v in _L1_ffn_all.items() if k in ('gate_w', 'w1', 'w3', 'w2')}
    del _L1_ffn_all
    return {'x': x, 'ctx_2048': ctx_2048, 'mask_BxS2_if0': mask_BxS2_if0, 'L0_xattn_W_in': _L0_xattn_in['W_in'], 'L0_xattn_b_in': _L0_xattn_in['b_in'], 'L0_xattn_g_res': _L0_xattn_in['g_res'], 'L0_xattn_g_init': _L0_xattn_in['g_init'], 'L0_attn_gate_w': _L0_attn_in['gate_w'], 'L0_attn_q_w': _L0_attn_in['q_w'], 'L0_attn_k_w': _L0_attn_in['k_w'], 'L0_attn_v_w': _L0_attn_in['v_w'], 'L0_attn_fmq1_w': _L0_attn_in['fmq1_w'], 'L0_attn_fmq2_w': _L0_attn_in['fmq2_w'], 'L0_attn_fmk1_w': _L0_attn_in['fmk1_w'], 'L0_attn_fmk2_w': _L0_attn_in['fmk2_w'], 'L0_attn_norm_w': _L0_attn_in['norm_w'], 'L0_attn_o_w': _L0_attn_in['o_w'], 'L0_ffn_keys': _L0_ffn_in['keys'], 'L0_ffn_w1': _L0_ffn_in['w1'], 'L0_ffn_b1': _L0_ffn_in['b1'], 'L0_ffn_w2': _L0_ffn_in['w2'], 'L0_ffn_b2': _L0_ffn_in['b2'], 'L0_ffn_rw': _L0_ffn_in['rw'], 'L0_ffn_rb': _L0_ffn_in['rb'], 'L1_xattn_Wq': _L1_xattn_in['Wq'], 'L1_xattn_Wkv': _L1_xattn_in['Wkv'], 'L1_xattn_null_kv': _L1_xattn_in['null_kv'], 'L1_xattn_Wout': _L1_xattn_in['Wout'], 'L1_xattn_ln_scale': _L1_xattn_in['ln_scale'], 'L1_xattn_ln_bias': _L1_xattn_in['ln_bias'], 'L1_attn_w_qkv': _L1_attn_in['w_qkv'], 'L1_attn_b_qkv': _L1_attn_in['b_qkv'], 'L1_attn_w_proj': _L1_attn_in['w_proj'], 'L1_attn_b_proj': _L1_attn_in['b_proj'], 'L1_ffn_gate_w': _L1_ffn_in['gate_w'], 'L1_ffn_w1': _L1_ffn_in['w1'], 'L1_ffn_w3': _L1_ffn_in['w3'], 'L1_ffn_w2': _L1_ffn_in['w2']}

def reference(x, ctx_2048, mask_BxS2_if0, L0_xattn_W_in, L0_xattn_b_in, L0_xattn_g_res, L0_xattn_g_init, L0_attn_gate_w, L0_attn_q_w, L0_attn_k_w, L0_attn_v_w, L0_attn_fmq1_w, L0_attn_fmq2_w, L0_attn_fmk1_w, L0_attn_fmk2_w, L0_attn_norm_w, L0_attn_o_w, L0_ffn_keys, L0_ffn_w1, L0_ffn_b1, L0_ffn_w2, L0_ffn_b2, L0_ffn_rw, L0_ffn_rb, L1_xattn_Wq, L1_xattn_Wkv, L1_xattn_null_kv, L1_xattn_Wout, L1_xattn_ln_scale, L1_xattn_ln_bias, L1_attn_w_qkv, L1_attn_b_qkv, L1_attn_w_proj, L1_attn_b_proj, L1_ffn_gate_w, L1_ffn_w1, L1_ffn_w3, L1_ffn_w2):
    import jax
    import jax.numpy as jnp

    def _L0_xattn_ref(embeds, patch_embeds, patch_lens, W_in, b_in, g_res, g_init):
        import jax, jax.numpy as jnp
        import numpy as np
        B, L, P = (4, 512, 128)
        D_MODEL = 128
        D_GLOBAL = 256
        HEADDIM = 32
        EPSILON = 0.001
        RMS_EPS = 1e-05

        def rmsnorm(x, g, eps=RMS_EPS):
            var = jnp.mean(jnp.square(x), axis=-1, keepdims=True)
            return x * jax.lax.rsqrt(var + eps) * g

        def _hnet_depool(h, h_patch_full, patch_lens):
            h_patch = h_patch_full[..., :D_MODEL]
            bsz, plen = (h_patch.shape[0], h_patch.shape[1])
            seqlen = h.shape[1]
            logp = jnp.full((bsz, plen), -EPSILON, dtype=jnp.float32)
            bidx = jnp.cumsum(patch_lens, axis=1) - 1
            boundary_mask = jnp.zeros((bsz, seqlen), dtype=jnp.int32)
            boundary_mask = boundary_mask.at[jnp.arange(bsz)[:, None], bidx].set(1)
            dt = (-jnp.log(-jnp.expm1(logp))).astype(h_patch.dtype)
            x = h_patch / dt[..., None]
            n_heads = D_MODEL // HEADDIM
            A = -jnp.ones((n_heads,), dtype=jnp.float32)
            bcoef = jnp.exp(logp).astype(h_patch.dtype)
            x4 = x.reshape(bsz, plen, n_heads, HEADDIM)
            a = jnp.exp(dt[:, :, None] * A[None, None, :])
            u = (dt * bcoef)[:, :, None, None] * x4
            a_b = jnp.broadcast_to(a[..., None], u.shape)

            def comb(lft, rgt):
                aL, uL = lft
                aR, uR = rgt
                return (aL * aR, uL * aR + uR)
            _, s = jax.lax.associative_scan(comb, (a_b, u), axis=1)
            depool = s.reshape(bsz, plen, D_MODEL)
            plug = jnp.clip(jnp.cumsum(boundary_mask, axis=1) - 1, 0, plen - 1)
            depool_out = depool[jnp.arange(bsz)[:, None], plug]
            return depool_out + h
        h = rmsnorm(embeds, g_res)
        h = jnp.einsum('bld,ed->ble', h, W_in) + b_in
        h_patch = rmsnorm(patch_embeds, g_init)
        return _hnet_depool(h, h_patch, patch_lens)

    def _L0_attn_ref(x, gate_w, q_w, k_w, v_w, fmq1_w, fmq2_w, fmk1_w, fmk2_w, norm_w, o_w):
        import jax, jax.numpy as jnp
        import numpy as np
        B, S, HID = (4, 256, 128)
        E, K, H = (8, 2, 8)
        DK = HID // H
        DV = HID // H
        CAP = int(S * 1.0)
        CHUNK = 64
        EPS = 1e-05

        def chunk_linear_attn(q, k, v):
            Bt, T, Hh, Dk = q.shape
            Dv = v.shape[-1]
            nc = T // CHUNK
            q = q * Dk ** (-0.5)
            qc = q.reshape(Bt, nc, CHUNK, Hh, Dk).transpose(1, 0, 2, 3, 4)
            kc = k.reshape(Bt, nc, CHUNK, Hh, Dk).transpose(1, 0, 2, 3, 4)
            vc = v.reshape(Bt, nc, CHUNK, Hh, Dv).transpose(1, 0, 2, 3, 4)
            causal = jnp.tril(jnp.ones((CHUNK, CHUNK), q.dtype))

            def step(Sst, qkv):
                qb, kb, vb = qkv
                attn = jnp.einsum('bihd,bjhd->bhij', qb, kb) * causal
                intra = jnp.einsum('bhij,bjhe->bihe', attn, vb)
                inter = jnp.einsum('bihd,bhde->bihe', qb, Sst)
                Sst = Sst + jnp.einsum('bjhd,bjhe->bhde', kb, vb)
                return (Sst, intra + inter)
            S0 = jnp.zeros((Bt, Hh, Dk, Dv), q.dtype)
            _, o = jax.lax.scan(step, S0, (qc, kc, vc))
            return o.transpose(1, 0, 2, 3, 4).reshape(Bt, T, Hh, Dv)

        def _forward(x, gate_w, q_w, k_w, v_w, fmq1_w, fmq2_w, fmk1_w, fmk2_w, norm_w, o_w):
            b, s0, d = x.shape
            logits = jnp.einsum('bsd,ed->bse', x, gate_w)
            scores = jax.nn.softmax(logits.astype(jnp.float32), axis=-1)
            rw, sel = jax.lax.top_k(scores, K)
            rw = (rw / rw.sum(-1, keepdims=True)).astype(x.dtype)
            routing_mask = jax.nn.one_hot(sel, E, dtype=jnp.int32).sum(2)
            s = s0 * K
            x_rep = jnp.repeat(x, K, axis=1).reshape(b * s, d)
            sel_flat = sel.reshape(b * s).astype(jnp.int32)
            batch_idx = jnp.repeat(jnp.arange(b, dtype=jnp.int32), s)
            combined = batch_idx * E + sel_flat
            sorted_indices = jnp.argsort(combined)
            x_sorted = x_rep[sorted_indices]
            tokens = routing_mask.sum(axis=1)
            flat_off = (jnp.cumsum(tokens, axis=1) + (jnp.arange(b, dtype=jnp.int32) * s)[:, None]).reshape(-1)
            starts = jnp.concatenate([jnp.zeros((1,), flat_off.dtype), flat_off[:-1]])
            idx = starts[:, None] + jnp.arange(CAP, dtype=flat_off.dtype)[None, :]
            shift = jnp.maximum(tokens.reshape(-1) - CAP, 0)
            tidx = idx + shift[:, None]
            dmask = tidx < flat_off[:, None]
            tidx = jnp.where(dmask, tidx, 0)
            xe = x_sorted[tidx.reshape(-1)].reshape(b * E, CAP, d) * dmask[..., None].astype(x.dtype)
            xe = xe.reshape(b, E, CAP, d).transpose(1, 0, 2, 3)
            q = jnp.einsum('ebtc,kc->ebtk', xe, q_w).reshape(E, b, CAP, H, DK)
            k = jnp.einsum('ebtc,ekc->ebtk', xe, k_w).reshape(E, b, CAP, H, DK)
            v = jnp.einsum('ebtc,ekc->ebtk', xe, v_w).reshape(E, b, CAP, H, DV)
            q = jnp.einsum('...d,kd->...k', q, fmq1_w) * jnp.einsum('...d,kd->...k', q, fmq2_w)
            k = jnp.einsum('...d,kd->...k', k, fmk1_w) * jnp.einsum('...d,kd->...k', k, fmk2_w)
            o = chunk_linear_attn(q.reshape(E * b, CAP, H, DK), k.reshape(E * b, CAP, H, DK), v.reshape(E * b, CAP, H, DV))
            oflat = o.reshape(E, b, CAP, H, DV).transpose(1, 0, 2, 3, 4).reshape(b * E * CAP, H, DV)
            oflat = oflat * dmask.reshape(-1)[:, None, None].astype(o.dtype)
            res = jnp.zeros((b * s, H, DV), o.dtype).at[tidx.reshape(-1)].add(oflat)
            inv = jnp.argsort(sorted_indices)
            restored = res[inv].reshape(b, s0, K, H, DV)
            out = (restored * rw[..., None, None]).sum(axis=2)
            out = out * jax.lax.rsqrt(jnp.mean(out * out, axis=-1, keepdims=True) + EPS) * norm_w
            out = out.reshape(b, s0, H * DV)
            return jnp.einsum('bsv,dv->bsd', out, o_w)
        return _forward(x, gate_w, q_w, k_w, v_w, fmq1_w, fmq2_w, fmk1_w, fmk2_w, norm_w, o_w)

    def _L0_ffn_ref(x, keys, w1, b1, w2, b2, rw, rb):
        import jax, jax.numpy as jnp
        import numpy as np
        B, L, D = (4, 64, 128)
        E, TOP_K = (16, 4)
        F = 4 * D
        diff = x[:, :, None, :] - keys
        dist2 = jnp.sum(diff * diff, axis=-1)
        logits = -dist2 + jnp.einsum('bld,ed->ble', x, rw) + rb
        topv, topi = jax.lax.top_k(logits, TOP_K)
        w = jax.nn.softmax(topv, axis=-1)
        hidden = jax.nn.gelu(jnp.einsum('bld,efd->blef', x, w1) + b1, approximate=False)
        exp_out = jnp.einsum('blef,edf->bled', hidden, w2) + b2
        sel = jnp.take_along_axis(exp_out, topi[..., None], axis=2)
        fused = jnp.sum(w[..., None] * sel, axis=2)
        return fused

    def _L1_xattn_ref(x, context, Wq, Wkv, null_kv, Wout, ln_scale, ln_bias):
        import jax, jax.numpy as jnp
        import numpy as np
        B, N, DIM = (8, 512, 128)
        M, CTX = (32, 256)
        HEADS, DH = (16, 64)
        INNER = HEADS * DH
        EPS = 1e-06

        def _split_heads(t):
            b, n, _ = t.shape
            return t.reshape(b, n, HEADS, DH).transpose(0, 2, 1, 3)
        scale = DH ** (-0.5)
        b = x.shape[0]
        q = _split_heads(jnp.einsum('bnd,df->bnf', x, Wq))
        kv = jnp.einsum('bmc,cf->bmf', context, Wkv)
        k, v = jnp.split(kv, 2, axis=-1)
        k, v = (_split_heads(k), _split_heads(v))
        nk = jnp.broadcast_to(null_kv[0], (b, HEADS, 1, DH))
        nv = jnp.broadcast_to(null_kv[1], (b, HEADS, 1, DH))
        k = jnp.concatenate((nk, k), axis=-2)
        v = jnp.concatenate((nv, v), axis=-2)
        q = q * scale
        sim = jnp.einsum('bhid,bhjd->bhij', q, k)
        attn = jax.nn.softmax(sim, axis=-1)
        out = jnp.einsum('bhij,bhjd->bhid', attn, v)
        out = out.transpose(0, 2, 1, 3).reshape(b, -1, INNER)
        out = jnp.einsum('bnf,fd->bnd', out, Wout)
        mu = jnp.mean(out, axis=-1, keepdims=True)
        var = jnp.var(out, axis=-1, keepdims=True)
        out = (out - mu) * jax.lax.rsqrt(var + EPS) * ln_scale + ln_bias
        return out

    def _L1_attn_ref(x, w_qkv, b_qkv, w_proj, b_proj):
        import jax, jax.numpy as jnp
        import numpy as np
        EMBED_DIM = 128
        NUM_HEADS = 16
        HEAD_DIM = EMBED_DIM // NUM_HEADS
        SCALE = HEAD_DIM ** (-0.5)
        B, N = (2, 256)
        b, n, c = x.shape
        qkv = x @ w_qkv + b_qkv
        qkv = qkv.reshape(b, n, 3, NUM_HEADS, HEAD_DIM)
        qkv = jnp.transpose(qkv, (2, 0, 3, 1, 4))
        q, k, v = (qkv[0], qkv[1], qkv[2])
        attn = jnp.einsum('bhnd,bhmd->bhnm', q, k) * SCALE
        attn = jax.nn.softmax(attn, axis=-1)
        out = jnp.einsum('bhnm,bhmd->bhnd', attn, v)
        out = jnp.transpose(out, (0, 2, 1, 3)).reshape(b, n, c)
        return out @ w_proj + b_proj

    def _L1_ffn_ref(x, gate_w, w1, w3, w2):
        import jax, jax.numpy as jnp
        import numpy as np
        TOP_K = 2
        logits = jnp.einsum('btd,de->bte', x, gate_w)
        probs = jax.nn.softmax(logits, axis=-1)
        expert_weights, expert_indices = jax.lax.top_k(probs, TOP_K)
        expert_weights = expert_weights / expert_weights.sum(-1, keepdims=True)
        E = w1.shape[0]
        out = jnp.zeros_like(x)
        for i in range(E):
            wi = jnp.where(expert_indices == i, expert_weights, 0.0).sum(-1)
            h = jax.nn.silu(jnp.einsum('btd,df->btf', x, w1[i])) * jnp.einsum('btd,df->btf', x, w3[i])
            out = out + jnp.einsum('btf,fd->btd', h, w2[i]) * wi[..., None]
        return out
    x = x + _L0_xattn_ref(_layernorm(x, axis=-1), ctx_2048, mask_BxS2_if0, L0_xattn_W_in, L0_xattn_b_in, L0_xattn_g_res, L0_xattn_g_init)
    x = x + _L0_attn_ref(_layernorm(x, axis=-1), L0_attn_gate_w, L0_attn_q_w, L0_attn_k_w, L0_attn_v_w, L0_attn_fmq1_w, L0_attn_fmq2_w, L0_attn_fmk1_w, L0_attn_fmk2_w, L0_attn_norm_w, L0_attn_o_w)
    x = x + _L0_ffn_ref(_layernorm(x, axis=-1), L0_ffn_keys, L0_ffn_w1, L0_ffn_b1, L0_ffn_w2, L0_ffn_b2, L0_ffn_rw, L0_ffn_rb)
    x = x + _L1_xattn_ref(_layernorm(x, axis=-1), ctx_2048, L1_xattn_Wq, L1_xattn_Wkv, L1_xattn_null_kv, L1_xattn_Wout, L1_xattn_ln_scale, L1_xattn_ln_bias)
    x = x + _L1_attn_ref(_layernorm(x, axis=-1), L1_attn_w_qkv, L1_attn_b_qkv, L1_attn_w_proj, L1_attn_b_proj)
    x = x + _L1_ffn_ref(_layernorm(x, axis=-1), L1_ffn_gate_w, L1_ffn_w1, L1_ffn_w3, L1_ffn_w2)
    return x

_drawn_inputs = setup_inputs


def setup_inputs(seed=0):
    import zlib

    import numpy as np

    out = dict(_drawn_inputs(seed))
    spreads = {'L0_xattn_b_in': (0.0, 0.1),
     'L0_xattn_g_res': (1.0, 0.6),
     'L0_xattn_g_init': (1.0, 0.2),
     'L0_attn_norm_w': (1.0, 0.6),
     'L0_ffn_b1': (0.0, 0.587),
     'L0_ffn_b2': (0.0, 0.1),
     'L0_ffn_rb': (0.0, 2.0),
     'L1_xattn_ln_scale': (1.0, 0.2),
     'L1_xattn_ln_bias': (0.0, 0.1),
     'L1_attn_b_qkv': (0.0, 0.1),
     'L1_attn_b_proj': (0.0, 0.1)}
    factors = {'L0_attn_gate_w': 8.0,
     'L0_attn_q_w': 8.0,
     'L0_attn_k_w': 8.0,
     'L0_attn_v_w': 8.0,
     'L0_attn_fmq1_w': 8.0,
     'L0_attn_fmq2_w': 8.0,
     'L0_attn_fmk1_w': 8.0,
     'L0_attn_fmk2_w': 8.0,
     'L0_attn_o_w': 8.0,
     'L0_ffn_rw': 8.0,
     'L1_xattn_null_kv': 8.0,
     'L1_ffn_gate_w': 8.0,
     'L1_ffn_w1': 8.0,
     'L1_ffn_w3': 8.0,
     'L1_ffn_w2': 8.0}
    for name, (base, spread) in spreads.items():
        noise = np.random.default_rng([zlib.crc32(name.encode()), seed]).standard_normal(out[name].shape)
        drawn = base * np.exp(spread * noise) if base else spread * noise
        out[name] = jnp.asarray(drawn.astype(out[name].dtype))
    for name, factor in factors.items():
        out[name] = (out[name] * factor).astype(out[name].dtype)
    return out
```

```python
import concourse.bass as bass
from concourse import mybir
from concourse.alu_op_type import AluOpType as ALU
from contextlib import ExitStack
import numpy as np

STAGES = 6


def perceiver_kernel(nc, x, ctx_2048, patch_lens, L0_W_in, L0_b_in, L0_g_res, L0_g_init,
                     gate_w, q_w, k_w, v_w, fmq1, fmq2, fmk1, fmk2, norm_w, o_w,
                     keys, f0_w1, f0_b1, f0_w2, f0_b2, f0_rw, f0_rb,
                     Wq, Wkv, null_kv, Wout, ln_scale, ln_bias,
                     w_qkv, b_qkv, w_proj, b_proj, f1_gate, f1_w1, f1_w3, f1_w2, out):
    F32, F16, BF16, I32 = mybir.dt.float32, mybir.dt.float16, mybir.dt.bfloat16, mybir.dt.int32
    ACT = mybir.ActivationFunctionType
    AX = mybir.AxisListType

    B, S, D = x.shape
    NK, DC = ctx_2048.shape[1:]
    T = B * S
    NCH = NK // S
    CT = DC // 128
    E1, H1 = gate_w.shape[0], 8
    DK1 = D // H1
    E2, F2 = f0_w1.shape[0], f0_w1.shape[1]
    FT2 = F2 // 128
    H3 = Wq.shape[1] // 64
    DH3 = 64
    H4 = 16
    DH4 = D // H4
    E5, F5 = f1_w1.shape[0], f1_w1.shape[2]
    FT5 = F5 // 128
    TOPK1, TOPK2, TOPK5 = 2, 4, 2
    LN_EPS, RMS_EPS, XLN_EPS = 1e-5, 1e-5, 1e-6
    LOGP = np.float32(-0.001)
    DT = float(-np.log(-np.expm1(LOGP)))
    BCOEF = float(np.exp(LOGP))
    MAGIC = float(0x5F3759DF)
    TINY = 1.1754944e-38

    es = ExitStack()
    with es:
        def sb(name, shape, dt=F32):
            return es.enter_context(nc.sbuf_tensor(name, shape, dt))

        names = {}

        def sem(name):
            if name not in names:
                names[name] = es.enter_context(nc.semaphore(name))
            return names[name]

        def bc(ap, axis, n):
            u = ap.unsqueeze(axis)
            shape = list(u.shape)
            shape[axis] = n
            return u.broadcast_to(shape)

        KB = 256
        arena = sb("arena", [128, 160 * KB])
        main = sb("main", [128, 24 * KB])

        def at(base, kb, shape, dt=F32):
            words = int(np.prod(shape)) * (2 if dt in (F16, BF16) else 4) // 4
            o = int(kb * KB)
            v = base[:, o:o + words]
            if dt is not F32:
                v = v.bitcast(dt)
            if len(shape) == 2:
                v = v.rearrange("p (a b) -> p a b", a=shape[0])
            elif len(shape) == 3:
                v = v.rearrange("p (a b c) -> p a b c", a=shape[0], b=shape[1])
            elif len(shape) == 4:
                v = v.rearrange("p (a b c d) -> p a b c d", a=shape[0], b=shape[1], c=shape[2])
            return v

        xs = [sb(f"x{i}", [128, B, D]) for i in range(3)]
        yy = sb("yy", [128, 2 * T])
        y = yy[:, 0:T].rearrange("p (b d) -> p b d", b=B)
        yT = yy[:, T:2 * T]
        zat = sb("zat", [128, H3 * DH3])
        ident = sb("ident", [128, 128])
        causal = sb("causal", [128, 128])
        ones = sb("ones", [128, 128])
        stats = sb("stats", [128, B, 6])
        mv = sb("mv", [128, B, 2])
        small = sb("small", [128, 9, 32])
        route_s = sb("route_s", [128, 6, 64])
        wgt = sb("wgt", [128, B, E2])
        ctx_nat = [sb(f"ctx_nat{i}", [128, 2, DC]) for i in range(2)]
        wv_hi = sb("wv_hi", [128, CT, 1024], F16)
        wv_lo = sb("wv_lo", [128, CT, 1024], F16)
        wout_sb = sb("wout_sb", [128, 8, D])
        nv_bc = sb("nv_bc", [128, DH3])
        lns_bc = sb("lns_bc", [128, 2, D])
        sim0 = sb("sim0", [128, B, H3])
        nsim0 = sb("nsim0", [128, B, H3])
        unit_s = sb("unit_s", [128, 2, 8])
        biases = sb("biases", [128, 8])
        rows = at(arena, 148, [512])
        rows4 = at(arena, 68, [256])

        c0 = at(arena, 96, [B, DC])
        u0 = at(arena, 100, [B, D])
        wt0 = at(arena, 102, [B, S])
        t0 = at(arena, 104, [B, S])
        e0 = at(arena, 106, [B, S])
        patch_i = at(arena, 108, [B, NCH], I32)
        parts_i = at(arena, 108.25, [3, B * NCH], I32)
        parts_f = at(arena, 109, [3 * B * NCH])
        reset = at(arena, 109.75, [3 * B * NCH])
        scan = at(arena, 110.5, [3 * B * NCH])
        cum_i = at(arena, 111.25, [3, B * NCH], I32)
        pint = at(arena, 112, [12, 64], I32)
        pflt = at(arena, 115, [4, 64])
        lo_oh = at(arena, 116, [64, 16], BF16)
        hi_oh = at(arena, 118, [64, 8], BF16)
        iota16 = at(arena, 119, [16])
        iota8 = at(arena, 119.0625, [8])
        iotap = at(arena, 119.125, [2])
        iotap_i = at(arena, 119.25, [2], I32)
        iota16_i = at(arena, 119.5, [24], I32)
        mask16 = at(arena, 119.75, [16])
        bnd = at(arena, 120, [B, 16], BF16)
        after_b = at(arena, 152, [16, S], BF16)
        strict = at(arena, 121, [128])
        w_in = at(arena, 121.5, [D])
        w_inT = at(arena, 122, [D])
        ginit_bc = at(arena, 122.5, [D])
        r0T = at(arena, 123, [T])
        sq_junk = at(arena, 151, [DC])

        k_nat = at(arena, 136, [E1, D])
        v_nat = at(arena, 140, [E1, D])
        qo_nat = at(arena, 80, [2, D])
        gate_nat = at(arena, 81, [D])
        keysT = at(arena, 92, [2, E2])
        gateT = at(arena, 92.25, [E1])
        f_nat = at(arena, 82, [4, DK1])
        bdT = at(arena, 82.5, [4, 128])
        blk16 = at(arena, 84.5, [H1, DK1])
        o_wT = at(arena, 85, [D])
        mqT = at(arena, 86, [2, D])
        mkT = at(arena, 0, [E1, 2, D])
        v_wT = at(arena, 8, [E1, D])
        kT1 = at(arena, 12, [E1, T])
        qbd = at(arena, 28, [B, H1, S])
        v1 = at(arena, 44, [B, E1, D])
        gmask = at(arena, 60, [E1, B, S])
        am = [at(arena, 76, [H1, S]), at(arena, 87, [H1, S])]
        q1 = at(arena, 93, [T])
        f_rep = at(arena, 93, [4, H1, DK1])
        rT_sb = at(arena, 146, [T])
        rank_t = sb("rank_t", [128, E2, E2])

        w1n = [at(arena, 96 + 4 * i, [FT2, D]) for i in range(2)]
        w2n = [at(arena, 98 + 4 * i, [F2]) for i in range(2)]
        w1T = [at(arena, 104 + 4 * i, [F2]) for i in range(2)]
        w2T = [at(arena, 106 + 4 * i, [FT2, D]) for i in range(2)]
        hT2 = [at(arena, 112 + 8 * i, [FT2, T]) for i in range(2)]
        b1n = at(arena, 128, [F2])
        b2n = at(arena, 130, [D])
        b1T = at(arena, 130.5, [FT2, E2])
        cmp = at(arena, 131, [B, E2, E2])
        kk_nat = at(arena, 135, [2, D])

        qk_hi = at(arena, 0, [H3, CT, T], F16)
        qk_lo = at(arena, 32, [H3, CT, T], F16)
        v3 = [at(arena, 64 + 32 * i, [NCH, 512]) for i in range(2)]
        cT_hi = [at(arena, 128 + 16 * i, [CT, NK], F16) for i in range(2)]
        cT_lo = [at(arena, 136 + 16 * i, [CT, NK], F16) for i in range(2)]
        A3 = at(arena, 144, [H3, DC])
        wq_nat = at(main, 0, [1024])
        wk_nat = at(main, 4, [CT, 1024])
        wqT = at(main, 12, [8, 128])
        wkT = at(main, 16, [8, DC])
        wn = at(arena, 132, [H3])
        wv_nat = at(arena, 64, [CT, 1024])
        p3 = [at(main, 8 * i, [NK]) for i in range(2)]
        pT3 = at(main, 16, [NCH, 128])
        oT3 = yy[:, :].rearrange("p (f q) -> p f q", f=8)
        nk_col = sb("nk_col", [128, 1])

        wqkv_sb = at(arena, 0, [3 * D])
        wproj_sb = at(arena, 1.5, [D])
        qT4 = at(arena, 2, [T])
        kT4 = at(arena, 4, [T])
        kbd = at(arena, 6, [B, H4, S])
        v4 = at(arena, 38, [B, H4, DH4 + 1])
        d4 = at(arena, 41, [H4, S])
        p4 = at(arena, 49, [H4, S])
        pT4 = at(arena, 57, [H4, S])
        m16 = at(arena, 65, [H4])
        mx4 = at(arena, 65.25, [H4])
        rs4 = at(arena, 65.5, [H4])
        z4 = at(arena, 66, [D])
        zT4 = at(arena, 67, [D])
        w1g = [at(arena, 72 + 6 * i, [F5]) for i in range(2)]
        w3g = [at(arena, 74 + 6 * i, [F5]) for i in range(2)]
        w2g = [at(arena, 76 + 6 * i, [FT5, D]) for i in range(2)]
        sg = [at(arena, 84 + 2 * i, [T]) for i in range(2)]
        hT5 = [at(arena, 88 + 8 * i, [FT5, T]) for i in range(2)]
        f1g = at(arena, 104, [E5])
        cmp5 = at(arena, 106, [B, E5, E5])

        ps = es.enter_context(nc.psum_tensor("ps", [128, 8, 512], F32))

        def bank(i):
            return ps[:, i, :]

        for n in ("ld_x", "ld_patch", "ld_c0", "ld_s0", "ld_a0", "ld_f0", "ld_x3", "ld_a1", "ld_g1"):
            sem(n)
        block = es.enter_context(nc.Block())

        ndma = {}

        def load(eng, name, dst, src):
            ndma[name] = ndma.get(name, 0) + 16
            eng.dma_start(dst, src).then_inc(sem(name), 16)

        def row(ap1):
            return ap1.rearrange("(a n) -> a n", a=1)

        def col(ap1):
            return ap1.rearrange("(n a) -> n a", a=1)

        def rowb(ap1, n=128):
            return ap1.partition_broadcast(n)

        x_v = x.rearrange("b s d -> s b d")
        out_v = out.rearrange("b s d -> s b d")
        ctx_v = ctx_2048.rearrange("b (c p) f -> b p c f", p=128)

        @block.sync
        def _(sp):
            load(sp, "ld_x", xs[0][:], x_v)
            load(sp, "ld_patch", patch_i, patch_lens.rearrange("b (p c) -> p b c", c=NCH))
            load(sp, "ld_c0", c0, ctx_2048[:, 0:128, :].rearrange("b p f -> p b f"))
            load(sp, "ld_s0", w_in, L0_W_in)
            load(sp, "ld_s0", biases[:, 0:1], col(L0_g_res))
            load(sp, "ld_s0", ginit_bc, rowb(L0_g_init[0:D]))
            load(sp, "ld_s0", rows[0:1, 0:D], row(L0_b_in))
            for i, f in enumerate((fmq1, fmq2, fmk1, fmk2)):
                load(sp, "ld_a0", f_nat[0:DK1, i, :], f)
            load(sp, "ld_a0", qo_nat[:, 0, :], q_w)
            load(sp, "ld_a0", qo_nat[:, 1, :], o_w)
            load(sp, "ld_a0", gate_nat[0:E1, :], gate_w)
            load(sp, "ld_a0", k_nat, k_w.rearrange("e k c -> k e c"))
            load(sp, "ld_a0", v_nat, v_w.rearrange("e k c -> k e c"))
            for h in range(H1):
                load(sp, "ld_a0", biases[h * DK1:(h + 1) * DK1, 1:2], col(norm_w))
            load(sp, "ld_f0", kk_nat[0:E2, 0, :], keys)
            load(sp, "ld_f0", kk_nat[0:E2, 1, :], f0_rw)
            load(sp, "ld_f0", rows[0:1, 128:128 + E2], row(f0_rb))
            load(sp, "ld_f0", b1n[0:E2, :], f0_b1)
            load(sp, "ld_f0", b2n[0:E2, :], f0_b2)
            load(sp, "ld_x3", wq_nat, Wq)
            load(sp, "ld_x3", wk_nat, Wkv[:, 0:1024].rearrange("(t c) f -> c t f", c=128))
            load(sp, "ld_x3", wout_sb[:], Wout.rearrange("(t f) d -> f t d", f=128))
            load(sp, "ld_x3", nk_col[0:64, :], col(null_kv[0]))
            load(sp, "ld_x3", nk_col[64:128, :], col(null_kv[0]))
            load(sp, "ld_x3", nv_bc[:], rowb(null_kv[1]))
            load(sp, "ld_x3", lns_bc[:, 0, :], rowb(ln_scale))
            load(sp, "ld_x3", lns_bc[:, 1, :], rowb(ln_bias))
            for i in range(2):
                load(sp, "ld_x3", biases[:, 2 + i:3 + i], col(b_qkv[i * D:(i + 1) * D]))
            for e in range(E2 if STAGES > 2 else 0):
                if e == 0:
                    sp.wait_ge(sem("x_ready"), 1)
                if e >= 2:
                    sp.wait_ge(sem("f0_turned"), e - 1)
                sp.dma_start(w1n[e % 2], f0_w1[e].rearrange("(t f) d -> f t d", f=128)).then_inc(sem(f"w0_{e % 2}"), 16)
                sp.dma_start(w2n[e % 2], f0_w2[e]).then_inc(sem(f"w0_{e % 2}"), 16)
            if STAGES > 3:
                sp.wait_ge(sem("x_ready"), 2)
                load(sp, "ld_wv", wv_nat, Wkv[:, 1024:2048].rearrange("(t c) f -> c t f", c=128))
                for i in range(B * NCH // 2):
                    b, c = divmod(2 * i, NCH)
                    if i >= 2:
                        sp.wait_ge(sem("ctx_turned"), i - 1)
                    sp.dma_start(ctx_nat[i % 2][:], ctx_v[b, :, c:c + 2, :]).then_inc(sem(f"ctx_in{i % 2}"), 16)
            if STAGES > 4:
                sp.wait_ge(sem("o3_ready"), B)
                load(sp, "ld_a1", wqkv_sb, w_qkv)
                load(sp, "ld_a1", wproj_sb, w_proj)
                load(sp, "ld_a1", rows4[0:1, 0:D], row(b_qkv[2 * D:3 * D]))
                load(sp, "ld_a1", rows4[0:1, D:2 * D], row(b_proj))
                load(sp, "ld_g1", f1g, f1_gate)
            for e in range(E5 if STAGES > 5 else 0):
                if e >= 2:
                    sp.wait_ge(sem("f1_used"), e - 1)
                k = e % 2
                sp.dma_start(w1g[k], f1_w1[e]).then_inc(sem(f"w5_{k}"), 16)
                sp.dma_start(w3g[k], f1_w3[e]).then_inc(sem(f"w5_{k}"), 16)
                sp.dma_start(w2g[k], f1_w2[e].rearrange("(t f) d -> f t d", f=128)).then_inc(sem(f"w5_{k}"), 16)
            sp.wait_ge(sem("x_ready"), STAGES)
            if STAGES < 6:
                for name, v in ndma.items():
                    sp.wait_ge(sem(name), v)
            sp.dma_start(out_v, xs[STAGES % 3][:]).then_inc(sem("out_done"), 16)
            sp.wait_ge(sem("out_done"), 16)

        @block.gpsimd
        def _(pool):
            n = [0]

            def step(ins):
                n[0] += 1
                ins.then_inc(sem("pool_step"), 1)
                pool.wait_ge(sem("pool_step"), n[0])

            def mask(ap, pattern, base, mult, op, fill):
                step(pool.affine_select(out=ap, in_=ap, compare_op=op, fill=fill, base=base,
                                        pattern=pattern, channel_multiplier=mult))

            step(pool.memset(ident[:], 0.0))
            mask(ident[:], [[-1, 128]], 0, 1, ALU.not_equal, 1.0)
            step(pool.memset(ones[:], 1.0))
            step(pool.memset(causal[:], 1.0))
            mask(causal[:], [[1, 128]], 0, -1, ALU.is_ge, 0.0)
            step(pool.memset(strict, 1.0))
            mask(strict, [[1, 128]], 0, -1, ALU.is_gt, 0.0)
            step(pool.memset(reset, 1.0))
            step(pool.memset(reset.rearrange("p (a c) -> p a c", c=NCH)[:, :, 0:1], 0.0))
            step(pool.iota(iotap_i[:, 0:1], pattern=[[0, 1]], base=0, channel_multiplier=1))
            step(pool.iota(iota16_i[:, 0:16], pattern=[[1, 16]], base=0, channel_multiplier=0))
            step(pool.memset(after_b, 1.0))
            mask(after_b, [[-1, 16], [1, S]], 0, -16, ALU.is_ge, 0.0)
            pool.sem_inc(sem("const_a"), 1)
            step(pool.memset(blk16, 1.0))
            mask(blk16, [[-DK1, H1], [0, DK1]], 0, 1, ALU.is_ge, 0.0)
            mask(blk16, [[DK1, H1], [0, DK1]], DK1 - 1, -1, ALU.is_ge, 0.0)
            step(pool.memset(rank_t[:], 0.0))
            mask(rank_t[:], [[1, E2], [-1, E2]], 0, 0, ALU.is_gt, TINY)
            pool.wait_ge(sem("ld_a0"), ndma["ld_a0"])
            step(pool.tensor_copy(f_rep[0:DK1], bc(f_nat[0:DK1, :, :], 2, H1)))
            pool.sem_inc(sem("const_b"), 1)
            if STAGES > 4:
                pool.wait_ge(sem("o3_ready"), B)
                step(pool.memset(m16, 1.0))
                mask(m16, [[-DH4, H4]], 0, 1, ALU.is_ge, 0.0)
                mask(m16, [[DH4, H4]], DH4 - 1, -1, ALU.is_ge, 0.0)
                step(pool.memset(v4, 1.0))
                pool.sem_inc(sem("const_c"), 1)

        @block.tensor
        def _(pe):
            def mm(o, lhsT, rhs, start=True, stop=True, **k):
                return pe.matmul(o, lhsT, rhs, start=start, stop=stop, **k)

            def tr(o, i, n=128):
                return pe.transpose(o, i, ident[0:n, 0:n])

            def turn_y(stage, b_ps):
                pe.wait_ge(sem("y_ready"), stage + 1)
                for b in range(B):
                    last = tr(bank(b_ps)[:, b * S:(b + 1) * S], y[:, b, :])
                last.then_inc(sem("yT_ps"), 1)

            pe.wait_ge(sem("const_a"), 1)
            pe.wait_ge(sem("ld_s0"), ndma["ld_s0"])
            tr(bank(0)[:, 0:D], w_in).then_inc(sem("w_inT_ps"), 1)
            turn_y(0, 3)
            pe.wait_ge(sem("scan_ready"), 1)
            mm(bank(1)[:, 0:12], strict, scan.rearrange("p (a c) -> p a c", c=NCH)[:, :, NCH - 1])\
                .then_inc(sem("prefix_ps"), 1)
            pe.wait_ge(sem("onehot_ready"), 1)
            for b in range(B):
                for c in range(NCH):
                    last = mm(bank(1)[0:8, 64 + 16 * b:80 + 16 * b], hi_oh[:, b * NCH + c, :],
                              lo_oh[:, b * NCH + c, :], start=(c == 0), stop=(c == NCH - 1))
            last.then_inc(sem("count_ps"), 1)
            pe.wait_ge(sem("bnd_ready"), 1)
            for b in range(B):
                for l in range(16):
                    last = mm(bank(2)[:, b * S:(b + 1) * S], bnd[0:8, b, l:l + 1].broadcast_to([8, 128]),
                              after_b[0:8, l, :], start=(l == 0), stop=(l == 15))
            last.then_inc(sem("plug_ps"), 1)
            pe.wait_ge(sem("const_b"), 1)
            pe.wait_ge(sem("ld_a0"), ndma["ld_a0"])
            for i in range(4):
                last = mm(bank(5)[:, i * 128:(i + 1) * 128], f_rep[0:DK1, i, :, :].rearrange("p a b -> p (a b)"),
                          bc(ident[0:DK1, 0:DK1], 1, H1))
            last.then_inc(sem("bd_ps"), 1)
            tr(bank(6)[:, 0:D], qo_nat[:, 1, :])
            tr(bank(6)[:, D:D + E1], gate_nat[0:E1, :], E1).then_inc(sem("og_ps"), 1)
            pe.wait_ge(sem("w0T_ready"), 1)
            pe.wait_ge(sem("r0T_ready"), 1)
            pe.wait_ge(sem("wt0_ready"), 1)
            for b in range(B):
                o = bank(4)[:, b * D:(b + 1) * D]
                mm(o, r0T[:, b * S:(b + 1) * S], w_inT, stop=False)
                mm(o, wt0[:, b, :], u0[:, b, :], start=False, stop=False)
                last = mm(o, ones[0:1, 0:S], rows[0:1, 0:D], start=False)
            last.then_inc(sem("s0_ps"), 1)

            pe.wait_ge(sem("bd_ready"), 1)
            mm(bank(7)[:, 0:256], qo_nat[:, 0, :], bdT[:, 0:2, :].rearrange("p a b -> p (a b)")).then_inc(sem("mq_ps"), 1)
            for e in range(E1):
                if e % 2 == 0 and e >= 4:
                    pe.wait_ge(sem("mk_ready"), e // 2 - 1)
                if e == 2:
                    pe.wait_ge(sem("og_ready"), 1)
                last = mm(bank(5 + (e // 2) % 2)[:, (e % 2) * 256:(e % 2) * 256 + 256],
                          k_nat[:, e, :], bdT[:, 2:4, :].rearrange("p a b -> p (a b)"))
                if e % 2 == 1:
                    last.then_inc(sem("mk_ps"), 1)
            for g in range(2):
                pe.wait_ge(sem("mk_ready"), 3 + g)
                for e in range(4):
                    last = tr(bank(5 + g)[:, e * 128:(e + 1) * 128], v_nat[:, 4 * g + e, :])
                last.then_inc(sem("vw_ps"), 1)
            if STAGES < 2:
                return
            turn_y(1, 3)
            pe.wait_ge(sem("yT_ready"), 1)
            for b in range(B):
                last = mm(bank(0)[:, b * E1:(b + 1) * E1], yT[:, b * S:(b + 1) * S], gateT)
            last.then_inc(sem("logit_ps"), 1)
            pe.wait_ge(sem("mq_ready"), 1)
            mm(bank(1), mqT[:, 0, :], yT)
            mm(bank(2), mqT[:, 1, :], yT).then_inc(sem("qk_ps"), 1)
            pe.wait_ge(sem("mk_ready"), 4)
            for e in range(E1):
                if e == 0:
                    pe.wait_ge(sem("vw_ready"), 2)
                lo = 4 + 2 * (e % 2)
                if e == 1:
                    pass
                if e >= 2:
                    pe.wait_ge(sem("k1_ready"), e)
                mm(bank(lo), mkT[:, e, 0, :], yT)
                mm(bank(lo + 1), mkT[:, e, 1, :], yT).then_inc(sem("qk_ps"), 1)
            pe.wait_ge(sem("k1_ready"), 1)
            for i in range(2 * B):
                b, g = divmod(i, 2)
                if i >= 2:
                    pe.wait_ge(sem("v1_ready"), i - 1)
                mm(bank(1 + i % 2), yT[:, b * S:(b + 1) * S],
                   v_wT[:, 4 * g:4 * g + 4, :].rearrange("p a b -> p (a b)")).then_inc(sem("v1_ps"), 1)
            pe.wait_ge(sem("w_ready"), 1)
            for b in range(B):
                last = tr(bank(0)[0:E1, b * S:(b + 1) * S], wgt[:, b, 0:E1])
            last.then_inc(sem("rT_ps"), 1)
            pe.wait_ge(sem("rT_ready"), 1)
            for e in range(E1):
                if e >= 2:
                    pe.wait_ge(sem("g_ready"), e - 1)
                if e == 1:
                    pe.wait_ge(sem("yT_ready"), 1)
                mm(bank(0 if e % 2 else 3), ident[0:E1, e:e + 1].broadcast_to([E1, 128]), rT_sb[0:E1, :])\
                    .then_inc(sem("g_ps"), 1)
            pe.wait_ge(sem("g_ready"), E1)
            pe.wait_ge(sem("v1_ready"), 2 * B)
            pe.wait_ge(sem("k1_ready"), E1 + 1)
            pe.wait_ge(sem("qbd_ready"), B)

            def scores1(i):
                b, e = divmod(i, E1)
                lo = 2 * (i % 2)
                if i >= 2:
                    pe.wait_ge(sem("am_ready"), i - 1)
                lhsT = kT1[:, e, b * S:(b + 1) * S]
                mm(bank(lo), lhsT, qbd[:, b, 0:4, :].rearrange("p a b -> p (a b)"))
                mm(bank(lo + 1), lhsT, qbd[:, b, 4:8, :].rearrange("p a b -> p (a b)")).then_inc(sem("sc1_ps"), 1)

            def mix1(i):
                b, e = divmod(i, E1)
                pe.wait_ge(sem("am_ready"), i + 1)
                for h in range(H1):
                    o = bank(4)[:, b * D + h * DK1:b * D + (h + 1) * DK1]
                    last = mm(o, am[i % 2][:, h, :], v1[:, b, e, h * DK1:(h + 1) * DK1],
                              start=(i == 0 and h == 0), stop=(e == E1 - 1), skip_group_check=True)
                last.then_inc(sem("o1_ps"), 1)

            scores1(0)
            for i in range(B * E1):
                if i + 1 < B * E1:
                    scores1(i + 1)
                mix1(i)
            pe.wait_ge(sem("z1_ready"), 1)
            for b in range(B):
                last = tr(bank(5)[:, b * S:(b + 1) * S], y[:, b, :])
            last.then_inc(sem("z1T_ps"), 1)
            pe.wait_ge(sem("z1T_ready"), 1)
            for b in range(B):
                last = mm(bank(6)[:, b * D:(b + 1) * D], yT[:, b * S:(b + 1) * S], o_wT)
            last.then_inc(sem("s1_ps"), 1)
            if STAGES < 3:
                return

            pe.wait_ge(sem("ld_f0"), ndma["ld_f0"])
            for t in range(FT2):
                tr(bank(0)[:, 64 + t * E2:64 + (t + 1) * E2], b1n[0:E2, t * 128:(t + 1) * 128], E2)
            pe.wait_ge(sem("kk_ready"), 1)
            for i in range(2):
                last = tr(bank(0)[:, i * E2:(i + 1) * E2], kk_nat[0:E2, i, :], E2)
            last.then_inc(sem("keysT_ps"), 1)
            turn_y(2, 3)
            pe.wait_ge(sem("keysT_ready"), 1)
            pe.wait_ge(sem("yT_ready"), 2)
            for b in range(B):
                o = bank(1)[:, b * E2:(b + 1) * E2]
                mm(o, yT[:, b * S:(b + 1) * S], keysT[:, 1, :], stop=False)
                mm(o, ones[:, 0:S], keysT[:, 0, :], start=False, stop=False)
                last = mm(o, ones[0:1, 0:S], rows[0:1, 128:128 + E2], start=False)
            last.then_inc(sem("logit_ps"), 1)

            def turn_weights0(e):
                pe.wait_ge(sem(f"w0_{e % 2}"), 32 * (e // 2 + 1))
                if e >= 1:
                    pe.wait_ge(sem("w1T_ready"), e)
                    pe.wait_ge(sem("w2T_ready"), e)
                for t in range(FT2):
                    last = tr(bank(4)[:, t * 128:(t + 1) * 128], w1n[e % 2][:, t, :])
                last.then_inc(sem("w1T_ps"), 1)
                for t in range(FT2):
                    last = tr(bank(5)[:, t * 128:(t + 1) * 128], w2n[e % 2][:, t * 128:(t + 1) * 128])
                last.then_inc(sem("f0_turned"), 1)

            turn_weights0(0)
            pe.wait_ge(sem("w_ready"), 2)
            for b in range(B):
                last = tr(bank(0)[0:E2, b * S:(b + 1) * S], wgt[:, b, :])
            last.then_inc(sem("rT_ps"), 1)
            pe.wait_ge(sem("rT_ready"), 2)
            for b in range(B):
                last = mm(bank(2)[:, b * D:(b + 1) * D], rT_sb[0:E2, b * S:(b + 1) * S], b2n[0:E2, :])
            last.then_inc(sem("b2_ps"), 1)

            def down0(e):
                pe.wait_ge(sem("w2T_ready"), e + 1)
                if e >= 2:
                    pe.wait_ge(sem("acc0_ready"), e - 1)
                for b in range(B):
                    for t in range(FT2):
                        if b == 0:
                            pe.wait_ge(sem("gelu_done"), FT2 * e + t + 1)
                        last = mm(bank(6 + e % 2)[:, b * D:(b + 1) * D], hT2[e % 2][:, t, b * S:(b + 1) * S],
                                  w2T[e % 2][:, t, :], start=(t == 0), stop=(t == FT2 - 1))
                last.then_inc(sem("down0_ps"), 1)

            for e in range(E2):
                pe.wait_ge(sem("w1T_ready"), e + 1)
                if e == 0:
                    pe.wait_ge(sem("acc0_start"), 1)
                for t in range(FT2):
                    k = FT2 * e + t
                    if k >= 4:
                        pe.wait_ge(sem("gelu_done"), k - 3)
                    mm(bank(k % 4), w1T[e % 2][:, t * 128:(t + 1) * 128], yT).then_inc(sem("up0_ps"), 1)
                if e + 1 < E2:
                    turn_weights0(e + 1)
                down0(e)
            if STAGES < 4:
                return

            pe.wait_ge(sem("ld_x3"), ndma["ld_x3"])
            pe.wait_ge(sem("acc0_ready"), E2)
            for i in range(2):
                for j in range(4):
                    last = tr(bank(i)[:, j * 128:(j + 1) * 128], wq_nat[:, (4 * i + j) * 128:(4 * i + j + 1) * 128])
                last.then_inc(sem("x3w_ps"), 1)
            for i in range(4):
                if i >= 2:
                    pe.wait_ge(sem("x3w_ready"), i - 1)
                for j in range(4):
                    f, c = divmod(4 * i + j, 2)
                    last = tr(bank((2 + i) % 4)[:, j * 128:(j + 1) * 128], wk_nat[:, c, f * 128:(f + 1) * 128])
                last.then_inc(sem("x3w_ps"), 1)
            pe.wait_ge(sem("x3w_ready"), 6)
            for h in range(H3):
                p = 64 * (h % 2)
                i = h // 2
                if h % 2 == 0 and i >= 2:
                    pe.wait_ge(sem("a3_ready"), i - 1)
                last = mm(bank(4 + 2 * (i % 2) + h % 2)[:, 0:DC], wqT[p:p + 64, h // 2, :],
                          wkT[p:p + 64, h // 2, :])
                if h % 2:
                    last.then_inc(sem("a3_ps"), 1)
            for h in range(H3):
                p = 64 * (h % 2)
                last = mm(bank(h % 2)[:, h:h + 1], wqT[p:p + 64, h // 2, :], nk_col[p:p + 64, :])
            last.then_inc(sem("wn_ps"), 1)

            turn_y(3, 3)
            pe.wait_ge(sem("yT_ready"), 3)
            pe.wait_ge(sem("wn_ready"), 1)
            for b in range(B):
                last = mm(bank(1)[:, b * H3:(b + 1) * H3], yT[:, b * S:(b + 1) * S], wn)
            last.then_inc(sem("sim0_ps"), 1)
            pe.wait_ge(sem("a3_ready"), 8)
            pe.wait_ge(sem("sim0_ready"), 1)
            for i in range(H3 * CT):
                h, c = divmod(i, CT)
                if i >= 4:
                    pe.wait_ge(sem("qk3_ready"), i - 3)
                mm(bank(i % 4), A3[:, h, c * 128:(c + 1) * 128], yT).then_inc(sem("qk3_ps"), 1)

            nv6 = [0]

            def ctx_turn(i):
                pe.wait_ge(sem(f"ctx_in{i % 2}"), 16 * (i // 2 + 1))
                if nv6[0]:
                    pe.wait_ge(sem("bank6_free"), nv6[0])
                nv6[0] += 1
                for c in range(2):
                    for t in range(CT):
                        last = tr(bank(6)[:, (t * 2 + c) * 128:(t * 2 + c + 1) * 128],
                                  ctx_nat[i % 2][:, c, t * 128:(t + 1) * 128])
                last.then_inc(sem("ctx_turned"), 1)

            def v_proj(n):
                g, c = divmod(n, NCH)
                b = g // 2
                pe.wait_ge(sem("ctxT_ready"), b * 8 + c // 2 + 1)
                if c == 0:
                    pe.wait_ge(sem("wv_ready"), 1)
                if nv6[0]:
                    pe.wait_ge(sem("bank6_free"), nv6[0])
                nv6[0] += 1
                k, f = b % 2, (g % 2) * 512
                first = True
                for t in range(CT):
                    ch, cl = cT_hi[k][:, t, c * 128:(c + 1) * 128], cT_lo[k][:, t, c * 128:(c + 1) * 128]
                    wh, wl = wv_hi[:, t, f:f + 512], wv_lo[:, t, f:f + 512]
                    mm(bank(6), ch, wh, start=(t == 0), stop=False)
                    mm(bank(6), ch, wl, start=False, stop=False)
                    last = mm(bank(6), cl, wh, start=False, stop=(t == CT - 1))
                last.then_inc(sem("v3_ps"), 1)

            def scores3(u):
                b, h = divmod(u, H3)
                if u >= 1:
                    pe.wait_ge(sem("exp_done"), u)
                if h == 0:
                    pe.wait_ge(sem("ctxT_ready"), 8 * (b + 1))
                k = b % 2
                for j in range(4):
                    for t in range(CT):
                        qh, ql = qk_hi[:, h, t, b * S:(b + 1) * S], qk_lo[:, h, t, b * S:(b + 1) * S]
                        ch, cl = cT_hi[k][:, t, j * 512:(j + 1) * 512], cT_lo[k][:, t, j * 512:(j + 1) * 512]
                        mm(bank(j), qh, ch, start=(t == 0), stop=False)
                        mm(bank(j), qh, cl, start=False, stop=False)
                        last = mm(bank(j), ql, ch, start=False, stop=(t == CT - 1))
                    if j % 2:
                        last.then_inc(sem("s3_ps"), 1)

            def p_turn(u, g):
                n = 4 * u + g
                if g == 0:
                    pe.wait_ge(sem("exp_done"), u + 1)
                if n >= 2:
                    pe.wait_ge(sem(f"pT_ready{n % 2}"), n // 2)
                for j in range(4):
                    c = 4 * g + j
                    last = tr(bank(4 + n % 2)[:, j * 128:(j + 1) * 128], p3[u % 2][:, c * 128:(c + 1) * 128])
                last.then_inc(sem("pT_ps"), 1)

            def pv(u):
                if u >= 1:
                    pe.wait_ge(sem("o_head"), u)
                for c in range(NCH):
                    if c % 4 == 0:
                        n = 4 * u + c // 4
                        pe.wait_ge(sem(f"pT_ready{n % 2}"), n // 2 + 1)
                    hh = (u % H3) % 8
                    last = mm(bank(7)[:, 0:DH3], pT3[:, c, :], v3[(u // 8) % 2][:, c, hh * DH3:(hh + 1) * DH3],
                              start=(c == 0), stop=(c == NCH - 1))
                last.then_inc(sem("pv_ps"), 1)

            def out_proj3(b):
                pe.wait_ge(sem("o_head"), H3 * (b + 1))
                for i in range(2):
                    n = 2 * b + i
                    k = 4 * H3 * (b + 1)
                    pe.wait_ge(sem(f"pT_ready{i}"), k // 2)
                    if b >= 1 or i >= 0:
                        pass
                    for j in range(4):
                        f = 4 * i + j
                        last = tr(bank(4 + i)[:, j * 128:(j + 1) * 128], zat[:, f * 128:(f + 1) * 128])
                    last.then_inc(sem("oT_ps"), 1)
                pe.wait_ge(sem("oT_ready"), 2 * (b + 1))
                for f in range(8):
                    last = mm(bank(7)[:, 0:D], oT3[:, f, :], wout_sb[:, f, :], start=(f == 0), stop=(f == 7))
                last.then_inc(sem("o3_ps"), 1)

            pe.wait_ge(sem("qk3_ready"), H3 * CT)
            for i in range(8):
                ctx_turn(i)
            for n in range(NCH):
                v_proj(n)
            NU = B * H3
            for u in range(NU + 1):
                if u < NU:
                    scores3(u)
                n = NCH + 2 * u
                project = u < NU and n < 2 * B * NCH
                late = u % 8 == 0 and u > 0
                if project and not late:
                    v_proj(n)
                if u >= 1:
                    p_turn(u - 1, 0)
                    p_turn(u - 1, 1)
                if project and not late:
                    v_proj(n + 1)
                if u >= 1:
                    p_turn(u - 1, 2)
                    p_turn(u - 1, 3)
                b, h = divmod(u, H3)
                if u < NU and b + 1 < B and h < 8:
                    ctx_turn(8 * (b + 1) + h)
                if u >= 1:
                    pv(u - 1)
                if project and late:
                    v_proj(n)
                    v_proj(n + 1)
                if u >= 1 and u % H3 == 0:
                    out_proj3(u // H3 - 1)
            if STAGES < 5:
                return

            turn_y(4, 3)
            pe.wait_ge(sem("ld_a1"), ndma["ld_a1"])
            pe.wait_ge(sem("yT_ready"), 4)
            mm(bank(0), wqkv_sb[:, 0:D], yT)
            mm(bank(1), wqkv_sb[:, D:2 * D], yT).then_inc(sem("qk4_ps"), 1)
            for b in range(B):
                o = bank(2)[:, b * D:(b + 1) * D]
                mm(o, yT[:, b * S:(b + 1) * S], wqkv_sb[:, 2 * D:3 * D], stop=False)
                last = mm(o, ones[0:1, 0:S], rows4[0:1, 0:D], start=False)
            last.then_inc(sem("v4_ps"), 1)
            pe.wait_ge(sem("v4_ready"), 1)

            def scores4(b):
                pe.wait_ge(sem("kbd_ready"), b + 1)
                if b >= 1:
                    pe.wait_ge(sem("d4_ready"), b)
                for j in range(4):
                    last = mm(bank(j), qT4[:, b * S:(b + 1) * S], kbd[:, b, 4 * j:4 * j + 4, :].rearrange("p a b -> p (a b)"))
                last.then_inc(sem("s4_ps"), 1)

            def mix4(b):
                pe.wait_ge(sem("p4_ready"), b + 1)
                for g in range(4):
                    n = 4 * b + g
                    if n >= 2:
                        pe.wait_ge(sem("pT4_ready"), n - 1)
                    for j in range(4):
                        last = tr(bank(4 + n % 2)[:, j * 128:(j + 1) * 128], p4[:, 4 * g + j, :])
                    last.then_inc(sem("pT4_ps"), 1)
                pe.wait_ge(sem("pT4_ready"), 4 * b + 4)
                if b >= 1:
                    pe.wait_ge(sem("z4_ready"), b)
                W = DH4 + 1
                for h in range(H4):
                    last = mm(bank(6)[:, h * W:(h + 1) * W], pT4[:, h, :], v4[:, b, h, :])
                last.then_inc(sem("o4_ps"), 1)

            def proj4(b):
                pe.wait_ge(sem("z4_ready"), b + 1)
                if b >= 1:
                    pe.wait_ge(sem("s4_out"), b)
                tr(bank(7)[:, 0:128], z4).then_inc(sem("zT4_ps"), 1)
                pe.wait_ge(sem("zT4_ready"), b + 1)
                o = bank(7)[:, 128:256]
                mm(o, zT4, wproj_sb, stop=False)
                mm(o, ones[0:1, 0:S], rows4[0:1, D:2 * D], start=False).then_inc(sem("s4o_ps"), 1)

            scores4(0)
            for b in range(B):
                if b + 1 < B:
                    scores4(b + 1)
                mix4(b)
                proj4(b)
            if STAGES < 6:
                return

            turn_y(5, 3)
            pe.wait_ge(sem("ld_g1"), ndma["ld_g1"])
            pe.wait_ge(sem("yT_ready"), 5)
            for b in range(B):
                last = mm(bank(0)[:, b * E5:(b + 1) * E5], yT[:, b * S:(b + 1) * S], f1g)
            last.then_inc(sem("logit_ps"), 1)
            pe.wait_ge(sem("l5_ready"), 1)

            def up5(e, t):
                k = FT5 * e + t
                lo = 2 * (k % 3)
                if k >= 3:
                    pe.wait_ge(sem("h5_ready"), k - 2)
                if t == 0:
                    pe.wait_ge(sem(f"w5_{e % 2}"), 48 * (e // 2 + 1))
                mm(bank(lo), w1g[e % 2][:, t * 128:(t + 1) * 128], yT)
                mm(bank(lo + 1), w3g[e % 2][:, t * 128:(t + 1) * 128], yT).then_inc(sem("up5_ps"), 1)

            def down5(e):
                pe.wait_ge(sem("h5_ready"), FT5 * (e + 1))
                if e >= 2:
                    pe.wait_ge(sem("acc5_ready"), e - 1)
                for b in range(B):
                    for t in range(FT5):
                        last = mm(bank(6 + e % 2)[:, b * D:(b + 1) * D], hT5[e % 2][:, t, b * S:(b + 1) * S],
                                  w2g[e % 2][:, t, :], start=(t == 0), stop=(t == FT5 - 1))
                last.then_inc(sem("f1_used"), 1)

            for e in range(E5 + 1):
                for t in range(FT5):
                    if e < E5:
                        up5(e, t)
                    if t == 0 and e >= 1:
                        down5(e - 1)

        @block.vector
        def _(dve):
            n = [0]

            def step(ins):
                n[0] += 1
                ins.then_inc(sem("dve_step"), 1)
                dve.wait_ge(sem("dve_step"), n[0])

            def tt(o, a, b, op):
                return dve.tensor_tensor(o, a, b, op)

            def ts(o, a, s1, op0, s2=None, op1=None):
                if s2 is None:
                    return dve.tensor_scalar(o, a, s1, None, op0)
                return dve.tensor_scalar(o, a, s1, s2, op0, op1)

            def stt(o, a, s, b, op0, op1):
                return dve.scalar_tensor_tensor(out=o, in0=a, scalar=s, in1=b, op0=op0, op1=op1)

            def rsqrt(o, v, t):
                step(dve.tensor_scalar(t.bitcast(I32), v.bitcast(I32), 1, None, ALU.logical_shift_right))
                step(ts(o.bitcast(I32), t.bitcast(I32), -1.0, ALU.mult, MAGIC, ALU.add))
                for _ in range(3):
                    step(stt(t, o, -0.5, o, ALU.mult, ALU.mult))
                    step(tt(t, t, v, ALU.mult))
                    step(stt(o, t, 1.5, o, ALU.add, ALU.mult))

            def moments(src):
                for b in range(B):
                    ins = dve.bn_stats(stats[:, b, :], src[:, b, :])
                step(ins)
                for b in range(B):
                    ins = dve.bn_aggr(mv[:, b, :], stats[:, b, :])
                step(ins)

            mean, var = (lambda b: mv[:, b, 0:1]), mv[:, :, 1]

            def layernorm(stage):
                src = xs[stage % 3]
                moments(src)
                v, r, t = small[:, 0, 0:B], small[:, 1, 0:B], small[:, 2, 0:B]
                step(ts(v, var, LN_EPS, ALU.add))
                rsqrt(r, v, t)
                if stage == 2:
                    q = small[:, 3, 0:B]
                    step(tt(q, r, r, ALU.mult))
                    step(stt(q, q, float(D), var, ALU.mult, ALU.mult))
                for b in range(B):
                    ins = ts(y[:, b, :], src[:, b, :], mean(b), ALU.subtract, r[:, b:b + 1], ALU.mult)
                ins.then_inc(sem("y_ready"), 1)

            def yT_copy(stage):
                dve.wait_ge(sem("yT_ps"), stage + 1)
                dve.tensor_copy(yT, bank(3)).then_inc(sem("yT_ready"), 1)

            def route(stage, k, E, logits, by_prob, cmp_t):
                K = {1: 1, 2: 2, 5: 3}[stage]
                mx, d, ex = route_s[:, 0, 0:B], route_s[:, 1, 0:B * E].rearrange("p (b e) -> p b e", b=B), \
                    route_s[:, 2, 0:B * E].rearrange("p (b e) -> p b e", b=B)
                rank = route_s[:, 3, 0:B * E].rearrange("p (b e) -> p b e", b=B)
                den = route_s[:, 4, 0:B]
                step(dve.tensor_reduce(mx, logits, AX.X, ALU.max))
                tt(d, logits, bc(mx, 2, E), ALU.subtract).then_inc(sem("route_d"), 1)
                dve.wait_ge(sem("route_e"), K)
                by = ex if by_prob else logits
                step(tt(cmp_t, bc(by, 2, E), bc(by, 3, E), ALU.subtract))
                step(tt(cmp_t, cmp_t, bc(rank_t[:, 0:E, 0:E], 1, B), ALU.is_ge))
                step(dve.tensor_reduce(rank, cmp_t, AX.X, ALU.add))
                step(ts(rank, rank, float(k), ALU.is_lt))
                step(tt(ex, ex, rank, ALU.mult))
                step(dve.tensor_reduce(den, ex, AX.X, ALU.add))
                step(dve.reciprocal(den, den))
                tt(wgt[:, :, 0:E], ex, bc(den, 2, E), ALU.mult).then_inc(sem("w_ready"), 1)
                return rank

            dve.wait_ge(sem("ld_x"), 16)
            moments(xs[0])
            v, r, t = small[:, 0, 0:B], small[:, 1, 0:B], small[:, 2, 0:B]
            v2, r2 = small[:, 3, 0:B], small[:, 4, 0:B]
            step(ts(v, var, LN_EPS, ALU.add))
            rsqrt(r, v, t)
            step(tt(v2, var, r, ALU.mult))
            step(tt(v2, v2, r, ALU.mult))
            step(ts(v2, v2, RMS_EPS, ALU.add))
            rsqrt(r2, v2, t)
            step(tt(r2, r2, r, ALU.mult))
            for b in range(B):
                ins = ts(y[:, b, :], xs[0][:, b, :], mean(b), ALU.subtract, r2[:, b:b + 1], ALU.mult)
            ins.then_inc(sem("y_ready"), 1)
            dve.wait_ge(sem("ld_patch"), 16)
            pl = patch_i.rearrange("p b c -> p (b c)")
            ts(parts_i[:, 0, :], pl, 2047, ALU.bitwise_and)
            ts(parts_i[:, 1, :], pl, 11, ALU.logical_shift_right, 2047, ALU.bitwise_and)
            step(ts(parts_i[:, 2, :], pl, 22, ALU.logical_shift_right, 1023, ALU.bitwise_and))
            step(dve.tensor_copy(parts_f, parts_i.rearrange("p a b -> p (a b)")))
            dve.wait_ge(sem("const_a"), 1)
            dve.tensor_tensor_scan(scan, reset, parts_f, 0.0, ALU.mult, ALU.add).then_inc(sem("scan_ready"), 1)
            ts(iotap[:, 1:2], iotap_i[:, 0:1], 1.0, ALU.add)
            dve.tensor_copy(iota8, iota16_i[:, 0:8])
            ts(iota16, iota16_i[:, 0:16], 1.0, ALU.add)
            dve.wait_ge(sem("prefix_ps"), 1)
            dve.wait_ge(sem("scan_ready"), 1)
            step(tt(cum_i.rearrange("p a (b c) -> p (a b) c", c=NCH), scan.rearrange("p (a c) -> p a c", c=NCH),
                    bc(bank(1)[:, 0:12], 2, NCH), ALU.add))
            P = [pint[:, i, :] for i in range(12)]
            step(ts(P[0], cum_i[:, 0, :], 2047.0, ALU.add))
            step(ts(P[1], P[0], 11, ALU.logical_shift_right))
            step(stt(P[2], cum_i[:, 1, :], 2047.0, P[1], ALU.add, ALU.add))
            step(ts(P[3], P[2], 11, ALU.logical_shift_right))
            step(stt(P[4], cum_i[:, 2, :], 1023.0, P[3], ALU.add, ALU.add))
            ts(P[5], P[0], 1920, ALU.bitwise_and)
            ts(P[6], P[2], 2047, ALU.bitwise_and)
            ts(P[7], P[4], 1023, ALU.bitwise_and)
            ts(P[8], P[0], 15, ALU.bitwise_and)
            step(ts(P[9], P[0], 4, ALU.logical_shift_right, 7, ALU.bitwise_and))
            step(tt(pflt[:, 0, :], P[5], P[6], ALU.add))
            step(tt(pflt[:, 0, :], pflt[:, 0, :], P[7], ALU.add))
            step(ts(pflt[:, 1, :], pflt[:, 0, :], 0.0, ALU.is_equal))
            step(stt(pflt[:, 1, :], pflt[:, 0, :], float(1920 + 2047 + 1023), pflt[:, 1, :], ALU.is_equal, ALU.add))
            step(stt(pflt[:, 2, :], P[8], 1.0, pflt[:, 1, :], ALU.add, ALU.mult))
            step(dve.tensor_copy(pflt[:, 3, :], P[9]))
            tt(lo_oh, bc(pflt[:, 2, :], 2, 16), bc(iota16, 1, 64), ALU.is_equal)
            tt(hi_oh, bc(pflt[:, 3, :], 2, 8), bc(iota8, 1, 64), ALU.is_equal).then_inc(sem("onehot_ready"), 1)
            dve.wait_ge(sem("ssq_ready"), 1)
            dve.wait_ge(sem("ld_s0"), ndma["ld_s0"])
            v5, r5 = small[:, 5, 0:B], small[:, 6, 0:B]
            step(ts(v5, small[:, 7, 0:B], 1.0 / DC, ALU.mult, RMS_EPS, ALU.add))
            rsqrt(r5, v5, t)
            step(ts(r5, r5, BCOEF, ALU.mult))
            for b in range(B):
                ins = stt(u0[:, b, :], c0[:, b, 0:D], r5[:, b:b + 1], ginit_bc, ALU.mult, ALU.mult)
            step(ins)
            dve.wait_ge(sem("w_inT_ps"), 1)
            ts(w_inT, bank(0)[:, 0:D], biases[:, 0:1], ALU.mult).then_inc(sem("w0T_ready"), 1)
            dve.wait_ge(sem("yT_ps"), 1)
            dve.tensor_copy(r0T, bank(3)).then_inc(sem("r0T_ready"), 1)
            dve.wait_ge(sem("count_ps"), 1)
            ts(bnd[0:8], bank(1)[0:8, 64:128].rearrange("p (b l) -> p b l", b=B), 1.0, ALU.min)\
                .then_inc(sem("bnd_ready"), 1)
            dve.wait_ge(sem("plug_ps"), 1)
            fl = lambda a: a.rearrange("p b s -> p (b s)")
            step(ts(fl(t0), bank(2), 1.0, ALU.max, iotap[:, 1:2], ALU.subtract))
            ts(fl(e0), fl(t0), 0.0, ALU.max).then_inc(sem("plug_ready"), 1)
            dve.wait_ge(sem("pw_ready"), 1)
            stt(fl(wt0), fl(t0), 0.0, fl(e0), ALU.is_ge, ALU.mult).then_inc(sem("wt0_ready"), 1)
            dve.wait_ge(sem("s0_ps"), 1)
            tt(xs[1][:].rearrange("p b d -> p (b d)"), xs[0][:].rearrange("p b d -> p (b d)"), bank(4), ALU.add)\
                .then_inc(sem("x_ready"), 1)
            dve.wait_ge(sem("bd_ps"), 1)
            dve.wait_ge(sem("const_b"), 1)
            tt(bdT, bank(5).rearrange("p (a b) -> p a b", a=4),
               bc(blk16.rearrange("p a b -> p (a b)"), 1, 4), ALU.mult).then_inc(sem("bd_ready"), 1)
            if STAGES < 2:
                return

            dve.wait_ge(sem("x_ready"), 1)
            layernorm(1)
            yT_copy(1)
            dve.wait_ge(sem("logit_ps"), 1)
            lg = route_s[:, 5, 0:B * E1].rearrange("p (b e) -> p b e", b=B)
            step(dve.tensor_copy(lg, bank(0)[:, 0:B * E1].rearrange("p (b e) -> p b e", b=B)))
            rank1 = route(1, TOPK1, E1, lg, True, cmp[:, :, 0:E1, 0:E1].rearrange("p b e f -> p b e f"))
            dve.wait_ge(sem("qk1_sb"), 1)
            step(tt(q1, q1, bank(2), ALU.mult))
            dve.sem_inc(sem("k1_ready"), 1)
            mask8 = blk16[:, :, 0]
            for b in range(B):
                tt(qbd[:, b, :, :], bc(q1[:, b * S:(b + 1) * S], 1, H1), bc(mask8, 2, S), ALU.mult)\
                    .then_inc(sem("qbd_ready"), 1)
            for e in range(E1):
                dve.wait_ge(sem("qk1_sb"), e + 2)
                tt(kT1[:, e, :], kT1[:, e, :], bank(5 + 2 * (e % 2)), ALU.mult).then_inc(sem("k1_ready"), 1)
            for i in range(2 * B):
                b, g = divmod(i, 2)
                dve.wait_ge(sem("v1_ps"), i + 1)
                tt(v1[:, b, 4 * g:4 * g + 4, :], bank(1 + i % 2).rearrange("p (e d) -> p e d", e=4),
                   bc(rank1[:, b, 4 * g:4 * g + 4], 2, D), ALU.mult).then_inc(sem("v1_ready"), 1)
            dve.wait_ge(sem("rT_ps"), 1)
            dve.tensor_copy(rT_sb[0:E1, :], bank(0)[0:E1, :]).then_inc(sem("rT_ready"), 1)
            for e in range(E1):
                dve.wait_ge(sem("g_ps"), e + 1)
                tt(gmask[:, e, :, :], bank(0 if e % 2 else 3).rearrange("p (b s) -> p b s", b=B),
                   bc(causal[:], 1, B), ALU.mult).then_inc(sem("g_ready"), 1)
            dve.wait_ge(sem("g_ready"), E1)
            for i in range(B * E1):
                b, e = divmod(i, E1)
                lo = 2 * (i % 2)
                dve.wait_ge(sem("sc1_ps"), i + 1)
                if i >= 2:
                    dve.wait_ge(sem("o1_ps"), i - 1)
                tt(am[i % 2], ps[:, lo:lo + 2, :].rearrange("p a (h s) -> p (a h) s", h=4),
                   bc(gmask[:, e, b, :], 1, H1), ALU.mult).then_inc(sem("am_ready"), 1)
            dve.wait_ge(sem("sq1_ready"), 1)
            hs, hr, ht = small[:, 5, 0:B * H1], small[:, 6, 0:B * H1], small[:, 7, 0:B * H1]
            step(dve.tensor_reduce(hs, q1.rearrange("p (h v) -> p h v", v=DK1), AX.X, ALU.add))
            step(ts(hs, hs, 1.0 / DK1, ALU.mult, LN_EPS, ALU.add))
            rsqrt(hr, hs, ht)
            tt(y.rearrange("p b d -> p (b d)").rearrange("p (h v) -> p h v", v=DK1),
               bank(4).rearrange("p (h v) -> p h v", v=DK1), bc(hr, 2, DK1), ALU.mult).then_inc(sem("z1_ready"), 1)
            dve.wait_ge(sem("z1T_ps"), 1)
            dve.tensor_copy(yT, bank(5)).then_inc(sem("z1T_ready"), 1)
            if STAGES > 2:
                dve.wait_ge(sem("ld_f0"), ndma["ld_f0"])
                stt(kk_nat[0:E2, 1, :], kk_nat[0:E2, 0, :], 2.0, kk_nat[0:E2, 1, :], ALU.mult, ALU.add)\
                    .then_inc(sem("kk_ready"), 1)
            dve.wait_ge(sem("s1_ps"), 1)
            tt(xs[2][:].rearrange("p b d -> p (b d)"), xs[1][:].rearrange("p b d -> p (b d)"), bank(6), ALU.add)\
                .then_inc(sem("x_ready"), 1)
            if STAGES < 3:
                return

            dve.wait_ge(sem("x_ready"), 2)
            layernorm(2)
            dve.wait_ge(sem("keysT_ps"), 1)
            step(dve.tensor_copy(keysT, bank(0)[:, 0:2 * E2].rearrange("p (a e) -> p a e", a=2)))
            dve.tensor_copy(b1T, bank(0)[:, 64:64 + FT2 * E2].rearrange("p (a e) -> p a e", a=FT2))
            step(stt(keysT[:, 0, :], keysT[:, 0, :], -1.0, keysT[:, 0, :], ALU.mult, ALU.mult))
            dve.sem_inc(sem("keysT_ready"), 1)
            yT_copy(2)
            dve.wait_ge(sem("logit_ps"), 2)
            lg = route_s[:, 5, 0:B * E2].rearrange("p (b e) -> p b e", b=B)
            step(tt(lg, bank(1)[:, 0:B * E2].rearrange("p (b e) -> p b e", b=B), bc(small[:, 3, 0:B], 2, E2),
                    ALU.subtract))
            route(2, TOPK2, E2, lg, False, cmp)
            dve.wait_ge(sem("rT_ps"), 2)
            dve.tensor_copy(rT_sb[0:E2, :], bank(0)[0:E2, :]).then_inc(sem("rT_ready"), 1)
            dve.wait_ge(sem("b2_ps"), 1)
            acc = xs[0]
            tt(acc[:].rearrange("p b d -> p (b d)"), xs[2][:].rearrange("p b d -> p (b d)"), bank(2), ALU.add)\
                .then_inc(sem("acc0_start"), 1)

            def w2T_copy(e):
                dve.wait_ge(sem("f0_turned"), e + 1)
                if e >= 2:
                    dve.wait_ge(sem("down0_ps"), e - 1)
                dve.tensor_copy(w2T[e % 2].rearrange("p a b -> p (a b)"), bank(5)).then_inc(sem("w2T_ready"), 1)

            def gather_expert(acc, w, bk):
                for b in range(B):
                    ins = stt(acc[:, b, :], bank(bk)[:, b * D:(b + 1) * D], w[:, b, :], acc[:, b, :],
                              ALU.mult, ALU.add)
                return ins

            w2T_copy(0)
            dve.wait_ge(sem("acc0_start"), 1)
            for e in range(E2):
                if e + 1 < E2:
                    w2T_copy(e + 1)
                dve.wait_ge(sem("down0_ps"), e + 1)
                if e >= 1:
                    dve.wait_ge(sem("acc0_ready"), e)
                gather_expert(acc, wgt[:, :, e:e + 1], 6 + e % 2).then_inc(sem("acc0_ready"), 1)
            dve.wait_ge(sem("acc0_ready"), E2)
            dve.sem_inc(sem("x_ready"), 1)
            if STAGES < 4:
                return

            layernorm(3)
            for i in range(2):
                dve.wait_ge(sem("x3w_ps"), i + 1)
                dve.tensor_copy(wqT[:, 4 * i:4 * i + 4, :].rearrange("p a b -> p (a b)"), bank(i))\
                    .then_inc(sem("x3w_ready"), 1)
            for i in range(4):
                dve.wait_ge(sem("x3w_ps"), i + 3)
                dve.tensor_copy(wkT[:, 2 * i:2 * i + 2, :].rearrange("p a b -> p (a b)"), bank((2 + i) % 4))\
                    .then_inc(sem("x3w_ready"), 1)
            dve.wait_ge(sem("wn_ps"), 1)
            ts(wn[:, 0:H3:2], bank(0)[:, 0:H3:2], DH3 ** -0.5, ALU.mult)
            ts(wn[:, 1:H3:2], bank(1)[:, 1:H3:2], DH3 ** -0.5, ALU.mult).then_inc(sem("wn_ready"), 1)
            yT_copy(3)
            dve.wait_ge(sem("sim0_ps"), 1)
            s0v = bank(1)[:, 0:B * H3].rearrange("p (b h) -> p b h", b=B)
            dve.tensor_copy(sim0[:], s0v)
            ts(nsim0[:], s0v, -1.0, ALU.mult).then_inc(sem("sim0_ready"), 1)
            dve.wait_ge(sem("wvh_ready"), 1)
            tt(wv_lo[:], wv_nat, wv_hi[:], ALU.subtract).then_inc(sem("wv_ready"), 1)
            for i in range(H3 * CT):
                h, c = divmod(i, CT)
                dve.wait_ge(sem("qk3_hi"), i + 1)
                tt(qk_lo[:, h, c, :], bank(i % 4), qk_hi[:, h, c, :], ALU.subtract).then_inc(sem("qk3_ready"), 1)

            def ctx_lo(i):
                b, c = divmod(2 * i, NCH)
                k = b % 2
                dve.wait_ge(sem("ctx_hi"), i + 1)
                tt(cT_lo[k][:, :, c * 128:(c + 2) * 128], bank(6).rearrange("p (t s) -> p t s", t=CT),
                   cT_hi[k][:, :, c * 128:(c + 2) * 128], ALU.subtract).then_inc(sem("ctxT_ready"), 1)
                dve.wait_ge(sem("ctxT_ready"), i + 1)
                dve.sem_inc(sem("bank6_free"), 1)

            def v_copy(n):
                g, c = divmod(n, NCH)
                dve.wait_ge(sem("v3_ps"), n + 1)
                dve.tensor_copy(v3[g % 2][:, c, :], bank(6)).then_inc(sem("bank6_free"), 1)

            def pT_copy(u, g):
                m = 4 * u + g
                dve.wait_ge(sem("pT_ps"), m + 1)
                if g == 0 and u >= 1:
                    dve.wait_ge(sem("pv_ps"), u)
                dve.tensor_copy(pT3[:, 4 * g:4 * g + 4, :].rearrange("p a b -> p (a b)"), bank(4 + m % 2))\
                    .then_inc(sem(f"pT_ready{m % 2}"), 1)

            us = lambda u, i: unit_s[:, u % 2, i:i + 1]

            def maxima(u):
                b, h = divmod(u, H3)
                if u >= 2:
                    dve.wait_ge(sem("o_head"), u - 1)
                for j in range(2):
                    dve.wait_ge(sem("s3_ps"), 2 * u + j + 1)
                    ins = dve.tensor_reduce(us(u, j), ps[:, 2 * j:2 * j + 2, :], AX.XY, ALU.max, negate=True)
                step(ins)
                stt(us(u, 2), us(u, 0), us(u, 1), nsim0[:, b, h:h + 1], ALU.min, ALU.min).then_inc(sem("nmax_ready"), 1)

            def head_out(u):
                b, h = divmod(u, H3)
                dve.wait_ge(sem("p0_ready"), u + 1)
                step(tt(us(u, 5), us(u, 3), us(u, 4), ALU.add))
                step(dve.reciprocal(us(u, 5), us(u, 5)))
                dve.wait_ge(sem("pv_ps"), u + 1)
                if h == 0 and b >= 1:
                    dve.wait_ge(sem("oT_ready"), 2 * b)
                z = zat[:, h * DH3:(h + 1) * DH3]
                step(stt(z, nv_bc[:], us(u, 4), bank(7)[:, 0:DH3], ALU.mult, ALU.add))
                ts(z, z, us(u, 5), ALU.mult).then_inc(sem("o_head"), 1)

            for i in range(8):
                ctx_lo(i)
            for m in range(NCH):
                v_copy(m)
            NU = B * H3
            for u in range(NU + 1):
                if u < NU:
                    maxima(u)
                nn = NCH + 2 * u
                project = u < NU and nn < 2 * B * NCH
                late = u % 8 == 0 and u > 0
                if project and not late:
                    v_copy(nn)
                if u >= 1:
                    pT_copy(u - 1, 0)
                if u >= 1:
                    pT_copy(u - 1, 2)
                b, h = divmod(u, H3)
                if u < NU and b + 1 < B and h < 8:
                    ctx_lo(8 * (b + 1) + h)
                if u >= 1:
                    head_out(u - 1)
                if project and late:
                    v_copy(nn)
                if u >= 1 and u % H3 == 0:
                    bb = u // H3 - 1
                    dve.wait_ge(sem("o3_ps"), bb + 1)
                    dve.tensor_copy(xs[1][:, bb, :], bank(7)[:, 0:D]).then_inc(sem("o3_ready"), 1)
            dve.wait_ge(sem("o3_ready"), B)
            o3 = xs[1]
            moments(o3)
            step(ts(v, var, XLN_EPS, ALU.add))
            rsqrt(r, v, t)
            for b in range(B):
                ins = ts(o3[:, b, :], o3[:, b, :], mean(b), ALU.subtract, r[:, b:b + 1], ALU.mult)
            step(ins)
            step(tt(o3[:], o3[:], bc(lns_bc[:, 0, :], 1, B), ALU.mult))
            step(tt(o3[:], o3[:], bc(lns_bc[:, 1, :], 1, B), ALU.add))
            tt(o3[:], o3[:], xs[0][:], ALU.add).then_inc(sem("x_ready"), 1)
            if STAGES < 5:
                return

            dve.wait_ge(sem("x_ready"), 4)
            layernorm(4)
            yT_copy(4)
            dve.wait_ge(sem("qk4_ps"), 1)
            dve.wait_ge(sem("ld_a1"), ndma["ld_a1"])
            dve.wait_ge(sem("const_c"), 1)
            ts(qT4, bank(0), biases[:, 2:3], ALU.add, DH4 ** -0.5, ALU.mult)
            step(ts(kT4, bank(1), biases[:, 3:4], ALU.add))
            for b in range(B):
                tt(kbd[:, b, :, :], bc(kT4[:, b * S:(b + 1) * S], 1, H4), bc(m16, 2, S), ALU.mult)\
                    .then_inc(sem("kbd_ready"), 1)
                if b == 0:
                    dve.wait_ge(sem("v4_ps"), 1)
                    dve.tensor_copy(v4[:, :, :, 0:DH4],
                                    bank(2).rearrange("p (b h v) -> p b h v", b=B, h=H4)).then_inc(sem("v4_ready"), 1)

            def out4(b):
                dve.wait_ge(sem("s4o_ps"), b + 1)
                tt(xs[2][:, b, :], bank(7)[:, 128:256], xs[1][:, b, :], ALU.add).then_inc(sem("s4_out"), 1)

            def soft4(b):
                dve.wait_ge(sem("s4_ps"), b + 1)
                sv = ps[:, 0:4, :].rearrange("p a (h s) -> p (a h) s", h=4)
                step(dve.tensor_reduce(mx4, sv, AX.X, ALU.max))
                if b >= 1:
                    dve.wait_ge(sem("p4_ready"), b)
                tt(d4, sv, bc(mx4, 2, S), ALU.subtract).then_inc(sem("d4_ready"), 1)

            soft4(0)
            for b in range(B):
                if b + 1 < B:
                    soft4(b + 1)
                for g in (0, 2):
                    m = 4 * b + g
                    dve.wait_ge(sem("pT4_ps"), m + 1)
                    if b >= 1 and g == 0:
                        dve.wait_ge(sem("o4_ps"), b)
                    if m:
                        dve.wait_ge(sem("pT4_ready"), m)
                    dve.tensor_copy(pT4[:, 4 * g:4 * g + 4, :].rearrange("p a b -> p (a b)"), bank(4 + m % 2))\
                        .then_inc(sem("pT4_ready"), 1)
                dve.wait_ge(sem("o4_ps"), b + 1)
                o4 = bank(6)[:, 0:H4 * (DH4 + 1)].rearrange("p (h v) -> p h v", h=H4)
                step(dve.reciprocal(rs4, o4[:, :, DH4]))
                if b >= 1:
                    dve.wait_ge(sem("zT4_ps"), b)
                tt(z4.rearrange("p (h v) -> p h v", h=H4), o4[:, :, 0:DH4], bc(rs4, 2, DH4), ALU.mult)\
                    .then_inc(sem("z4_ready"), 1)
                dve.wait_ge(sem("zT4_ps"), b + 1)
                dve.tensor_copy(zT4, bank(7)[:, 0:128]).then_inc(sem("zT4_ready"), 1)
                out4(b)
            dve.wait_ge(sem("s4_out"), B)
            dve.sem_inc(sem("x_ready"), 1)
            if STAGES < 6:
                return

            layernorm(5)
            yT_copy(5)
            dve.wait_ge(sem("logit_ps"), 3)
            lg = route_s[:, 5, 0:B * E5].rearrange("p (b e) -> p b e", b=B)
            step(dve.tensor_copy(lg, bank(0)[:, 0:B * E5].rearrange("p (b e) -> p b e", b=B)))
            dve.sem_inc(sem("l5_ready"), 1)
            route(5, TOPK5, E5, lg, True, cmp5)
            acc = xs[0]
            step(dve.tensor_copy(acc[:], xs[2][:]))
            for e in range(E5 + 1):
                for t_ in range(FT5):
                    k = FT5 * e + t_
                    if e < E5:
                        dve.wait_ge(sem("silu_done"), k + 1)
                        if t_ == 0 and e >= 2:
                            dve.wait_ge(sem("f1_used"), e - 1)
                        tt(hT5[e % 2][:, t_, :], sg[k % 2], bank(2 * (k % 3) + 1), ALU.mult).then_inc(sem("h5_ready"), 1)
                    if e >= 1 and t_ == 1:
                        dve.wait_ge(sem("f1_used"), e)
                        if e >= 2:
                            dve.wait_ge(sem("acc5_ready"), e - 1)
                        if e == 1:
                            dve.wait_ge(sem("w_ready"), 3)
                        gather_expert(acc, wgt[:, :, e - 1:e], 6 + (e - 1) % 2).then_inc(sem("acc5_ready"), 1)
            dve.wait_ge(sem("acc5_ready"), E5)
            dve.sem_inc(sem("x_ready"), 1)

        @block.scalar
        def _(act):
            def copy(o, i, scale=1.0):
                return act.activation(o, i, ACT.Copy, scale=scale)

            act.wait_ge(sem("ld_c0"), 16)
            for b in range(B):
                if b:
                    act.wait_ge(sem("ssq_b"), b)
                ins = act.activation(sq_junk, c0[:, b, :], ACT.Square, accum_out=small[:, 7, b:b + 1])
                ins.then_inc(sem("ssq_b") if b < B - 1 else sem("ssq_ready"), 1)
            act.wait_ge(sem("plug_ready"), 1)
            e0f = e0.rearrange("p b s -> p (b s)")
            act.activation(e0f, e0f, ACT.Exp, scale=-DT).then_inc(sem("pw_ready"), 1)
            act.wait_ge(sem("og_ps"), 1)
            act.activation(o_wT, bank(6)[:, 0:D], ACT.Copy, scale=biases[:, 1:2])
            copy(gateT, bank(6)[:, D:D + E1]).then_inc(sem("og_ready"), 1)
            act.wait_ge(sem("mq_ps"), 1)
            act.activation(mqT[:, 0, :], bank(7)[:, 0:D], ACT.Copy, scale=DK1 ** -0.5)
            copy(mqT[:, 1, :], bank(7)[:, D:2 * D]).then_inc(sem("mq_ready"), 1)
            for i in range(4):
                act.wait_ge(sem("mk_ps"), i + 1)
                copy(mkT[:, 2 * i:2 * i + 2, :, :].rearrange("p a b c -> p (a b c)"), bank(5 + i % 2))\
                    .then_inc(sem("mk_ready"), 1)
            for g in range(2):
                act.wait_ge(sem("vw_ps"), g + 1)
                copy(v_wT[:, 4 * g:4 * g + 4, :].rearrange("p a b -> p (a b)"), bank(5 + g)).then_inc(sem("vw_ready"), 1)
            if STAGES < 2:
                return

            def route_exp(k, E):
                act.wait_ge(sem("route_d"), k)
                act.activation(route_s[:, 2, 0:B * E], route_s[:, 1, 0:B * E], ACT.Exp).then_inc(sem("route_e"), 1)

            route_exp(1, E1)
            act.wait_ge(sem("qk_ps"), 1)
            copy(q1, bank(1)).then_inc(sem("qk1_sb"), 1)
            for e in range(E1):
                act.wait_ge(sem("qk_ps"), e + 2)
                copy(kT1[:, e, :], bank(4 + 2 * (e % 2))).then_inc(sem("qk1_sb"), 1)
            act.wait_ge(sem("o1_ps"), B * E1)
            act.activation(q1, bank(4), ACT.Square).then_inc(sem("sq1_ready"), 1)
            if STAGES < 3:
                return

            route_exp(2, E2)

            def w1T_copy(e):
                act.wait_ge(sem("w1T_ps"), e + 1)
                copy(w1T[e % 2], bank(4)).then_inc(sem("w1T_ready"), 1)

            w1T_copy(0)
            for e in range(E2):
                for t in range(FT2):
                    k = FT2 * e + t
                    act.wait_ge(sem("up0_ps"), k + 1)
                    if t == 0 and e >= 2:
                        act.wait_ge(sem("down0_ps"), e - 1)
                    act.activation(hT2[e % 2][:, t, :], bank(k % 4), ACT.Gelu, bias=b1T[:, t, e:e + 1])\
                        .then_inc(sem("gelu_done"), 1)
                if e + 1 < E2:
                    w1T_copy(e + 1)
            if STAGES < 4:
                return

            for i in range(8):
                act.wait_ge(sem("a3_ps"), i + 1)
                copy(A3[:, 2 * i:2 * i + 2, :], ps[:, 4 + 2 * (i % 2):6 + 2 * (i % 2), 0:DC], DH3 ** -0.5)\
                    .then_inc(sem("a3_ready"), 1)
            act.wait_ge(sem("ld_wv"), 16)
            copy(wv_hi[:], wv_nat).then_inc(sem("wvh_ready"), 1)
            for i in range(H3 * CT):
                h, c = divmod(i, CT)
                act.wait_ge(sem("qk3_ps"), i + 1)
                copy(qk_hi[:, h, c, :], bank(i % 4)).then_inc(sem("qk3_hi"), 1)

            def ctx_hi(i):
                b, c = divmod(2 * i, NCH)
                act.wait_ge(sem("ctx_turned"), i + 1)
                copy(cT_hi[b % 2][:, :, c * 128:(c + 2) * 128], bank(6).rearrange("p (t s) -> p t s", t=CT))\
                    .then_inc(sem("ctx_hi"), 1)

            def v_copy(m):
                g, c = divmod(m, NCH)
                act.wait_ge(sem("v3_ps"), m + 1)
                copy(v3[g % 2][:, c, :], bank(6)).then_inc(sem("bank6_free"), 1)

            def pT_copy(u, g):
                m = 4 * u + g
                act.wait_ge(sem("pT_ps"), m + 1)
                if g == 1 and u >= 1:
                    act.wait_ge(sem("pv_ps"), u)
                copy(pT3[:, 4 * g:4 * g + 4, :].rearrange("p a b -> p (a b)"), bank(4 + m % 2))\
                    .then_inc(sem(f"pT_ready{m % 2}"), 1)

            us = lambda u, i: unit_s[:, u % 2, i:i + 1]

            def exps(u):
                b, h = divmod(u, H3)
                act.wait_ge(sem("nmax_ready"), u + 1)
                if u >= 2:
                    act.wait_ge(sem("pT_ps"), 4 * (u - 1))
                act.activation(p3[u % 2], ps[:, 0:4, :].rearrange("p a b -> p (a b)"), ACT.Exp, bias=us(u, 2),
                               accum_out=us(u, 3)).then_inc(sem("exp_done"), 1)
                act.activation(us(u, 4), sim0[:, b, h:h + 1], ACT.Exp, bias=us(u, 2)).then_inc(sem("p0_ready"), 1)

            for i in range(8):
                ctx_hi(i)
            NU = B * H3
            for u in range(NU + 1):
                if u < NU:
                    exps(u)
                nn = NCH + 2 * u
                if u >= 1:
                    pT_copy(u - 1, 1)
                project = u < NU and nn < 2 * B * NCH
                late = u % 8 == 0 and u > 0
                if project and not late:
                    v_copy(nn + 1)
                if u >= 1:
                    pT_copy(u - 1, 3)
                b, h = divmod(u, H3)
                if u < NU and b + 1 < B and h < 8:
                    ctx_hi(8 * (b + 1) + h)
                if project and late:
                    v_copy(nn + 1)
                if u >= 1 and u % H3 == 0:
                    bb = u // H3 - 1
                    for i in range(2):
                        act.wait_ge(sem("oT_ps"), 2 * bb + i + 1)
                        copy(oT3[:, 4 * i:4 * i + 4, :].rearrange("p a b -> p (a b)"), bank(4 + i))\
                            .then_inc(sem("oT_ready"), 1)
            if STAGES < 5:
                return

            for b in range(B):
                act.wait_ge(sem("d4_ready"), b + 1)
                if b >= 1:
                    act.wait_ge(sem("pT4_ps"), 4 * b)
                act.activation(p4, d4, ACT.Exp).then_inc(sem("p4_ready"), 1)
                for g in (1, 3):
                    m = 4 * b + g
                    act.wait_ge(sem("pT4_ps"), m + 1)
                    act.wait_ge(sem("pT4_ready"), m)
                    copy(pT4[:, 4 * g:4 * g + 4, :].rearrange("p a b -> p (a b)"), bank(4 + m % 2))\
                        .then_inc(sem("pT4_ready"), 1)
            if STAGES < 6:
                return

            route_exp(3, E5)
            for k in range(E5 * FT5):
                act.wait_ge(sem("up5_ps"), k + 1)
                if k >= 2:
                    act.wait_ge(sem("h5_ready"), k - 1)
                act.activation(sg[k % 2], bank(2 * (k % 3)), ACT.Silu).then_inc(sem("silu_done"), 1)


_INS = ['x', 'ctx_2048', 'mask_BxS2_if0', 'L0_xattn_W_in', 'L0_xattn_b_in', 'L0_xattn_g_res', 'L0_xattn_g_init',
        'L0_attn_gate_w', 'L0_attn_q_w', 'L0_attn_k_w', 'L0_attn_v_w', 'L0_attn_fmq1_w', 'L0_attn_fmq2_w',
        'L0_attn_fmk1_w', 'L0_attn_fmk2_w', 'L0_attn_norm_w', 'L0_attn_o_w',
        'L0_ffn_keys', 'L0_ffn_w1', 'L0_ffn_b1', 'L0_ffn_w2', 'L0_ffn_b2', 'L0_ffn_rw', 'L0_ffn_rb',
        'L1_xattn_Wq', 'L1_xattn_Wkv', 'L1_xattn_null_kv', 'L1_xattn_Wout', 'L1_xattn_ln_scale', 'L1_xattn_ln_bias',
        'L1_attn_w_qkv', 'L1_attn_b_qkv', 'L1_attn_w_proj', 'L1_attn_b_proj',
        'L1_ffn_gate_w', 'L1_ffn_w1', 'L1_ffn_w3', 'L1_ffn_w2']
_OUTS = [((4, 128, 128), 'float32')]


def kernel(**inputs):
    import numpy as _np
    import concourse.bacc as _bacc
    from concourse import mybir as _mybir
    from concourse.bass_utils import run_bass_kernel_spmd as _run

    nc = _bacc.Bacc("TRN2", target_bir_lowering=False, num_devices=1, dynamic_dma_scratch_size=1024)
    arrays, args = {}, []
    for name in _INS:
        a = _np.ascontiguousarray(inputs[name])
        arrays[f"in_{name}_dram"] = a
        args.append(nc.dram_tensor(f"in_{name}_dram", a.shape, _mybir.dt.from_np(a.dtype), kind="ExternalInput").ap())
    for i, (shape, dtype) in enumerate(_OUTS):
        dt = _mybir.dt.from_np(_np.dtype(dtype))
        args.append(nc.dram_tensor(f"out_{i}_dram", shape, dt, kind="ExternalOutput").ap())
    perceiver_kernel(nc, *args)
    r = _run(nc, [arrays], core_ids=[0])
    return r.results[0]["out_0_dram"]
```

```python
import concourse.bass as bass
from concourse import mybir
from concourse.alu_op_type import AluOpType as ALU
from contextlib import ExitStack
import numpy as np

STAGES = 6


def perceiver_kernel(nc, x, ctx_2048, patch_lens, L0_W_in, L0_b_in, L0_g_res, L0_g_init,
                     gate_w, q_w, k_w, v_w, fmq1, fmq2, fmk1, fmk2, norm_w, o_w,
                     keys, f0_w1, f0_b1, f0_w2, f0_b2, f0_rw, f0_rb,
                     Wq, Wkv, null_kv, Wout, ln_scale, ln_bias,
                     w_qkv, b_qkv, w_proj, b_proj, f1_gate, f1_w1, f1_w3, f1_w2, out):
    F32, F16, BF16, I32 = mybir.dt.float32, mybir.dt.float16, mybir.dt.bfloat16, mybir.dt.int32
    ACT = mybir.ActivationFunctionType
    AX = mybir.AxisListType

    B, S, D = x.shape
    NK, DC = ctx_2048.shape[1:]
    T = B * S
    NCH = NK // S
    CT = DC // 128
    E1, H1 = gate_w.shape[0], 8
    DK1 = D // H1
    E2, F2 = f0_w1.shape[0], f0_w1.shape[1]
    FT2 = F2 // 128
    H3 = Wq.shape[1] // 64
    DH3 = 64
    H4 = 16
    DH4 = D // H4
    E5, F5 = f1_w1.shape[0], f1_w1.shape[2]
    FT5 = F5 // 128
    TOPK1, TOPK2, TOPK5 = 2, 4, 2
    LN_EPS, RMS_EPS, XLN_EPS = 1e-5, 1e-5, 1e-6
    LOGP = np.float32(-0.001)
    DT = float(-np.log(-np.expm1(LOGP)))
    BCOEF = float(np.exp(LOGP))
    MAGIC = float(0x5F3759DF)
    TINY = 1.1754944e-38
    LIFT = float(12 * np.log(2.0))

    es = ExitStack()
    with es:
        def sb(name, shape, dt=F32):
            return es.enter_context(nc.sbuf_tensor(name, shape, dt))

        names = {}

        def sem(name):
            if name not in names:
                names[name] = es.enter_context(nc.semaphore(name))
            return names[name]

        def bc(ap, axis, n):
            u = ap.unsqueeze(axis)
            shape = list(u.shape)
            shape[axis] = n
            return u.broadcast_to(shape)

        KB = 256
        arena = sb("arena", [128, 160 * KB])
        main = sb("main", [128, 24 * KB])

        def at(base, kb, shape, dt=F32):
            words = int(np.prod(shape)) * (2 if dt in (F16, BF16) else 4) // 4
            o = int(kb * KB)
            v = base[:, o:o + words]
            if dt is not F32:
                v = v.bitcast(dt)
            if len(shape) == 2:
                v = v.rearrange("p (a b) -> p a b", a=shape[0])
            elif len(shape) == 3:
                v = v.rearrange("p (a b c) -> p a b c", a=shape[0], b=shape[1])
            elif len(shape) == 4:
                v = v.rearrange("p (a b c d) -> p a b c d", a=shape[0], b=shape[1], c=shape[2])
            return v

        xs = [sb(f"x{i}", [128, B, D]) for i in range(3)]
        yy = sb("yy", [128, 2 * T])
        y = yy[:, 0:T].rearrange("p (b d) -> p b d", b=B)
        yT = yy[:, T:2 * T]
        zat = sb("zat", [128, H3 * DH3])
        ident = sb("ident", [128, 128])
        causal = sb("causal", [128, 128])
        ones = sb("ones", [128, 128])
        stats = sb("stats", [128, B, 6])
        mv = sb("mv", [128, B, 2])
        small = sb("small", [128, 9, 32])
        route_s = sb("route_s", [128, 6, 64])
        wgt = sb("wgt", [128, B, E2])
        ctx_nat = [sb(f"ctx_nat{i}", [128, 2, DC]) for i in range(2)]
        wv_hi = sb("wv_hi", [128, CT, 1024], F16)
        wv_lo = sb("wv_lo", [128, CT, 1024], F16)
        wout_sb = sb("wout_sb", [128, 8, D])
        nv_bc = sb("nv_bc", [128, DH3])
        lns_bc = sb("lns_bc", [128, 2, D])
        sim0 = sb("sim0", [128, B, H3])
        nsim0 = sb("nsim0", [128, B, H3])
        unit_s = sb("unit_s", [128, 2, 8])
        lift = sb("lift", [128, 1])
        biases = sb("biases", [128, 8])
        rows = at(arena, 148, [512])
        rows4 = at(arena, 68, [256])

        c0 = at(arena, 96, [B, DC])
        u0 = at(arena, 100, [B, D])
        wt0 = at(arena, 102, [B, S])
        t0 = at(arena, 104, [B, S])
        e0 = at(arena, 106, [B, S])
        patch_i = at(arena, 108, [B, NCH], I32)
        parts_i = at(arena, 108.25, [3, B * NCH], I32)
        parts_f = at(arena, 109, [3 * B * NCH])
        reset = at(arena, 109.75, [3 * B * NCH])
        scan = at(arena, 110.5, [3 * B * NCH])
        cum_i = at(arena, 111.25, [3, B * NCH], I32)
        pint = at(arena, 112, [12, 64], I32)
        pflt = at(arena, 115, [4, 64])
        lo_oh = at(arena, 116, [64, 16], BF16)
        hi_oh = at(arena, 118, [64, 8], BF16)
        iota16 = at(arena, 119, [16])
        iota8 = at(arena, 119.0625, [8])
        iotap = at(arena, 119.125, [2])
        iotap_i = at(arena, 119.25, [2], I32)
        iota16_i = at(arena, 119.5, [24], I32)
        mask16 = at(arena, 119.75, [16])
        bnd = at(arena, 120, [B, 16], BF16)
        after_b = at(arena, 152, [16, S], BF16)
        strict = at(arena, 121, [128])
        w_in = at(arena, 121.5, [D])
        w_inT = at(arena, 122, [D])
        ginit_bc = at(arena, 122.5, [D])
        r0T = at(arena, 123, [T])
        sq_junk = at(arena, 151, [DC])

        k_nat = at(arena, 136, [E1, D])
        v_nat = at(arena, 140, [E1, D])
        qo_nat = at(arena, 80, [2, D])
        gate_nat = at(arena, 81, [D])
        keysT = at(arena, 92, [2, E2])
        gateT = at(arena, 92.25, [E1])
        f_nat = at(arena, 82, [4, DK1])
        bdT = at(arena, 82.5, [4, 128])
        blk16 = at(arena, 84.5, [H1, DK1])
        o_wT = at(arena, 85, [D])
        mqT = at(arena, 86, [2, D])
        mkT = at(arena, 0, [E1, 2, D])
        v_wT = at(arena, 8, [E1, D])
        kT1 = at(arena, 12, [E1, T])
        qbd = at(arena, 28, [B, H1, S])
        v1 = at(arena, 44, [B, E1, D])
        gmask = at(arena, 60, [E1, B, S])
        am = [at(arena, 76, [H1, S]), at(arena, 87, [H1, S])]
        q1 = at(arena, 93, [T])
        f_rep = at(arena, 93, [4, H1, DK1])
        rT_sb = at(arena, 146, [T])
        rank_t = sb("rank_t", [128, E2, E2])

        w1n = [at(arena, 96 + 4 * i, [FT2, D]) for i in range(2)]
        w2n = [at(arena, 98 + 4 * i, [F2]) for i in range(2)]
        w1T = [at(arena, 104 + 4 * i, [F2]) for i in range(2)]
        w2T = [at(arena, 106 + 4 * i, [FT2, D]) for i in range(2)]
        hT2 = [at(arena, 112 + 8 * i, [FT2, T]) for i in range(2)]
        b1n = at(arena, 128, [F2])
        b2n = at(arena, 130, [D])
        b1T = at(arena, 130.5, [FT2, E2])
        cmp = at(arena, 131, [B, E2, E2])
        kk_nat = at(arena, 135, [2, D])

        qk_hi = at(arena, 0, [H3, CT, T], F16)
        qk_lo = at(arena, 32, [H3, CT, T], F16)
        v3 = [at(arena, 64 + 32 * i, [NCH, 8, 2 * DH3], F16) for i in range(2)]
        cT_hi = [at(arena, 128 + 16 * i, [CT, NK], F16) for i in range(2)]
        cT_lo = [at(arena, 136 + 16 * i, [CT, NK], F16) for i in range(2)]
        A3 = at(arena, 144, [H3, DC])
        wq_nat = at(main, 0, [1024])
        wk_nat = at(main, 4, [CT, 1024])
        wqT = at(main, 12, [8, 128])
        wkT = at(main, 16, [8, DC])
        wn = at(arena, 132, [H3])
        wv_nat = at(arena, 64, [CT, 1024])
        p3 = [at(main, 8 * i, [NK]) for i in range(2)]
        pT_hi = at(main, 16, [NCH, 128], F16)
        pT_lo = at(main, 20, [NCH, 128], F16)
        oT3 = yy[:, :].rearrange("p (f q) -> p f q", f=8)
        nk_col = sb("nk_col", [128, 1])

        wqkv_sb = at(arena, 0, [3 * D])
        wproj_sb = at(arena, 1.5, [D])
        qT4 = at(arena, 2, [T])
        kT4 = at(arena, 4, [T])
        kbd = at(arena, 6, [B, H4, S])
        v4 = at(arena, 38, [B, H4, DH4 + 1])
        d4 = at(arena, 41, [H4, S])
        p4 = at(arena, 49, [H4, S])
        pT4 = at(arena, 57, [H4, S])
        m16 = at(arena, 65, [H4])
        mx4 = at(arena, 65.25, [H4])
        rs4 = at(arena, 65.5, [H4])
        z4 = at(arena, 66, [D])
        zT4 = at(arena, 67, [D])
        w1g = [at(arena, 72 + 6 * i, [F5]) for i in range(2)]
        w3g = [at(arena, 74 + 6 * i, [F5]) for i in range(2)]
        w2g = [at(arena, 76 + 6 * i, [FT5, D]) for i in range(2)]
        sg = [at(arena, 84 + 2 * i, [T]) for i in range(2)]
        hT5 = [at(arena, 88 + 8 * i, [FT5, T]) for i in range(2)]
        f1g = at(arena, 104, [E5])
        cmp5 = at(arena, 106, [B, E5, E5])

        ps = es.enter_context(nc.psum_tensor("ps", [128, 8, 512], F32))

        def bank(i):
            return ps[:, i, :]

        for n in ("ld_x", "ld_patch", "ld_c0", "ld_s0", "ld_a0", "ld_f0", "ld_x3", "ld_a1", "ld_g1"):
            sem(n)
        block = es.enter_context(nc.Block())

        ndma = {}

        def load(eng, name, dst, src):
            ndma[name] = ndma.get(name, 0) + 16
            eng.dma_start(dst, src).then_inc(sem(name), 16)

        def row(ap1):
            return ap1.rearrange("(a n) -> a n", a=1)

        def col(ap1):
            return ap1.rearrange("(n a) -> n a", a=1)

        def rowb(ap1, n=128):
            return ap1.partition_broadcast(n)

        x_v = x.rearrange("b s d -> s b d")
        out_v = out.rearrange("b s d -> s b d")
        ctx_v = ctx_2048.rearrange("b (c p) f -> b p c f", p=128)

        def ctx_tile(i):
            b, h = divmod(i, NCH // 2)
            if b == 0:
                return i + 1
            u = H3 * (b - 1) + h
            before = NCH // 2 + NCH + 4 * max(u - 1, 0) + 2 * u + (i - NCH // 2)
            return before + (2 if u else 0) + 1

        @block.sync
        def _(sp):
            load(sp, "ld_x", xs[0][:], x_v)
            load(sp, "ld_patch", patch_i, patch_lens.rearrange("b (p c) -> p b c", c=NCH))
            load(sp, "ld_c0", c0, ctx_2048[:, 0:128, :].rearrange("b p f -> p b f"))
            load(sp, "ld_s0", w_in, L0_W_in)
            load(sp, "ld_s0", biases[:, 0:1], col(L0_g_res))
            load(sp, "ld_s0", ginit_bc, rowb(L0_g_init[0:D]))
            load(sp, "ld_s0", rows[0:1, 0:D], row(L0_b_in))
            for i, f in enumerate((fmq1, fmq2, fmk1, fmk2)):
                load(sp, "ld_a0", f_nat[0:DK1, i, :], f)
            load(sp, "ld_a0", qo_nat[:, 0, :], q_w)
            load(sp, "ld_a0", qo_nat[:, 1, :], o_w)
            load(sp, "ld_a0", gate_nat[0:E1, :], gate_w)
            load(sp, "ld_a0", k_nat, k_w.rearrange("e k c -> k e c"))
            load(sp, "ld_a0", v_nat, v_w.rearrange("e k c -> k e c"))
            for h in range(H1):
                load(sp, "ld_a0", biases[h * DK1:(h + 1) * DK1, 1:2], col(norm_w))
            load(sp, "ld_f0", kk_nat[0:E2, 0, :], keys)
            load(sp, "ld_f0", kk_nat[0:E2, 1, :], f0_rw)
            load(sp, "ld_f0", rows[0:1, 128:128 + E2], row(f0_rb))
            load(sp, "ld_f0", b1n[0:E2, :], f0_b1)
            load(sp, "ld_f0", b2n[0:E2, :], f0_b2)
            load(sp, "ld_x3", wq_nat, Wq)
            load(sp, "ld_x3", wk_nat, Wkv[:, 0:1024].rearrange("(t c) f -> c t f", c=128))
            load(sp, "ld_x3", wout_sb[:], Wout.rearrange("(t f) d -> f t d", f=128))
            load(sp, "ld_x3", nk_col[0:64, :], col(null_kv[0]))
            load(sp, "ld_x3", nk_col[64:128, :], col(null_kv[0]))
            load(sp, "ld_x3", nv_bc[:], rowb(null_kv[1]))
            load(sp, "ld_x3", lns_bc[:, 0, :], rowb(ln_scale))
            load(sp, "ld_x3", lns_bc[:, 1, :], rowb(ln_bias))
            for i in range(2):
                load(sp, "ld_x3", biases[:, 2 + i:3 + i], col(b_qkv[i * D:(i + 1) * D]))
            for e in range(E2 if STAGES > 2 else 0):
                if e == 0:
                    sp.wait_ge(sem("x_ready"), 1)
                if e >= 2:
                    sp.wait_ge(sem("f0_turned"), e - 1)
                sp.dma_start(w1n[e % 2], f0_w1[e].rearrange("(t f) d -> f t d", f=128)).then_inc(sem(f"w0_{e % 2}"), 16)
                sp.dma_start(w2n[e % 2], f0_w2[e]).then_inc(sem(f"w0_{e % 2}"), 16)
            if STAGES > 3:
                sp.wait_ge(sem("x_ready"), 2)
                load(sp, "ld_wv", wv_nat, Wkv[:, 1024:2048].rearrange("(t c) f -> c t f", c=128))
                for i in range(B * NCH // 2):
                    b, c = divmod(2 * i, NCH)
                    if i >= 2:
                        sp.wait_ge(sem("tile_full"), ctx_tile(i - 2))
                    sp.dma_start(ctx_nat[i % 2][:], ctx_v[b, :, c:c + 2, :]).then_inc(sem(f"ctx_in{i % 2}"), 16)
            if STAGES > 4:
                sp.wait_ge(sem("o3_ready"), B)
                load(sp, "ld_a1", wqkv_sb, w_qkv)
                load(sp, "ld_a1", wproj_sb, w_proj)
                load(sp, "ld_a1", rows4[0:1, 0:D], row(b_qkv[2 * D:3 * D]))
                load(sp, "ld_a1", rows4[0:1, D:2 * D], row(b_proj))
                load(sp, "ld_g1", f1g, f1_gate)
            for e in range(E5 if STAGES > 5 else 0):
                if e >= 2:
                    sp.wait_ge(sem("f1_used"), e - 1)
                k = e % 2
                sp.dma_start(w1g[k], f1_w1[e]).then_inc(sem(f"w5_{k}"), 16)
                sp.dma_start(w3g[k], f1_w3[e]).then_inc(sem(f"w5_{k}"), 16)
                sp.dma_start(w2g[k], f1_w2[e].rearrange("(t f) d -> f t d", f=128)).then_inc(sem(f"w5_{k}"), 16)
            sp.wait_ge(sem("x_ready"), STAGES)
            if STAGES < 6:
                for name, v in ndma.items():
                    sp.wait_ge(sem(name), v)
            sp.dma_start(out_v, xs[STAGES % 3][:]).then_inc(sem("out_done"), 16)
            sp.wait_ge(sem("out_done"), 16)

        @block.gpsimd
        def _(pool):
            n = [0]

            def step(ins):
                n[0] += 1
                ins.then_inc(sem("pool_step"), 1)
                pool.wait_ge(sem("pool_step"), n[0])

            def mask(ap, pattern, base, mult, op, fill):
                step(pool.affine_select(out=ap, in_=ap, compare_op=op, fill=fill, base=base,
                                        pattern=pattern, channel_multiplier=mult))

            step(pool.memset(ident[:], 0.0))
            mask(ident[:], [[-1, 128]], 0, 1, ALU.not_equal, 1.0)
            step(pool.memset(ones[:], 1.0))
            step(pool.memset(lift[:], LIFT))
            step(pool.memset(causal[:], 1.0))
            mask(causal[:], [[1, 128]], 0, -1, ALU.is_ge, 0.0)
            step(pool.memset(strict, 1.0))
            mask(strict, [[1, 128]], 0, -1, ALU.is_gt, 0.0)
            step(pool.memset(reset, 1.0))
            step(pool.memset(reset.rearrange("p (a c) -> p a c", c=NCH)[:, :, 0:1], 0.0))
            step(pool.iota(iotap_i[:, 0:1], pattern=[[0, 1]], base=0, channel_multiplier=1))
            step(pool.iota(iota16_i[:, 0:16], pattern=[[1, 16]], base=0, channel_multiplier=0))
            step(pool.memset(after_b, 1.0))
            mask(after_b, [[-1, 16], [1, S]], 0, -16, ALU.is_ge, 0.0)
            pool.sem_inc(sem("const_a"), 1)
            step(pool.memset(blk16, 1.0))
            mask(blk16, [[-DK1, H1], [0, DK1]], 0, 1, ALU.is_ge, 0.0)
            mask(blk16, [[DK1, H1], [0, DK1]], DK1 - 1, -1, ALU.is_ge, 0.0)
            step(pool.memset(rank_t[:], 0.0))
            mask(rank_t[:], [[1, E2], [-1, E2]], 0, 0, ALU.is_gt, TINY)
            pool.wait_ge(sem("ld_a0"), ndma["ld_a0"])
            step(pool.tensor_copy(f_rep[0:DK1], bc(f_nat[0:DK1, :, :], 2, H1)))
            pool.sem_inc(sem("const_b"), 1)
            if STAGES > 4:
                pool.wait_ge(sem("o3_ready"), B)
                step(pool.memset(m16, 1.0))
                mask(m16, [[-DH4, H4]], 0, 1, ALU.is_ge, 0.0)
                mask(m16, [[DH4, H4]], DH4 - 1, -1, ALU.is_ge, 0.0)
                step(pool.memset(v4, 1.0))
                pool.sem_inc(sem("const_c"), 1)

        @block.tensor
        def _(pe):
            def mm(o, lhsT, rhs, start=True, stop=True, **k):
                return pe.matmul(o, lhsT, rhs, start=start, stop=stop, **k)

            def tr(o, i, n=128):
                return pe.transpose(o, i, ident[0:n, 0:n])

            def turn_y(stage, b_ps):
                pe.wait_ge(sem("y_ready"), stage + 1)
                for b in range(B):
                    last = tr(bank(b_ps)[:, b * S:(b + 1) * S], y[:, b, :])
                last.then_inc(sem("yT_ps"), 1)

            pe.wait_ge(sem("const_a"), 1)
            pe.wait_ge(sem("ld_s0"), ndma["ld_s0"])
            tr(bank(0)[:, 0:D], w_in).then_inc(sem("w_inT_ps"), 1)
            turn_y(0, 3)
            pe.wait_ge(sem("scan_ready"), 1)
            mm(bank(1)[:, 0:12], strict, scan.rearrange("p (a c) -> p a c", c=NCH)[:, :, NCH - 1])\
                .then_inc(sem("prefix_ps"), 1)
            pe.wait_ge(sem("onehot_ready"), 1)
            for b in range(B):
                for c in range(NCH):
                    last = mm(bank(1)[0:8, 64 + 16 * b:80 + 16 * b], hi_oh[:, b * NCH + c, :],
                              lo_oh[:, b * NCH + c, :], start=(c == 0), stop=(c == NCH - 1))
            last.then_inc(sem("count_ps"), 1)
            pe.wait_ge(sem("bnd_ready"), 1)
            for b in range(B):
                for l in range(16):
                    last = mm(bank(2)[:, b * S:(b + 1) * S], bnd[0:8, b, l:l + 1].broadcast_to([8, 128]),
                              after_b[0:8, l, :], start=(l == 0), stop=(l == 15))
            last.then_inc(sem("plug_ps"), 1)
            pe.wait_ge(sem("const_b"), 1)
            pe.wait_ge(sem("ld_a0"), ndma["ld_a0"])
            for i in range(4):
                last = mm(bank(5)[:, i * 128:(i + 1) * 128], f_rep[0:DK1, i, :, :].rearrange("p a b -> p (a b)"),
                          bc(ident[0:DK1, 0:DK1], 1, H1))
            last.then_inc(sem("bd_ps"), 1)
            tr(bank(6)[:, 0:D], qo_nat[:, 1, :])
            tr(bank(6)[:, D:D + E1], gate_nat[0:E1, :], E1).then_inc(sem("og_ps"), 1)
            pe.wait_ge(sem("w0T_ready"), 1)
            pe.wait_ge(sem("r0T_ready"), 1)
            pe.wait_ge(sem("wt0_ready"), 1)
            for b in range(B):
                o = bank(4)[:, b * D:(b + 1) * D]
                mm(o, r0T[:, b * S:(b + 1) * S], w_inT, stop=False)
                mm(o, wt0[:, b, :], u0[:, b, :], start=False, stop=False)
                last = mm(o, ones[0:1, 0:S], rows[0:1, 0:D], start=False)
            last.then_inc(sem("s0_ps"), 1)

            pe.wait_ge(sem("bd_ready"), 1)
            mm(bank(7)[:, 0:256], qo_nat[:, 0, :], bdT[:, 0:2, :].rearrange("p a b -> p (a b)")).then_inc(sem("mq_ps"), 1)
            for e in range(E1):
                if e % 2 == 0 and e >= 4:
                    pe.wait_ge(sem("mk_ready"), e // 2 - 1)
                if e == 2:
                    pe.wait_ge(sem("og_ready"), 1)
                last = mm(bank(5 + (e // 2) % 2)[:, (e % 2) * 256:(e % 2) * 256 + 256],
                          k_nat[:, e, :], bdT[:, 2:4, :].rearrange("p a b -> p (a b)"))
                if e % 2 == 1:
                    last.then_inc(sem("mk_ps"), 1)
            for g in range(2):
                pe.wait_ge(sem("mk_ready"), 3 + g)
                for e in range(4):
                    last = tr(bank(5 + g)[:, e * 128:(e + 1) * 128], v_nat[:, 4 * g + e, :])
                last.then_inc(sem("vw_ps"), 1)
            if STAGES < 2:
                return
            turn_y(1, 3)
            pe.wait_ge(sem("yT_ready"), 1)
            for b in range(B):
                last = mm(bank(0)[:, b * E1:(b + 1) * E1], yT[:, b * S:(b + 1) * S], gateT)
            last.then_inc(sem("logit_ps"), 1)
            pe.wait_ge(sem("mq_ready"), 1)
            mm(bank(1), mqT[:, 0, :], yT)
            mm(bank(2), mqT[:, 1, :], yT).then_inc(sem("qk_ps"), 1)
            pe.wait_ge(sem("mk_ready"), 4)
            for e in range(E1):
                if e == 0:
                    pe.wait_ge(sem("vw_ready"), 2)
                lo = 4 + 2 * (e % 2)
                if e == 1:
                    pass
                if e >= 2:
                    pe.wait_ge(sem("k1_ready"), e)
                mm(bank(lo), mkT[:, e, 0, :], yT)
                mm(bank(lo + 1), mkT[:, e, 1, :], yT).then_inc(sem("qk_ps"), 1)
            pe.wait_ge(sem("k1_ready"), 1)
            for i in range(2 * B):
                b, g = divmod(i, 2)
                if i >= 2:
                    pe.wait_ge(sem("v1_ready"), i - 1)
                mm(bank(1 + i % 2), yT[:, b * S:(b + 1) * S],
                   v_wT[:, 4 * g:4 * g + 4, :].rearrange("p a b -> p (a b)")).then_inc(sem("v1_ps"), 1)
            pe.wait_ge(sem("w_ready"), 1)
            for b in range(B):
                last = tr(bank(0)[0:E1, b * S:(b + 1) * S], wgt[:, b, 0:E1])
            last.then_inc(sem("rT_ps"), 1)
            pe.wait_ge(sem("rT_ready"), 1)
            for e in range(E1):
                if e >= 2:
                    pe.wait_ge(sem("g_ready"), e - 1)
                if e == 1:
                    pe.wait_ge(sem("yT_ready"), 1)
                mm(bank(0 if e % 2 else 3), ident[0:E1, e:e + 1].broadcast_to([E1, 128]), rT_sb[0:E1, :])\
                    .then_inc(sem("g_ps"), 1)
            pe.wait_ge(sem("g_ready"), E1)
            pe.wait_ge(sem("v1_ready"), 2 * B)
            pe.wait_ge(sem("k1_ready"), E1 + 1)
            pe.wait_ge(sem("qbd_ready"), B)

            def scores1(i):
                b, e = divmod(i, E1)
                lo = 2 * (i % 2)
                if i >= 2:
                    pe.wait_ge(sem("am_ready"), i - 1)
                lhsT = kT1[:, e, b * S:(b + 1) * S]
                mm(bank(lo), lhsT, qbd[:, b, 0:4, :].rearrange("p a b -> p (a b)"))
                mm(bank(lo + 1), lhsT, qbd[:, b, 4:8, :].rearrange("p a b -> p (a b)")).then_inc(sem("sc1_ps"), 1)

            def mix1(i):
                b, e = divmod(i, E1)
                pe.wait_ge(sem("am_ready"), i + 1)
                for h in range(H1):
                    o = bank(4)[:, b * D + h * DK1:b * D + (h + 1) * DK1]
                    last = mm(o, am[i % 2][:, h, :], v1[:, b, e, h * DK1:(h + 1) * DK1],
                              start=(i == 0 and h == 0), stop=(e == E1 - 1), skip_group_check=True)
                last.then_inc(sem("o1_ps"), 1)

            scores1(0)
            for i in range(B * E1):
                if i + 1 < B * E1:
                    scores1(i + 1)
                mix1(i)
            pe.wait_ge(sem("z1_ready"), 1)
            for b in range(B):
                last = tr(bank(5)[:, b * S:(b + 1) * S], y[:, b, :])
            last.then_inc(sem("z1T_ps"), 1)
            pe.wait_ge(sem("z1T_ready"), 1)
            for b in range(B):
                last = mm(bank(6)[:, b * D:(b + 1) * D], yT[:, b * S:(b + 1) * S], o_wT)
            last.then_inc(sem("s1_ps"), 1)
            if STAGES < 3:
                return

            pe.wait_ge(sem("ld_f0"), ndma["ld_f0"])
            for t in range(FT2):
                tr(bank(0)[:, 64 + t * E2:64 + (t + 1) * E2], b1n[0:E2, t * 128:(t + 1) * 128], E2)
            pe.wait_ge(sem("kk_ready"), 1)
            for i in range(2):
                last = tr(bank(0)[:, i * E2:(i + 1) * E2], kk_nat[0:E2, i, :], E2)
            last.then_inc(sem("keysT_ps"), 1)
            turn_y(2, 3)
            pe.wait_ge(sem("keysT_ready"), 1)
            pe.wait_ge(sem("yT_ready"), 2)
            for b in range(B):
                o = bank(1)[:, b * E2:(b + 1) * E2]
                mm(o, yT[:, b * S:(b + 1) * S], keysT[:, 1, :], stop=False)
                mm(o, ones[:, 0:S], keysT[:, 0, :], start=False, stop=False)
                last = mm(o, ones[0:1, 0:S], rows[0:1, 128:128 + E2], start=False)
            last.then_inc(sem("logit_ps"), 1)

            def turn_weights0(e):
                pe.wait_ge(sem(f"w0_{e % 2}"), 32 * (e // 2 + 1))
                if e >= 1:
                    pe.wait_ge(sem("w1T_ready"), e)
                    pe.wait_ge(sem("w2T_ready"), e)
                for t in range(FT2):
                    last = tr(bank(4)[:, t * 128:(t + 1) * 128], w1n[e % 2][:, t, :])
                last.then_inc(sem("w1T_ps"), 1)
                for t in range(FT2):
                    last = tr(bank(5)[:, t * 128:(t + 1) * 128], w2n[e % 2][:, t * 128:(t + 1) * 128])
                last.then_inc(sem("f0_turned"), 1)

            turn_weights0(0)
            pe.wait_ge(sem("w_ready"), 2)
            for b in range(B):
                last = tr(bank(0)[0:E2, b * S:(b + 1) * S], wgt[:, b, :])
            last.then_inc(sem("rT_ps"), 1)
            pe.wait_ge(sem("rT_ready"), 2)
            for b in range(B):
                last = mm(bank(2)[:, b * D:(b + 1) * D], rT_sb[0:E2, b * S:(b + 1) * S], b2n[0:E2, :])
            last.then_inc(sem("b2_ps"), 1)

            def down0(e):
                pe.wait_ge(sem("w2T_ready"), e + 1)
                if e >= 2:
                    pe.wait_ge(sem("acc0_ready"), e - 1)
                for b in range(B):
                    for t in range(FT2):
                        if b == 0:
                            pe.wait_ge(sem("gelu_done"), FT2 * e + t + 1)
                        last = mm(bank(6 + e % 2)[:, b * D:(b + 1) * D], hT2[e % 2][:, t, b * S:(b + 1) * S],
                                  w2T[e % 2][:, t, :], start=(t == 0), stop=(t == FT2 - 1))
                last.then_inc(sem("down0_ps"), 1)

            for e in range(E2):
                pe.wait_ge(sem("w1T_ready"), e + 1)
                if e == 0:
                    pe.wait_ge(sem("acc0_start"), 1)
                for t in range(FT2):
                    k = FT2 * e + t
                    if k >= 4:
                        pe.wait_ge(sem("gelu_done"), k - 3)
                    mm(bank(k % 4), w1T[e % 2][:, t * 128:(t + 1) * 128], yT).then_inc(sem("up0_ps"), 1)
                if e + 1 < E2:
                    turn_weights0(e + 1)
                down0(e)
            if STAGES < 4:
                return

            pe.wait_ge(sem("ld_x3"), ndma["ld_x3"])
            pe.wait_ge(sem("acc0_ready"), E2)
            for i in range(2):
                for j in range(4):
                    last = tr(bank(i)[:, j * 128:(j + 1) * 128], wq_nat[:, (4 * i + j) * 128:(4 * i + j + 1) * 128])
                last.then_inc(sem("x3w_ps"), 1)
            for i in range(4):
                if i >= 2:
                    pe.wait_ge(sem("x3w_ready"), i - 1)
                for j in range(4):
                    f, c = divmod(4 * i + j, 2)
                    last = tr(bank((2 + i) % 4)[:, j * 128:(j + 1) * 128], wk_nat[:, c, f * 128:(f + 1) * 128])
                last.then_inc(sem("x3w_ps"), 1)
            pe.wait_ge(sem("x3w_ready"), 6)
            for h in range(H3):
                p = 64 * (h % 2)
                i = h // 2
                if h % 2 == 0 and i >= 2:
                    pe.wait_ge(sem("a3_ready"), i - 1)
                last = mm(bank(4 + 2 * (i % 2) + h % 2)[:, 0:DC], wqT[p:p + 64, h // 2, :],
                          wkT[p:p + 64, h // 2, :])
                if h % 2:
                    last.then_inc(sem("a3_ps"), 1)
            for h in range(H3):
                p = 64 * (h % 2)
                last = mm(bank(h % 2)[:, h:h + 1], wqT[p:p + 64, h // 2, :], nk_col[p:p + 64, :])
            last.then_inc(sem("wn_ps"), 1)

            turn_y(3, 3)
            pe.wait_ge(sem("yT_ready"), 3)
            pe.wait_ge(sem("wn_ready"), 1)
            for b in range(B):
                last = mm(bank(1)[:, b * H3:(b + 1) * H3], yT[:, b * S:(b + 1) * S], wn)
            last.then_inc(sem("sim0_ps"), 1)
            pe.wait_ge(sem("a3_ready"), 8)
            pe.wait_ge(sem("sim0_ready"), 1)
            for i in range(H3 * CT):
                h, c = divmod(i, CT)
                if i >= 4:
                    pe.wait_ge(sem("qk3_ready"), i - 3)
                mm(bank(i % 4), A3[:, h, c * 128:(c + 1) * 128], yT).then_inc(sem("qk3_ps"), 1)

            tiles = [0]
            last_in = {}

            def claim(bk):
                if bk in last_in:
                    pe.wait_ge(sem("tile_lo"), last_in[bk])

            def full(ins, bk):
                tiles[0] += 1
                last_in[bk] = tiles[0]
                ins.then_inc(sem("tile_full"), 1)

            def ctx_turn(i, bk=6):
                pe.wait_ge(sem(f"ctx_in{i % 2}"), 16 * (i // 2 + 1))
                claim(bk)
                for c in range(2):
                    for t in range(CT):
                        last = tr(bank(bk)[:, (t * 2 + c) * 128:(t * 2 + c + 1) * 128],
                                  ctx_nat[i % 2][:, c, t * 128:(t + 1) * 128])
                full(last, bk)
                assert tiles[0] == ctx_tile(i)

            def v_proj(n, bk):
                g, c = divmod(n, NCH)
                b = g // 2
                pe.wait_ge(sem("tile_lo"), ctx_tile(8 * b + c // 2))
                if n == 0:
                    pe.wait_ge(sem("wv_ready"), 1)
                claim(bk)
                k, f = b % 2, (g % 2) * 512
                for t in range(CT):
                    ch, cl = cT_hi[k][:, t, c * 128:(c + 1) * 128], cT_lo[k][:, t, c * 128:(c + 1) * 128]
                    wh, wl = wv_hi[:, t, f:f + 512], wv_lo[:, t, f:f + 512]
                    mm(bank(bk), ch, wh, start=(t == 0), stop=False)
                    mm(bank(bk), ch, wl, start=False, stop=False)
                    last = mm(bank(bk), cl, wh, start=False, stop=(t == CT - 1))
                full(last, bk)

            def scores3(u, j):
                b, h = divmod(u, H3)
                if j == 0:
                    if u >= 1:
                        pe.wait_ge(sem("exp_done"), u)
                    if h == 0:
                        pe.wait_ge(sem("tile_lo"), ctx_tile(8 * b + 7))
                k = b % 2
                for t in range(CT):
                    qh, ql = qk_hi[:, h, t, b * S:(b + 1) * S], qk_lo[:, h, t, b * S:(b + 1) * S]
                    ch, cl = cT_hi[k][:, t, j * 512:(j + 1) * 512], cT_lo[k][:, t, j * 512:(j + 1) * 512]
                    mm(bank(j), qh, ch, start=(t == 0), stop=False)
                    mm(bank(j), qh, cl, start=False, stop=False)
                    last = mm(bank(j), ql, ch, start=False, stop=(t == CT - 1))
                if j >= 1:
                    last.then_inc(sem("s3_ps"), 1)

            def p_turn(u, g):
                bk = 4 + g % 2
                if g == 0:
                    pe.wait_ge(sem("exp_done"), u + 1)
                claim(bk)
                for j in range(4):
                    c = 4 * g + j
                    last = tr(bank(bk)[:, j * 128:(j + 1) * 128], p3[u % 2][:, c * 128:(c + 1) * 128])
                full(last, bk)
                pT_no[g] = tiles[0]

            pT_no = {}

            def pv(u):
                if u >= 1:
                    pe.wait_ge(sem("o_head"), u)
                hh = (u % H3) % 8
                v = v3[(u // 8) % 2]
                for c in range(NCH):
                    if c % 4 == 0:
                        pe.wait_ge(sem("tile_lo"), pT_no[c // 4])
                    mm(bank(7)[:, 0:2 * DH3], pT_hi[:, c, :], v[:, c, hh, :], start=(c == 0), stop=False,
                       skip_group_check=True)
                    last = mm(bank(7)[:, 0:DH3], pT_lo[:, c, :], v[:, c, hh, 0:DH3], start=False,
                              stop=(c == NCH - 1), skip_group_check=True)
                last.then_inc(sem("pv_ps"), 1)

            def heads_turn(b, i):
                if i == 0:
                    pe.wait_ge(sem("o_head"), H3 * (b + 1))
                    claim(4)
                for j in range(4):
                    f = 4 * i + j
                    last = tr(bank(4 + 3 * i)[:, j * 128:(j + 1) * 128], zat[:, f * 128:(f + 1) * 128])
                last.then_inc(sem("oT_ps"), 1)

            def out_proj3(b):
                pe.wait_ge(sem("oT_ready"), 2 * (b + 1))
                for f in range(8):
                    last = mm(bank(7)[:, 0:D], oT3[:, f, :], wout_sb[:, f, :], start=(f == 0), stop=(f == 7))
                last.then_inc(sem("o3_ps"), 1)

            pe.wait_ge(sem("qk3_ready"), H3 * CT)
            for i in range(8):
                ctx_turn(i, 4 + i % 3)
            for n in range(NCH):
                v_proj(n, 4 + n % 3)
            NU = B * H3
            for u in range(NU + 1):
                b, h = divmod(u, H3)
                done = b - 1 if h == 1 and b >= 1 else None
                if done is not None:
                    heads_turn(done, 0)
                if u < NU:
                    scores3(u, 0)
                if done is not None:
                    heads_turn(done, 1)
                    pe.wait_ge(sem("oT_ready"), 2 * done + 1)
                if u >= 1:
                    p_turn(u - 1, 0)
                if u < NU:
                    scores3(u, 1)
                if u >= 1:
                    p_turn(u - 1, 1)
                if done is not None:
                    out_proj3(done)
                if u < NU and b + 1 < B and h < 8:
                    ctx_turn(8 * (b + 1) + h)
                if u < NU:
                    scores3(u, 2)
                if u >= 1:
                    p_turn(u - 1, 2)
                    p_turn(u - 1, 3)
                if u < NU:
                    scores3(u, 3)
                if u >= 1:
                    if done is not None:
                        pe.wait_ge(sem("o3_ready"), done + 1)
                    pv(u - 1)
                n = NCH + 2 * u
                if n < 2 * B * NCH:
                    v_proj(n, 6)
                    v_proj(n + 1, 5)
            heads_turn(B - 1, 0)
            heads_turn(B - 1, 1)
            out_proj3(B - 1)
            if STAGES < 5:
                return

            turn_y(4, 3)
            pe.wait_ge(sem("ld_a1"), ndma["ld_a1"])
            pe.wait_ge(sem("yT_ready"), 4)
            mm(bank(0), wqkv_sb[:, 0:D], yT)
            mm(bank(1), wqkv_sb[:, D:2 * D], yT).then_inc(sem("qk4_ps"), 1)
            for b in range(B):
                o = bank(2)[:, b * D:(b + 1) * D]
                mm(o, yT[:, b * S:(b + 1) * S], wqkv_sb[:, 2 * D:3 * D], stop=False)
                last = mm(o, ones[0:1, 0:S], rows4[0:1, 0:D], start=False)
            last.then_inc(sem("v4_ps"), 1)
            pe.wait_ge(sem("v4_ready"), 1)

            def scores4(b):
                pe.wait_ge(sem("kbd_ready"), b + 1)
                if b >= 1:
                    pe.wait_ge(sem("d4_ready"), b)
                for j in range(4):
                    last = mm(bank(j), qT4[:, b * S:(b + 1) * S], kbd[:, b, 4 * j:4 * j + 4, :].rearrange("p a b -> p (a b)"))
                last.then_inc(sem("s4_ps"), 1)

            def mix4(b):
                pe.wait_ge(sem("p4_ready"), b + 1)
                for g in range(4):
                    n = 4 * b + g
                    if n >= 2:
                        pe.wait_ge(sem("pT4_ready"), n - 1)
                    for j in range(4):
                        last = tr(bank(4 + n % 2)[:, j * 128:(j + 1) * 128], p4[:, 4 * g + j, :])
                    last.then_inc(sem("pT4_ps"), 1)
                pe.wait_ge(sem("pT4_ready"), 4 * b + 4)
                if b >= 1:
                    pe.wait_ge(sem("z4_ready"), b)
                W = DH4 + 1
                for h in range(H4):
                    last = mm(bank(6)[:, h * W:(h + 1) * W], pT4[:, h, :], v4[:, b, h, :])
                last.then_inc(sem("o4_ps"), 1)

            def proj4(b):
                pe.wait_ge(sem("z4_ready"), b + 1)
                if b >= 1:
                    pe.wait_ge(sem("s4_out"), b)
                tr(bank(7)[:, 0:128], z4).then_inc(sem("zT4_ps"), 1)
                pe.wait_ge(sem("zT4_ready"), b + 1)
                o = bank(7)[:, 128:256]
                mm(o, zT4, wproj_sb, stop=False)
                mm(o, ones[0:1, 0:S], rows4[0:1, D:2 * D], start=False).then_inc(sem("s4o_ps"), 1)

            scores4(0)
            for b in range(B):
                if b + 1 < B:
                    scores4(b + 1)
                mix4(b)
                proj4(b)
            if STAGES < 6:
                return

            turn_y(5, 3)
            pe.wait_ge(sem("ld_g1"), ndma["ld_g1"])
            pe.wait_ge(sem("yT_ready"), 5)
            for b in range(B):
                last = mm(bank(0)[:, b * E5:(b + 1) * E5], yT[:, b * S:(b + 1) * S], f1g)
            last.then_inc(sem("logit_ps"), 1)
            pe.wait_ge(sem("l5_ready"), 1)

            def up5(e, t):
                k = FT5 * e + t
                lo = 2 * (k % 3)
                if k >= 3:
                    pe.wait_ge(sem("h5_ready"), k - 2)
                if t == 0:
                    pe.wait_ge(sem(f"w5_{e % 2}"), 48 * (e // 2 + 1))
                mm(bank(lo), w1g[e % 2][:, t * 128:(t + 1) * 128], yT)
                mm(bank(lo + 1), w3g[e % 2][:, t * 128:(t + 1) * 128], yT).then_inc(sem("up5_ps"), 1)

            def down5(e):
                pe.wait_ge(sem("h5_ready"), FT5 * (e + 1))
                if e >= 2:
                    pe.wait_ge(sem("acc5_ready"), e - 1)
                for b in range(B):
                    for t in range(FT5):
                        last = mm(bank(6 + e % 2)[:, b * D:(b + 1) * D], hT5[e % 2][:, t, b * S:(b + 1) * S],
                                  w2g[e % 2][:, t, :], start=(t == 0), stop=(t == FT5 - 1))
                last.then_inc(sem("f1_used"), 1)

            for e in range(E5 + 1):
                for t in range(FT5):
                    if e < E5:
                        up5(e, t)
                    if t == 0 and e >= 1:
                        down5(e - 1)

        @block.vector
        def _(dve):
            n = [0]

            def step(ins):
                n[0] += 1
                ins.then_inc(sem("dve_step"), 1)
                dve.wait_ge(sem("dve_step"), n[0])

            def tt(o, a, b, op):
                return dve.tensor_tensor(o, a, b, op)

            def ts(o, a, s1, op0, s2=None, op1=None):
                if s2 is None:
                    return dve.tensor_scalar(o, a, s1, None, op0)
                return dve.tensor_scalar(o, a, s1, s2, op0, op1)

            def stt(o, a, s, b, op0, op1):
                return dve.scalar_tensor_tensor(out=o, in0=a, scalar=s, in1=b, op0=op0, op1=op1)

            def rsqrt(o, v, t):
                step(dve.tensor_scalar(t.bitcast(I32), v.bitcast(I32), 1, None, ALU.logical_shift_right))
                step(ts(o.bitcast(I32), t.bitcast(I32), -1.0, ALU.mult, MAGIC, ALU.add))
                for _ in range(3):
                    step(stt(t, o, -0.5, o, ALU.mult, ALU.mult))
                    step(tt(t, t, v, ALU.mult))
                    step(stt(o, t, 1.5, o, ALU.add, ALU.mult))

            def moments(src):
                for b in range(B):
                    ins = dve.bn_stats(stats[:, b, :], src[:, b, :])
                step(ins)
                for b in range(B):
                    ins = dve.bn_aggr(mv[:, b, :], stats[:, b, :])
                step(ins)

            mean, var = (lambda b: mv[:, b, 0:1]), mv[:, :, 1]

            def layernorm(stage):
                src = xs[stage % 3]
                moments(src)
                v, r, t = small[:, 0, 0:B], small[:, 1, 0:B], small[:, 2, 0:B]
                step(ts(v, var, LN_EPS, ALU.add))
                rsqrt(r, v, t)
                if stage == 2:
                    q = small[:, 3, 0:B]
                    step(tt(q, r, r, ALU.mult))
                    step(stt(q, q, float(D), var, ALU.mult, ALU.mult))
                for b in range(B):
                    ins = ts(y[:, b, :], src[:, b, :], mean(b), ALU.subtract, r[:, b:b + 1], ALU.mult)
                ins.then_inc(sem("y_ready"), 1)

            def yT_copy(stage):
                dve.wait_ge(sem("yT_ps"), stage + 1)
                dve.tensor_copy(yT, bank(3)).then_inc(sem("yT_ready"), 1)

            def route(stage, k, E, logits, by_prob, cmp_t):
                K = {1: 1, 2: 2, 5: 3}[stage]
                mx, d, ex = route_s[:, 0, 0:B], route_s[:, 1, 0:B * E].rearrange("p (b e) -> p b e", b=B), \
                    route_s[:, 2, 0:B * E].rearrange("p (b e) -> p b e", b=B)
                rank = route_s[:, 3, 0:B * E].rearrange("p (b e) -> p b e", b=B)
                den = route_s[:, 4, 0:B]
                step(dve.tensor_reduce(mx, logits, AX.X, ALU.max))
                tt(d, logits, bc(mx, 2, E), ALU.subtract).then_inc(sem("route_d"), 1)
                dve.wait_ge(sem("route_e"), K)
                by = ex if by_prob else logits
                step(tt(cmp_t, bc(by, 2, E), bc(by, 3, E), ALU.subtract))
                step(tt(cmp_t, cmp_t, bc(rank_t[:, 0:E, 0:E], 1, B), ALU.is_ge))
                step(dve.tensor_reduce(rank, cmp_t, AX.X, ALU.add))
                step(ts(rank, rank, float(k), ALU.is_lt))
                step(tt(ex, ex, rank, ALU.mult))
                step(dve.tensor_reduce(den, ex, AX.X, ALU.add))
                step(dve.reciprocal(den, den))
                tt(wgt[:, :, 0:E], ex, bc(den, 2, E), ALU.mult).then_inc(sem("w_ready"), 1)
                return rank

            dve.wait_ge(sem("ld_x"), 16)
            moments(xs[0])
            v, r, t = small[:, 0, 0:B], small[:, 1, 0:B], small[:, 2, 0:B]
            v2, r2 = small[:, 3, 0:B], small[:, 4, 0:B]
            step(ts(v, var, LN_EPS, ALU.add))
            rsqrt(r, v, t)
            step(tt(v2, var, r, ALU.mult))
            step(tt(v2, v2, r, ALU.mult))
            step(ts(v2, v2, RMS_EPS, ALU.add))
            rsqrt(r2, v2, t)
            step(tt(r2, r2, r, ALU.mult))
            for b in range(B):
                ins = ts(y[:, b, :], xs[0][:, b, :], mean(b), ALU.subtract, r2[:, b:b + 1], ALU.mult)
            ins.then_inc(sem("y_ready"), 1)
            dve.wait_ge(sem("ld_patch"), 16)
            pl = patch_i.rearrange("p b c -> p (b c)")
            ts(parts_i[:, 0, :], pl, 2047, ALU.bitwise_and)
            ts(parts_i[:, 1, :], pl, 11, ALU.logical_shift_right, 2047, ALU.bitwise_and)
            step(ts(parts_i[:, 2, :], pl, 22, ALU.logical_shift_right, 1023, ALU.bitwise_and))
            step(dve.tensor_copy(parts_f, parts_i.rearrange("p a b -> p (a b)")))
            dve.wait_ge(sem("const_a"), 1)
            dve.tensor_tensor_scan(scan, reset, parts_f, 0.0, ALU.mult, ALU.add).then_inc(sem("scan_ready"), 1)
            ts(iotap[:, 1:2], iotap_i[:, 0:1], 1.0, ALU.add)
            dve.tensor_copy(iota8, iota16_i[:, 0:8])
            ts(iota16, iota16_i[:, 0:16], 1.0, ALU.add)
            dve.wait_ge(sem("prefix_ps"), 1)
            dve.wait_ge(sem("scan_ready"), 1)
            step(tt(cum_i.rearrange("p a (b c) -> p (a b) c", c=NCH), scan.rearrange("p (a c) -> p a c", c=NCH),
                    bc(bank(1)[:, 0:12], 2, NCH), ALU.add))
            P = [pint[:, i, :] for i in range(12)]
            step(ts(P[0], cum_i[:, 0, :], 2047.0, ALU.add))
            step(ts(P[1], P[0], 11, ALU.logical_shift_right))
            step(stt(P[2], cum_i[:, 1, :], 2047.0, P[1], ALU.add, ALU.add))
            step(ts(P[3], P[2], 11, ALU.logical_shift_right))
            step(stt(P[4], cum_i[:, 2, :], 1023.0, P[3], ALU.add, ALU.add))
            ts(P[5], P[0], 1920, ALU.bitwise_and)
            ts(P[6], P[2], 2047, ALU.bitwise_and)
            ts(P[7], P[4], 1023, ALU.bitwise_and)
            ts(P[8], P[0], 15, ALU.bitwise_and)
            step(ts(P[9], P[0], 4, ALU.logical_shift_right, 7, ALU.bitwise_and))
            step(tt(pflt[:, 0, :], P[5], P[6], ALU.add))
            step(tt(pflt[:, 0, :], pflt[:, 0, :], P[7], ALU.add))
            step(ts(pflt[:, 1, :], pflt[:, 0, :], 0.0, ALU.is_equal))
            step(stt(pflt[:, 1, :], pflt[:, 0, :], float(1920 + 2047 + 1023), pflt[:, 1, :], ALU.is_equal, ALU.add))
            step(stt(pflt[:, 2, :], P[8], 1.0, pflt[:, 1, :], ALU.add, ALU.mult))
            step(dve.tensor_copy(pflt[:, 3, :], P[9]))
            tt(lo_oh, bc(pflt[:, 2, :], 2, 16), bc(iota16, 1, 64), ALU.is_equal)
            tt(hi_oh, bc(pflt[:, 3, :], 2, 8), bc(iota8, 1, 64), ALU.is_equal).then_inc(sem("onehot_ready"), 1)
            dve.wait_ge(sem("ssq_ready"), 1)
            dve.wait_ge(sem("ld_s0"), ndma["ld_s0"])
            v5, r5 = small[:, 5, 0:B], small[:, 6, 0:B]
            step(ts(v5, small[:, 7, 0:B], 1.0 / DC, ALU.mult, RMS_EPS, ALU.add))
            rsqrt(r5, v5, t)
            step(ts(r5, r5, BCOEF, ALU.mult))
            for b in range(B):
                ins = stt(u0[:, b, :], c0[:, b, 0:D], r5[:, b:b + 1], ginit_bc, ALU.mult, ALU.mult)
            step(ins)
            dve.wait_ge(sem("w_inT_ps"), 1)
            ts(w_inT, bank(0)[:, 0:D], biases[:, 0:1], ALU.mult).then_inc(sem("w0T_ready"), 1)
            dve.wait_ge(sem("yT_ps"), 1)
            dve.tensor_copy(r0T, bank(3)).then_inc(sem("r0T_ready"), 1)
            dve.wait_ge(sem("count_ps"), 1)
            ts(bnd[0:8], bank(1)[0:8, 64:128].rearrange("p (b l) -> p b l", b=B), 1.0, ALU.min)\
                .then_inc(sem("bnd_ready"), 1)
            dve.wait_ge(sem("plug_ps"), 1)
            fl = lambda a: a.rearrange("p b s -> p (b s)")
            step(ts(fl(t0), bank(2), 1.0, ALU.max, iotap[:, 1:2], ALU.subtract))
            ts(fl(e0), fl(t0), 0.0, ALU.max).then_inc(sem("plug_ready"), 1)
            dve.wait_ge(sem("pw_ready"), 1)
            stt(fl(wt0), fl(t0), 0.0, fl(e0), ALU.is_ge, ALU.mult).then_inc(sem("wt0_ready"), 1)
            dve.wait_ge(sem("s0_ps"), 1)
            tt(xs[1][:].rearrange("p b d -> p (b d)"), xs[0][:].rearrange("p b d -> p (b d)"), bank(4), ALU.add)\
                .then_inc(sem("x_ready"), 1)
            dve.wait_ge(sem("bd_ps"), 1)
            dve.wait_ge(sem("const_b"), 1)
            tt(bdT, bank(5).rearrange("p (a b) -> p a b", a=4),
               bc(blk16.rearrange("p a b -> p (a b)"), 1, 4), ALU.mult).then_inc(sem("bd_ready"), 1)
            if STAGES < 2:
                return

            dve.wait_ge(sem("x_ready"), 1)
            layernorm(1)
            yT_copy(1)
            dve.wait_ge(sem("logit_ps"), 1)
            lg = route_s[:, 5, 0:B * E1].rearrange("p (b e) -> p b e", b=B)
            step(dve.tensor_copy(lg, bank(0)[:, 0:B * E1].rearrange("p (b e) -> p b e", b=B)))
            rank1 = route(1, TOPK1, E1, lg, True, cmp[:, :, 0:E1, 0:E1].rearrange("p b e f -> p b e f"))
            dve.wait_ge(sem("qk1_sb"), 1)
            step(tt(q1, q1, bank(2), ALU.mult))
            dve.sem_inc(sem("k1_ready"), 1)
            mask8 = blk16[:, :, 0]
            for b in range(B):
                tt(qbd[:, b, :, :], bc(q1[:, b * S:(b + 1) * S], 1, H1), bc(mask8, 2, S), ALU.mult)\
                    .then_inc(sem("qbd_ready"), 1)
            for e in range(E1):
                dve.wait_ge(sem("qk1_sb"), e + 2)
                tt(kT1[:, e, :], kT1[:, e, :], bank(5 + 2 * (e % 2)), ALU.mult).then_inc(sem("k1_ready"), 1)
            for i in range(2 * B):
                b, g = divmod(i, 2)
                dve.wait_ge(sem("v1_ps"), i + 1)
                tt(v1[:, b, 4 * g:4 * g + 4, :], bank(1 + i % 2).rearrange("p (e d) -> p e d", e=4),
                   bc(rank1[:, b, 4 * g:4 * g + 4], 2, D), ALU.mult).then_inc(sem("v1_ready"), 1)
            dve.wait_ge(sem("rT_ps"), 1)
            dve.tensor_copy(rT_sb[0:E1, :], bank(0)[0:E1, :]).then_inc(sem("rT_ready"), 1)
            for e in range(E1):
                dve.wait_ge(sem("g_ps"), e + 1)
                tt(gmask[:, e, :, :], bank(0 if e % 2 else 3).rearrange("p (b s) -> p b s", b=B),
                   bc(causal[:], 1, B), ALU.mult).then_inc(sem("g_ready"), 1)
            dve.wait_ge(sem("g_ready"), E1)
            for i in range(B * E1):
                b, e = divmod(i, E1)
                lo = 2 * (i % 2)
                dve.wait_ge(sem("sc1_ps"), i + 1)
                if i >= 2:
                    dve.wait_ge(sem("o1_ps"), i - 1)
                tt(am[i % 2], ps[:, lo:lo + 2, :].rearrange("p a (h s) -> p (a h) s", h=4),
                   bc(gmask[:, e, b, :], 1, H1), ALU.mult).then_inc(sem("am_ready"), 1)
            dve.wait_ge(sem("sq1_ready"), 1)
            hs, hr, ht = small[:, 5, 0:B * H1], small[:, 6, 0:B * H1], small[:, 7, 0:B * H1]
            step(dve.tensor_reduce(hs, q1.rearrange("p (h v) -> p h v", v=DK1), AX.X, ALU.add))
            step(ts(hs, hs, 1.0 / DK1, ALU.mult, LN_EPS, ALU.add))
            rsqrt(hr, hs, ht)
            tt(y.rearrange("p b d -> p (b d)").rearrange("p (h v) -> p h v", v=DK1),
               bank(4).rearrange("p (h v) -> p h v", v=DK1), bc(hr, 2, DK1), ALU.mult).then_inc(sem("z1_ready"), 1)
            dve.wait_ge(sem("z1T_ps"), 1)
            dve.tensor_copy(yT, bank(5)).then_inc(sem("z1T_ready"), 1)
            if STAGES > 2:
                dve.wait_ge(sem("ld_f0"), ndma["ld_f0"])
                stt(kk_nat[0:E2, 1, :], kk_nat[0:E2, 0, :], 2.0, kk_nat[0:E2, 1, :], ALU.mult, ALU.add)\
                    .then_inc(sem("kk_ready"), 1)
            dve.wait_ge(sem("s1_ps"), 1)
            tt(xs[2][:].rearrange("p b d -> p (b d)"), xs[1][:].rearrange("p b d -> p (b d)"), bank(6), ALU.add)\
                .then_inc(sem("x_ready"), 1)
            if STAGES < 3:
                return

            dve.wait_ge(sem("x_ready"), 2)
            layernorm(2)
            dve.wait_ge(sem("keysT_ps"), 1)
            step(dve.tensor_copy(keysT, bank(0)[:, 0:2 * E2].rearrange("p (a e) -> p a e", a=2)))
            dve.tensor_copy(b1T, bank(0)[:, 64:64 + FT2 * E2].rearrange("p (a e) -> p a e", a=FT2))
            step(stt(keysT[:, 0, :], keysT[:, 0, :], -1.0, keysT[:, 0, :], ALU.mult, ALU.mult))
            dve.sem_inc(sem("keysT_ready"), 1)
            yT_copy(2)
            dve.wait_ge(sem("logit_ps"), 2)
            lg = route_s[:, 5, 0:B * E2].rearrange("p (b e) -> p b e", b=B)
            step(tt(lg, bank(1)[:, 0:B * E2].rearrange("p (b e) -> p b e", b=B), bc(small[:, 3, 0:B], 2, E2),
                    ALU.subtract))
            route(2, TOPK2, E2, lg, False, cmp)
            dve.wait_ge(sem("rT_ps"), 2)
            dve.tensor_copy(rT_sb[0:E2, :], bank(0)[0:E2, :]).then_inc(sem("rT_ready"), 1)
            dve.wait_ge(sem("b2_ps"), 1)
            acc = xs[0]
            tt(acc[:].rearrange("p b d -> p (b d)"), xs[2][:].rearrange("p b d -> p (b d)"), bank(2), ALU.add)\
                .then_inc(sem("acc0_start"), 1)

            def w2T_copy(e):
                dve.wait_ge(sem("f0_turned"), e + 1)
                if e >= 2:
                    dve.wait_ge(sem("down0_ps"), e - 1)
                dve.tensor_copy(w2T[e % 2].rearrange("p a b -> p (a b)"), bank(5)).then_inc(sem("w2T_ready"), 1)

            def gather_expert(acc, w, bk):
                for b in range(B):
                    ins = stt(acc[:, b, :], bank(bk)[:, b * D:(b + 1) * D], w[:, b, :], acc[:, b, :],
                              ALU.mult, ALU.add)
                return ins

            w2T_copy(0)
            dve.wait_ge(sem("acc0_start"), 1)
            for e in range(E2):
                if e + 1 < E2:
                    w2T_copy(e + 1)
                dve.wait_ge(sem("down0_ps"), e + 1)
                if e >= 1:
                    dve.wait_ge(sem("acc0_ready"), e)
                gather_expert(acc, wgt[:, :, e:e + 1], 6 + e % 2).then_inc(sem("acc0_ready"), 1)
            dve.wait_ge(sem("acc0_ready"), E2)
            dve.sem_inc(sem("x_ready"), 1)
            if STAGES < 4:
                return

            layernorm(3)
            for i in range(2):
                dve.wait_ge(sem("x3w_ps"), i + 1)
                dve.tensor_copy(wqT[:, 4 * i:4 * i + 4, :].rearrange("p a b -> p (a b)"), bank(i))\
                    .then_inc(sem("x3w_ready"), 1)
            for i in range(4):
                dve.wait_ge(sem("x3w_ps"), i + 3)
                dve.tensor_copy(wkT[:, 2 * i:2 * i + 2, :].rearrange("p a b -> p (a b)"), bank((2 + i) % 4))\
                    .then_inc(sem("x3w_ready"), 1)
            dve.wait_ge(sem("wn_ps"), 1)
            ts(wn[:, 0:H3:2], bank(0)[:, 0:H3:2], DH3 ** -0.5, ALU.mult)
            ts(wn[:, 1:H3:2], bank(1)[:, 1:H3:2], DH3 ** -0.5, ALU.mult).then_inc(sem("wn_ready"), 1)
            yT_copy(3)
            dve.wait_ge(sem("sim0_ps"), 1)
            s0v = bank(1)[:, 0:B * H3].rearrange("p (b h) -> p b h", b=B)
            dve.tensor_copy(sim0[:], s0v)
            ts(nsim0[:], s0v, -1.0, ALU.mult).then_inc(sem("sim0_ready"), 1)
            dve.wait_ge(sem("wvh_ready"), 1)
            tt(wv_lo[:], wv_nat, wv_hi[:], ALU.subtract).then_inc(sem("wv_ready"), 1)
            for i in range(H3 * CT):
                h, c = divmod(i, CT)
                dve.wait_ge(sem("qk3_hi"), i + 1)
                tt(qk_lo[:, h, c, :], bank(i % 4), qk_hi[:, h, c, :], ALU.subtract).then_inc(sem("qk3_ready"), 1)

            tiles = [0]

            def split_lo(dst, bk, hi):
                tiles[0] += 1
                dve.wait_ge(sem("tile_hi"), tiles[0])
                tt(dst, bk, hi, ALU.subtract).then_inc(sem("tile_lo"), 1)

            def ctx_lo(i, bk=6):
                b, c = divmod(2 * i, NCH)
                o = (slice(None), slice(None), slice(c * 128, (c + 2) * 128))
                split_lo(cT_lo[b % 2][o], bank(bk).rearrange("p (t s) -> p t s", t=CT), cT_hi[b % 2][o])

            def v_lo(n, bk):
                g, c = divmod(n, NCH)
                v = v3[g % 2][:, c, :, :]
                split_lo(v[:, :, DH3:2 * DH3], bank(bk).rearrange("p (h d) -> p h d", h=8), v[:, :, 0:DH3])

            def pT_lo_(g):
                split_lo(pT_lo[:, 4 * g:4 * g + 4, :].rearrange("p a b -> p (a b)"), bank(4 + g % 2),
                         pT_hi[:, 4 * g:4 * g + 4, :].rearrange("p a b -> p (a b)"))

            us = lambda u, i: unit_s[:, u % 2, i:i + 1]

            def max_a(u):
                b, h = divmod(u, H3)
                dve.wait_ge(sem("s3_ps"), 3 * u + 1)
                step(dve.tensor_reduce(us(u, 0), ps[:, 0:2, :], AX.XY, ALU.max, negate=True))
                step(tt(us(u, 0), us(u, 0), nsim0[:, b, h:h + 1], ALU.min))

            def max_b(u):
                dve.wait_ge(sem("s3_ps"), 3 * u + 2)
                step(dve.tensor_reduce(us(u, 1), bank(2), AX.X, ALU.max, negate=True))
                step(tt(us(u, 0), us(u, 0), us(u, 1), ALU.min))

            def max_c(u):
                dve.wait_ge(sem("s3_ps"), 3 * u + 3)
                step(dve.tensor_reduce(us(u, 1), bank(3), AX.X, ALU.max, negate=True))
                stt(us(u, 2), us(u, 1), us(u, 0), lift[:], ALU.min, ALU.add).then_inc(sem("nmax_ready"), 1)

            def head_out(u):
                b, h = divmod(u, H3)
                dve.wait_ge(sem("p0_ready"), u + 1)
                step(tt(us(u, 5), us(u, 3), us(u, 4), ALU.add))
                step(dve.reciprocal(us(u, 5), us(u, 5)))
                dve.wait_ge(sem("pv_ps"), u + 1)
                if h == 0 and b >= 1:
                    dve.wait_ge(sem("oT_ps"), 2 * b)
                z = zat[:, h * DH3:(h + 1) * DH3]
                step(stt(z, nv_bc[:], us(u, 4), bank(7)[:, 0:DH3], ALU.mult, ALU.add))
                step(tt(z, z, bank(7)[:, DH3:2 * DH3], ALU.add))
                ts(z, z, us(u, 5), ALU.mult).then_inc(sem("o_head"), 1)

            def out3(b):
                dve.wait_ge(sem("o3_ps"), b + 1)
                dve.tensor_copy(xs[1][:, b, :], bank(7)[:, 0:D]).then_inc(sem("o3_ready"), 1)

            for i in range(8):
                ctx_lo(i, 4 + i % 3)
            for m in range(NCH):
                v_lo(m, 4 + m % 3)
            NU = B * H3
            for u in range(NU + 1):
                b, h = divmod(u, H3)
                if u >= 1:
                    pT_lo_(0)
                    pT_lo_(1)
                if u < NU:
                    max_a(u)
                if h == 1 and b >= 1:
                    out3(b - 1)
                if u < NU and b + 1 < B and h < 8:
                    ctx_lo(8 * (b + 1) + h)
                if u < NU:
                    max_b(u)
                if u >= 1:
                    pT_lo_(2)
                    pT_lo_(3)
                if u < NU:
                    max_c(u)
                if u >= 1:
                    head_out(u - 1)
                n_v = NCH + 2 * u
                if n_v < 2 * B * NCH:
                    v_lo(n_v, 6)
                    v_lo(n_v + 1, 5)
            out3(B - 1)
            dve.wait_ge(sem("o3_ready"), B)
            o3 = xs[1]
            moments(o3)
            step(ts(v, var, XLN_EPS, ALU.add))
            rsqrt(r, v, t)
            for b in range(B):
                ins = ts(o3[:, b, :], o3[:, b, :], mean(b), ALU.subtract, r[:, b:b + 1], ALU.mult)
            step(ins)
            step(tt(o3[:], o3[:], bc(lns_bc[:, 0, :], 1, B), ALU.mult))
            step(tt(o3[:], o3[:], bc(lns_bc[:, 1, :], 1, B), ALU.add))
            tt(o3[:], o3[:], xs[0][:], ALU.add).then_inc(sem("x_ready"), 1)
            if STAGES < 5:
                return

            dve.wait_ge(sem("x_ready"), 4)
            layernorm(4)
            yT_copy(4)
            dve.wait_ge(sem("qk4_ps"), 1)
            dve.wait_ge(sem("ld_a1"), ndma["ld_a1"])
            dve.wait_ge(sem("const_c"), 1)
            ts(qT4, bank(0), biases[:, 2:3], ALU.add, DH4 ** -0.5, ALU.mult)
            step(ts(kT4, bank(1), biases[:, 3:4], ALU.add))
            for b in range(B):
                tt(kbd[:, b, :, :], bc(kT4[:, b * S:(b + 1) * S], 1, H4), bc(m16, 2, S), ALU.mult)\
                    .then_inc(sem("kbd_ready"), 1)
                if b == 0:
                    dve.wait_ge(sem("v4_ps"), 1)
                    dve.tensor_copy(v4[:, :, :, 0:DH4],
                                    bank(2).rearrange("p (b h v) -> p b h v", b=B, h=H4)).then_inc(sem("v4_ready"), 1)

            def out4(b):
                dve.wait_ge(sem("s4o_ps"), b + 1)
                tt(xs[2][:, b, :], bank(7)[:, 128:256], xs[1][:, b, :], ALU.add).then_inc(sem("s4_out"), 1)

            def soft4(b):
                dve.wait_ge(sem("s4_ps"), b + 1)
                sv = ps[:, 0:4, :].rearrange("p a (h s) -> p (a h) s", h=4)
                step(dve.tensor_reduce(mx4, sv, AX.X, ALU.max))
                if b >= 1:
                    dve.wait_ge(sem("p4_ready"), b)
                tt(d4, sv, bc(mx4, 2, S), ALU.subtract).then_inc(sem("d4_ready"), 1)

            soft4(0)
            for b in range(B):
                if b + 1 < B:
                    soft4(b + 1)
                for g in (0, 2):
                    m = 4 * b + g
                    dve.wait_ge(sem("pT4_ps"), m + 1)
                    if b >= 1 and g == 0:
                        dve.wait_ge(sem("o4_ps"), b)
                    if m:
                        dve.wait_ge(sem("pT4_ready"), m)
                    dve.tensor_copy(pT4[:, 4 * g:4 * g + 4, :].rearrange("p a b -> p (a b)"), bank(4 + m % 2))\
                        .then_inc(sem("pT4_ready"), 1)
                dve.wait_ge(sem("o4_ps"), b + 1)
                o4 = bank(6)[:, 0:H4 * (DH4 + 1)].rearrange("p (h v) -> p h v", h=H4)
                step(dve.reciprocal(rs4, o4[:, :, DH4]))
                if b >= 1:
                    dve.wait_ge(sem("zT4_ps"), b)
                tt(z4.rearrange("p (h v) -> p h v", h=H4), o4[:, :, 0:DH4], bc(rs4, 2, DH4), ALU.mult)\
                    .then_inc(sem("z4_ready"), 1)
                dve.wait_ge(sem("zT4_ps"), b + 1)
                dve.tensor_copy(zT4, bank(7)[:, 0:128]).then_inc(sem("zT4_ready"), 1)
                out4(b)
            dve.wait_ge(sem("s4_out"), B)
            dve.sem_inc(sem("x_ready"), 1)
            if STAGES < 6:
                return

            layernorm(5)
            yT_copy(5)
            dve.wait_ge(sem("logit_ps"), 3)
            lg = route_s[:, 5, 0:B * E5].rearrange("p (b e) -> p b e", b=B)
            step(dve.tensor_copy(lg, bank(0)[:, 0:B * E5].rearrange("p (b e) -> p b e", b=B)))
            dve.sem_inc(sem("l5_ready"), 1)
            route(5, TOPK5, E5, lg, True, cmp5)
            acc = xs[0]
            step(dve.tensor_copy(acc[:], xs[2][:]))
            for e in range(E5 + 1):
                for t_ in range(FT5):
                    k = FT5 * e + t_
                    if e < E5:
                        dve.wait_ge(sem("silu_done"), k + 1)
                        if t_ == 0 and e >= 2:
                            dve.wait_ge(sem("f1_used"), e - 1)
                        tt(hT5[e % 2][:, t_, :], sg[k % 2], bank(2 * (k % 3) + 1), ALU.mult).then_inc(sem("h5_ready"), 1)
                    if e >= 1 and t_ == 1:
                        dve.wait_ge(sem("f1_used"), e)
                        if e >= 2:
                            dve.wait_ge(sem("acc5_ready"), e - 1)
                        if e == 1:
                            dve.wait_ge(sem("w_ready"), 3)
                        gather_expert(acc, wgt[:, :, e - 1:e], 6 + (e - 1) % 2).then_inc(sem("acc5_ready"), 1)
            dve.wait_ge(sem("acc5_ready"), E5)
            dve.sem_inc(sem("x_ready"), 1)

        @block.scalar
        def _(act):
            def copy(o, i, scale=1.0):
                return act.activation(o, i, ACT.Copy, scale=scale)

            act.wait_ge(sem("ld_c0"), 16)
            for b in range(B):
                if b:
                    act.wait_ge(sem("ssq_b"), b)
                ins = act.activation(sq_junk, c0[:, b, :], ACT.Square, accum_out=small[:, 7, b:b + 1])
                ins.then_inc(sem("ssq_b") if b < B - 1 else sem("ssq_ready"), 1)
            act.wait_ge(sem("plug_ready"), 1)
            e0f = e0.rearrange("p b s -> p (b s)")
            act.activation(e0f, e0f, ACT.Exp, scale=-DT).then_inc(sem("pw_ready"), 1)
            act.wait_ge(sem("og_ps"), 1)
            act.activation(o_wT, bank(6)[:, 0:D], ACT.Copy, scale=biases[:, 1:2])
            copy(gateT, bank(6)[:, D:D + E1]).then_inc(sem("og_ready"), 1)
            act.wait_ge(sem("mq_ps"), 1)
            act.activation(mqT[:, 0, :], bank(7)[:, 0:D], ACT.Copy, scale=DK1 ** -0.5)
            copy(mqT[:, 1, :], bank(7)[:, D:2 * D]).then_inc(sem("mq_ready"), 1)
            for i in range(4):
                act.wait_ge(sem("mk_ps"), i + 1)
                copy(mkT[:, 2 * i:2 * i + 2, :, :].rearrange("p a b c -> p (a b c)"), bank(5 + i % 2))\
                    .then_inc(sem("mk_ready"), 1)
            for g in range(2):
                act.wait_ge(sem("vw_ps"), g + 1)
                copy(v_wT[:, 4 * g:4 * g + 4, :].rearrange("p a b -> p (a b)"), bank(5 + g)).then_inc(sem("vw_ready"), 1)
            if STAGES < 2:
                return

            def route_exp(k, E):
                act.wait_ge(sem("route_d"), k)
                act.activation(route_s[:, 2, 0:B * E], route_s[:, 1, 0:B * E], ACT.Exp).then_inc(sem("route_e"), 1)

            route_exp(1, E1)
            act.wait_ge(sem("qk_ps"), 1)
            copy(q1, bank(1)).then_inc(sem("qk1_sb"), 1)
            for e in range(E1):
                act.wait_ge(sem("qk_ps"), e + 2)
                copy(kT1[:, e, :], bank(4 + 2 * (e % 2))).then_inc(sem("qk1_sb"), 1)
            act.wait_ge(sem("o1_ps"), B * E1)
            act.activation(q1, bank(4), ACT.Square).then_inc(sem("sq1_ready"), 1)
            if STAGES < 3:
                return

            route_exp(2, E2)

            def w1T_copy(e):
                act.wait_ge(sem("w1T_ps"), e + 1)
                copy(w1T[e % 2], bank(4)).then_inc(sem("w1T_ready"), 1)

            w1T_copy(0)
            for e in range(E2):
                for t in range(FT2):
                    k = FT2 * e + t
                    act.wait_ge(sem("up0_ps"), k + 1)
                    if t == 0 and e >= 2:
                        act.wait_ge(sem("down0_ps"), e - 1)
                    act.activation(hT2[e % 2][:, t, :], bank(k % 4), ACT.Gelu, bias=b1T[:, t, e:e + 1])\
                        .then_inc(sem("gelu_done"), 1)
                if e + 1 < E2:
                    w1T_copy(e + 1)
            if STAGES < 4:
                return

            for i in range(8):
                act.wait_ge(sem("a3_ps"), i + 1)
                copy(A3[:, 2 * i:2 * i + 2, :], ps[:, 4 + 2 * (i % 2):6 + 2 * (i % 2), 0:DC], DH3 ** -0.5)\
                    .then_inc(sem("a3_ready"), 1)
            act.wait_ge(sem("ld_wv"), 16)
            copy(wv_hi[:], wv_nat).then_inc(sem("wvh_ready"), 1)
            for i in range(H3 * CT):
                h, c = divmod(i, CT)
                act.wait_ge(sem("qk3_ps"), i + 1)
                copy(qk_hi[:, h, c, :], bank(i % 4)).then_inc(sem("qk3_hi"), 1)

            tiles = [0]

            def split_hi(dst, bk):
                tiles[0] += 1
                act.wait_ge(sem("tile_full"), tiles[0])
                copy(dst, bk).then_inc(sem("tile_hi"), 1)

            def ctx_hi(i, bk=6):
                b, c = divmod(2 * i, NCH)
                split_hi(cT_hi[b % 2][:, :, c * 128:(c + 2) * 128], bank(bk).rearrange("p (t s) -> p t s", t=CT))

            def v_hi(n, bk):
                g, c = divmod(n, NCH)
                split_hi(v3[g % 2][:, c, :, 0:DH3], bank(bk).rearrange("p (h d) -> p h d", h=8))

            def pT_hi_(g):
                split_hi(pT_hi[:, 4 * g:4 * g + 4, :].rearrange("p a b -> p (a b)"), bank(4 + g % 2))

            us = lambda u, i: unit_s[:, u % 2, i:i + 1]

            def exps(u):
                b, h = divmod(u, H3)
                act.wait_ge(sem("nmax_ready"), u + 1)
                act.activation(p3[u % 2], ps[:, 0:4, :].rearrange("p a b -> p (a b)"), ACT.Exp, bias=us(u, 2),
                               accum_out=us(u, 3)).then_inc(sem("exp_done"), 1)
                act.activation(us(u, 4), sim0[:, b, h:h + 1], ACT.Exp, bias=us(u, 2)).then_inc(sem("p0_ready"), 1)

            def heads_copy(b, i):
                act.wait_ge(sem("oT_ps"), 2 * b + i + 1)
                copy(oT3[:, 4 * i:4 * i + 4, :].rearrange("p a b -> p (a b)"), bank(4 + 3 * i))\
                    .then_inc(sem("oT_ready"), 1)

            for i in range(8):
                ctx_hi(i, 4 + i % 3)
            for m in range(NCH):
                v_hi(m, 4 + m % 3)
            NU = B * H3
            for u in range(NU + 1):
                b, h = divmod(u, H3)
                if h == 1 and b >= 1:
                    heads_copy(b - 1, 0)
                    heads_copy(b - 1, 1)
                if u >= 1:
                    pT_hi_(0)
                    pT_hi_(1)
                if u < NU and b + 1 < B and h < 8:
                    ctx_hi(8 * (b + 1) + h)
                if u >= 1:
                    pT_hi_(2)
                    pT_hi_(3)
                if u < NU:
                    exps(u)
                n_v = NCH + 2 * u
                if n_v < 2 * B * NCH:
                    v_hi(n_v, 6)
                    v_hi(n_v + 1, 5)
            for i in range(2):
                heads_copy(B - 1, i)
            if STAGES < 5:
                return

            for b in range(B):
                act.wait_ge(sem("d4_ready"), b + 1)
                if b >= 1:
                    act.wait_ge(sem("pT4_ps"), 4 * b)
                act.activation(p4, d4, ACT.Exp).then_inc(sem("p4_ready"), 1)
                for g in (1, 3):
                    m = 4 * b + g
                    act.wait_ge(sem("pT4_ps"), m + 1)
                    act.wait_ge(sem("pT4_ready"), m)
                    copy(pT4[:, 4 * g:4 * g + 4, :].rearrange("p a b -> p (a b)"), bank(4 + m % 2))\
                        .then_inc(sem("pT4_ready"), 1)
            if STAGES < 6:
                return

            route_exp(3, E5)
            for k in range(E5 * FT5):
                act.wait_ge(sem("up5_ps"), k + 1)
                if k >= 2:
                    act.wait_ge(sem("h5_ready"), k - 1)
                act.activation(sg[k % 2], bank(2 * (k % 3)), ACT.Silu).then_inc(sem("silu_done"), 1)


_INS = ['x', 'ctx_2048', 'mask_BxS2_if0', 'L0_xattn_W_in', 'L0_xattn_b_in', 'L0_xattn_g_res', 'L0_xattn_g_init',
        'L0_attn_gate_w', 'L0_attn_q_w', 'L0_attn_k_w', 'L0_attn_v_w', 'L0_attn_fmq1_w', 'L0_attn_fmq2_w',
        'L0_attn_fmk1_w', 'L0_attn_fmk2_w', 'L0_attn_norm_w', 'L0_attn_o_w',
        'L0_ffn_keys', 'L0_ffn_w1', 'L0_ffn_b1', 'L0_ffn_w2', 'L0_ffn_b2', 'L0_ffn_rw', 'L0_ffn_rb',
        'L1_xattn_Wq', 'L1_xattn_Wkv', 'L1_xattn_null_kv', 'L1_xattn_Wout', 'L1_xattn_ln_scale', 'L1_xattn_ln_bias',
        'L1_attn_w_qkv', 'L1_attn_b_qkv', 'L1_attn_w_proj', 'L1_attn_b_proj',
        'L1_ffn_gate_w', 'L1_ffn_w1', 'L1_ffn_w3', 'L1_ffn_w2']
_OUTS = [((4, 128, 128), 'float32')]


def kernel(**inputs):
    import numpy as _np
    import concourse.bacc as _bacc
    from concourse import mybir as _mybir
    from concourse.bass_utils import run_bass_kernel_spmd as _run

    nc = _bacc.Bacc("TRN2", target_bir_lowering=False, num_devices=1, dynamic_dma_scratch_size=1024)
    arrays, args = {}, []
    for name in _INS:
        a = _np.ascontiguousarray(inputs[name])
        arrays[f"in_{name}_dram"] = a
        args.append(nc.dram_tensor(f"in_{name}_dram", a.shape, _mybir.dt.from_np(a.dtype), kind="ExternalInput").ap())
    for i, (shape, dtype) in enumerate(_OUTS):
        dt = _mybir.dt.from_np(_np.dtype(dtype))
        args.append(nc.dram_tensor(f"out_{i}_dram", shape, dt, kind="ExternalOutput").ap())
    perceiver_kernel(nc, *args)
    r = _run(nc, [arrays], core_ids=[0])
    return r.results[0]["out_0_dram"]
```

```python
import concourse.bass as bass
from concourse import mybir
from concourse.alu_op_type import AluOpType as ALU
from contextlib import ExitStack
import numpy as np



def perceiver_kernel(nc, x, ctx_2048, patch_lens, L0_W_in, L0_b_in, L0_g_res, L0_g_init,
                     gate_w, q_w, k_w, v_w, fmq1, fmq2, fmk1, fmk2, norm_w, o_w,
                     keys, f0_w1, f0_b1, f0_w2, f0_b2, f0_rw, f0_rb,
                     Wq, Wkv, null_kv, Wout, ln_scale, ln_bias,
                     w_qkv, b_qkv, w_proj, b_proj, f1_gate, f1_w1, f1_w3, f1_w2, out):
    F32, F16, BF16, I32 = mybir.dt.float32, mybir.dt.float16, mybir.dt.bfloat16, mybir.dt.int32
    ACT = mybir.ActivationFunctionType
    AX = mybir.AxisListType

    B, S, D = x.shape
    NK, DC = ctx_2048.shape[1:]
    T = B * S
    NCH = NK // S
    CT = DC // 128
    E1, H1 = gate_w.shape[0], 8
    DK1 = D // H1
    HP1 = 5
    E2, F2 = f0_w1.shape[0], f0_w1.shape[1]
    FT2 = F2 // 128
    H3 = Wq.shape[1] // 64
    DH3 = 64
    H4 = 16
    DH4 = D // H4
    E5, F5 = f1_w1.shape[0], f1_w1.shape[2]
    FT5 = F5 // 128
    TOPK1, TOPK2, TOPK5 = 2, 4, 2
    LN_EPS, RMS_EPS, XLN_EPS = 1e-5, 1e-5, 1e-6
    LOGP = np.float32(-0.001)
    DT = float(-np.log(-np.expm1(LOGP)))
    BCOEF = float(np.exp(LOGP))
    MAGIC = float(0x5F3759DF)
    TINY = 1.1754944e-38
    LIFT = float(12 * np.log(2.0))

    es = ExitStack()
    with es:
        def sb(name, shape, dt=F32):
            return es.enter_context(nc.sbuf_tensor(name, shape, dt))

        names = {}

        def sem(name):
            if name not in names:
                names[name] = es.enter_context(nc.semaphore(name))
            return names[name]

        def bc(ap, axis, n):
            u = ap.unsqueeze(axis)
            shape = list(u.shape)
            shape[axis] = n
            return u.broadcast_to(shape)

        KB = 256
        arena = sb("arena", [128, 160 * KB])
        main = sb("main", [128, 24 * KB])

        def at(base, kb, shape, dt=F32):
            words = int(np.prod(shape)) * (2 if dt in (F16, BF16) else 4) // 4
            o = int(kb * KB)
            v = base[:, o:o + words]
            if dt is not F32:
                v = v.bitcast(dt)
            if len(shape) == 2:
                v = v.rearrange("p (a b) -> p a b", a=shape[0])
            elif len(shape) == 3:
                v = v.rearrange("p (a b c) -> p a b c", a=shape[0], b=shape[1])
            elif len(shape) == 4:
                v = v.rearrange("p (a b c d) -> p a b c d", a=shape[0], b=shape[1], c=shape[2])
            return v

        xs = [sb(f"x{i}", [128, B, D]) for i in range(3)]
        yy = sb("yy", [128, 2 * T])
        y = yy[:, 0:T].rearrange("p (b d) -> p b d", b=B)
        yT = yy[:, T:2 * T]
        zat = sb("zat", [128, H3 * DH3])
        ident = sb("ident", [128, 128])
        causal = sb("causal", [128, 128])
        ones = sb("ones", [128, 128])
        stats = sb("stats", [128, B, 6])
        mv = sb("mv", [128, B, 2])
        small = sb("small", [128, 9, 32])
        route_s = sb("route_s", [128, 6, 64])
        wgt = sb("wgt", [128, B, E2])
        ctx_nat = [sb(f"ctx_nat{i}", [128, 2, DC]) for i in range(2)]
        wv_hi = sb("wv_hi", [128, CT, 1024], F16)
        wv_lo = sb("wv_lo", [128, CT, 1024], F16)
        wout_sb = sb("wout_sb", [128, 8, D])
        nk_bc = sb("nk_bc", [128, DH3])
        nv_bc = sb("nv_bc", [128, DH3])
        lns_bc = sb("lns_bc", [128, 2, D])
        sim0 = sb("sim0", [128, B, H3])
        nsim0 = sb("nsim0", [128, B, H3])
        unit_s = sb("unit_s", [128, 2, 8])
        sums3 = sb("sums3", [128, 2, H3])
        p03 = sb("p03", [128, 2, H3])
        lift = sb("lift", [128, 1])
        biases = sb("biases", [128, 8])
        rows = at(arena, 148, [512])
        rows4 = at(arena, 151, [256])

        c0 = at(arena, 96, [B, DC])
        u0 = at(arena, 100, [B, D])
        wt0 = at(arena, 102, [B, S])
        t0 = at(arena, 104, [B, S])
        e0 = at(arena, 106, [B, S])
        patch_i = at(arena, 108, [B, NCH], I32)
        parts_i = at(arena, 108.25, [3, B * NCH], I32)
        parts_f = at(arena, 109, [3 * B * NCH])
        reset = at(arena, 109.75, [3 * B * NCH])
        scan = at(arena, 110.5, [3 * B * NCH])
        cum_i = at(arena, 111.25, [3, B * NCH], I32)
        pint = at(arena, 112, [12, 64], I32)
        pflt = at(arena, 115, [4, 64])
        lo_oh = at(arena, 116, [64, 16], BF16)
        hi_oh = at(arena, 118, [64, 8], BF16)
        iota16 = at(arena, 119, [16])
        iota8 = at(arena, 119.0625, [8])
        iotap = at(arena, 119.125, [2])
        iotap_i = at(arena, 119.25, [2], I32)
        iota16_i = at(arena, 119.5, [24], I32)
        bnd = at(arena, 120, [B, 16], BF16)
        after_b = at(arena, 152, [16, S], BF16)
        strict = at(arena, 121, [128])
        w_in = at(arena, 121.5, [D])
        w_inT = at(arena, 122, [D])
        ginit_bc = at(arena, 122.5, [D])
        r0T = at(arena, 123, [T])
        sq_junk = at(arena, 151, [DC])

        k_nat = at(arena, 136, [E1, D])
        v_nat = at(arena, 140, [E1, D])
        qo_nat = at(arena, 80, [2, D])
        gate_nat = at(arena, 81, [D])
        keysT = at(arena, 150, [2, E2])
        gateT = at(arena, 92.25, [E1])
        f_nat = at(arena, 82, [4, DK1])
        bdT = at(arena, 82.5, [4, 128])
        blk16 = at(arena, 84.5, [H1, DK1])
        o_wT = at(arena, 85, [D])
        mqT = at(arena, 86, [2, D])
        mkT = at(arena, 0, [E1, 2, D])
        v_wT = at(arena, 8, [E1, D])
        kT1_hi, kT1_lo = at(arena, 12, [E1, T], F16), at(arena, 20, [E1, T], F16)
        qbd_hi, qbd_lo = at(arena, 28, [B, H1, S], F16), at(arena, 36, [B, H1, S], F16)
        v1 = at(arena, 44, [B, E1, H1, 2 * DK1], F16)
        k32 = [at(arena, 116 + 2 * i, [T]) for i in range(2)]
        q1_hi, q1_lo = at(arena, 124, [T], F16), at(arena, 125, [T], F16)
        gmask = at(arena, 60, [E1, B, S])
        am = [at(arena, 76, [H1, S]), at(arena, 87, [H1, S]), at(arena, 120, [H1, S])]
        o1 = at(arena, 126, [T])
        am_hi = [at(arena, 104 + 2 * i, [H1, S], F16) for i in range(4)]
        am_lo = [at(arena, 112 + 2 * i, [H1, S], F16) for i in range(4)]
        q1 = at(arena, 93, [T])
        f_rep = at(arena, 93, [4, H1, DK1])
        rT_sb = at(arena, 146, [T])
        rank_t = sb("rank_t", [128, E2, E2])

        w1n = [at(arena, 96 + 4 * i, [FT2, D]) for i in range(2)]
        w2n = [at(arena, 98 + 4 * i, [F2]) for i in range(2)]
        w1T_hi, w1T_lo = ([at(arena, 104 + 2 * i + j, [F2], F16) for i in range(2)] for j in range(2))
        w2T_hi, w2T_lo = ([at(arena, 108 + 2 * i + j, [F2], F16) for i in range(2)] for j in range(2))
        h2_hi, h2_lo = ([at(arena, 112 + 8 * i + 4 * j, [FT2, T], F16) for i in range(2)] for j in range(2))
        h2_32 = [at(arena, 12 + 2 * i, [T]) for i in range(4)]
        y2_hi, y2_lo = at(arena, 20, [T], F16), at(arena, 21, [T], F16)
        b1n = at(arena, 128, [F2])
        b2n = at(arena, 130, [D])
        b1T = at(arena, 130.5, [FT2, E2])
        cmp = at(arena, 131, [B, E2, E2])
        kk_nat = at(arena, 135, [2, D])

        q_hh = at(arena, 0, [H3, T], F16)
        q_lo = at(arena, 16, [H3 // 2, T], F16)
        k3 = [at(arena, 24 + 8 * i, [2, NK], F16) for i in range(2)]
        wk_hi = at(arena, 40, [CT, 1024], F16)
        wk_lo = at(arena, 44, [CT, 1024], F16)
        v3 = [at(arena, 64 + 32 * i, [NCH, 8, 2 * DH3], F16) for i in range(2)]
        cT_hi = [at(arena, 48 + 80 * i, [CT, NK], F16) for i in range(2)]
        cT_lo = [at(arena, 56 + 80 * i, [CT, NK], F16) for i in range(2)]
        wq_nat = at(main, 0, [1024])
        wk_nat = at(main, 4, [CT, 1024])
        wv_nat = at(arena, 0, [CT, 1024])
        ctx0 = at(arena, 80, [NCH, DC])
        wq_nk = at(arena, 8, [H3, DH3])
        wn = sb("wn", [128, H3])
        p3 = [at(main, 8 * i, [NK]) for i in range(2)]
        pT_hi = at(main, 16, [NCH, 128], F16)
        pT_lo = at(main, 20, [NCH, 128], F16)
        oT3 = yy[:, :].rearrange("p (f q) -> p f q", f=8)

        wqkv_sb = at(arena, 152, [3 * D])
        wproj_sb = at(arena, 153.5, [D])
        f1g = at(arena, 154, [E5])
        m16 = at(arena, 144, [H4, S], F16)
        v4 = at(arena, 155, [B, H4, 2 * (DH4 + 1)], F16)
        qT4 = at(arena, 0, [T])
        kT4 = at(arena, 2, [T])
        q4_hi, q4_lo = at(arena, 4, [T], F16), at(arena, 5, [T], F16)
        k4_hi, k4_lo = at(arena, 6, [T], F16), at(arena, 7, [T], F16)
        kb_hi = [at(arena, 8 + i, [4, S], F16) for i in range(3)]
        kb_lo = [at(arena, 11 + i, [4, S], F16) for i in range(3)]
        p4 = [at(arena, 14 + 2 * i, [4, S]) for i in range(3)]
        pT4_hi = [at(arena, 20 + i, [4, S], F16) for i in range(3)]
        pT4_lo = [at(arena, 23 + i, [4, S], F16) for i in range(3)]
        nm4 = at(arena, 26, [3, 4])
        rs4 = at(arena, 26.5, [H4])
        z4, zl4 = at(arena, 27, [D]), at(arena, 27.5, [D])
        zT4 = at(arena, 28, [D])
        wg5 = [at(arena, 72 + 6 * i, [3 * F5]) for i in range(2)]
        wg_hi, wg_lo = ([at(arena, 30 + 6 * i + 3 * j, [3 * F5], F16) for i in range(4)] for j in range(2))
        y5_hi, y5_lo = at(arena, 54, [T], F16), at(arena, 55, [T], F16)
        h5_32 = [at(arena, 56 + 2 * i, [T]) for i in range(4)]
        sg = [at(arena, 84 + 2 * i, [T]) for i in range(2)]
        h5_hi, h5_lo = ([at(arena, 88 + 8 * i + 4 * j, [FT5, T], F16) for i in range(2)] for j in range(2))
        cmp5 = at(arena, 106, [B, E5, E5])

        ps = es.enter_context(nc.psum_tensor("ps", [128, 8, 512], F32))

        def bank(i):
            return ps[:, i, :]

        for n in ("ld_x", "ld_patch", "ld_c0", "ld_s0", "ld_a0", "ld_f0", "ld_x3", "ld_a1"):
            sem(n)
        block = es.enter_context(nc.Block())

        ndma = {}

        def load(eng, name, dst, src):
            ndma[name] = ndma.get(name, 0) + 16
            eng.dma_start(dst, src).then_inc(sem(name), 16)

        def row(ap1):
            return ap1.rearrange("(a n) -> a n", a=1)

        def col(ap1):
            return ap1.rearrange("(n a) -> n a", a=1)

        def rowb(ap1, n=128):
            return ap1.partition_broadcast(n)

        x_v = x.rearrange("b s d -> s b d")
        out_v = out.rearrange("b s d -> s b d")
        ctx_v = ctx_2048.rearrange("b (c p) f -> b p c f", p=128)

        def ctx_tile(i):
            b, h = divmod(i, NCH // 2)
            if b == 0:
                return i + 1
            u = H3 * (b - 1) + h
            first = NCH // 2 + NCH + H3 // 2 + 4
            return first + 4 * u + 4 * (u + 1) + (i - NCH // 2) + 1

        def swing(u):
            return (4, 6) if u % 2 == 0 else (6, 4)

        def t_bank(u, g):
            a = swing(u + 1)[0]
            return (a, 5, 7, a)[g]


        def pro_bank(n):
            return (0, 1, 2, 4, 5, 6, 7)[n % 7] if n < 31 else (4, 5, 6, 7, 4)[n - 31]

        def q_tile(i):
            return 13 if i == 0 else 17 + 2 * i

        @block.sync
        def _(sp):
            load(sp, "ld_x", xs[0][:], x_v)
            load(sp, "ld_patch", patch_i, patch_lens.rearrange("b (p c) -> p b c", c=NCH))
            load(sp, "ld_c0", c0, ctx_2048[:, 0:128, :].rearrange("b p f -> p b f"))
            load(sp, "ld_s0", w_in, L0_W_in)
            load(sp, "ld_s0", biases[:, 0:1], col(L0_g_res))
            load(sp, "ld_s0", ginit_bc, rowb(L0_g_init[0:D]))
            load(sp, "ld_s0", rows[0:1, 0:D], row(L0_b_in))
            for i, f in enumerate((fmq1, fmq2, fmk1, fmk2)):
                load(sp, "ld_a0", f_nat[0:DK1, i, :], f)
            load(sp, "ld_a0", qo_nat[:, 0, :], q_w)
            load(sp, "ld_a0", qo_nat[:, 1, :], o_w)
            load(sp, "ld_a0", gate_nat[0:E1, :], gate_w)
            load(sp, "ld_a0", k_nat, k_w.rearrange("e k c -> k e c"))
            load(sp, "ld_a0", v_nat, v_w.rearrange("e k c -> k e c"))
            for h in range(H1):
                load(sp, "ld_a0", biases[h * DK1:(h + 1) * DK1, 1:2], col(norm_w))
            load(sp, "ld_f0", kk_nat[0:E2, 0, :], keys)
            load(sp, "ld_f0", kk_nat[0:E2, 1, :], f0_rw)
            load(sp, "ld_f0", rows[0:1, 128:128 + E2], row(f0_rb))
            load(sp, "ld_f0", b1n[0:E2, :], f0_b1)
            load(sp, "ld_f0", b2n[0:E2, :], f0_b2)
            load(sp, "ld_x3", wq_nat, Wq)
            load(sp, "ld_x3", wk_nat, Wkv[:, 0:1024].rearrange("(t c) f -> c t f", c=128))
            load(sp, "ld_x3", wout_sb[:], Wout.rearrange("(t f) d -> f t d", f=128))
            load(sp, "ld_x3", nk_bc[:], rowb(null_kv[0]))
            load(sp, "ld_x3", nv_bc[:], rowb(null_kv[1]))
            load(sp, "ld_x3", lns_bc[:, 0, :], rowb(ln_scale))
            load(sp, "ld_x3", lns_bc[:, 1, :], rowb(ln_bias))
            for i in range(2):
                load(sp, "ld_x3", biases[:, 2 + i:3 + i], col(b_qkv[i * D:(i + 1) * D]))
            for e in range(E2):
                if e == 0:
                    sp.wait_ge(sem("x_ready"), 1)
                if e == 2:
                    sp.wait_ge(sem("x_ready"), 2)
                    load(sp, "ld_wv", wv_nat, Wkv[:, 1024:2048].rearrange("(t c) f -> c t f", c=128))
                    for i in range(2):
                        load(sp, "ld_ctx0", ctx0[:, 8 * i:8 * i + 8, :], ctx_v[0, :, 8 * i:8 * i + 8, :])
                if e >= 2:
                    sp.wait_ge(sem("f0_turned"), e - 1)
                sp.dma_start(w1n[e % 2], f0_w1[e].rearrange("(t f) d -> f t d", f=128)).then_inc(sem(f"w0_{e % 2}"), 16)
                sp.dma_start(w2n[e % 2], f0_w2[e]).then_inc(sem(f"w0_{e % 2}"), 16)
            sp.wait_ge(sem("y_ready"), 4)
            load(sp, "ld_a1", wqkv_sb, w_qkv)
            load(sp, "ld_a1", wproj_sb, w_proj)
            load(sp, "ld_a1", rows4[0:1, 0:D], row(b_qkv[2 * D:3 * D]))
            load(sp, "ld_a1", rows4[0:1, D:2 * D], row(b_proj))
            load(sp, "ld_a1", f1g, f1_gate)
            for i in range(NCH // 2, B * NCH // 2):
                b, c = divmod(2 * i, NCH)
                if i >= NCH // 2 + 2:
                    sp.wait_ge(sem("tile_full"), ctx_tile(i - 2))
                sp.dma_start(ctx_nat[i % 2][:], ctx_v[b, :, c:c + 2, :]).then_inc(sem(f"ctx_in{i % 2}"), 16)
            sp.wait_ge(sem("o3_ready"), B)
            for e in range(E5):
                if e >= 2:
                    sp.wait_ge(sem("wg_lo"), e - 1)
                k = e % 2
                sp.dma_start(wg5[k][:, 0:F5], f1_w1[e]).then_inc(sem(f"w5_{k}"), 16)
                sp.dma_start(wg5[k][:, F5:2 * F5], f1_w3[e]).then_inc(sem(f"w5_{k}"), 16)
                sp.dma_start(wg5[k][:, 2 * F5:].rearrange("p (t d) -> p t d", t=FT5),
                             f1_w2[e].rearrange("(t f) d -> f t d", f=128)).then_inc(sem(f"w5_{k}"), 16)
            sp.wait_ge(sem("x_ready"), 6)
            sp.dma_start(out_v, xs[0][:]).then_inc(sem("out_done"), 16)
            sp.wait_ge(sem("out_done"), 16)

        @block.gpsimd
        def _(pool):
            n = [0]

            def step(ins):
                n[0] += 1
                ins.then_inc(sem("pool_step"), 1)
                pool.wait_ge(sem("pool_step"), n[0])

            def mask(ap, pattern, base, mult, op, fill):
                step(pool.affine_select(out=ap, in_=ap, compare_op=op, fill=fill, base=base,
                                        pattern=pattern, channel_multiplier=mult))

            step(pool.memset(reset, 1.0))
            step(pool.memset(reset.rearrange("p (a c) -> p a c", c=NCH)[:, :, 0:1], 0.0))
            step(pool.memset(strict, 1.0))
            mask(strict, [[1, 128]], 0, -1, ALU.is_gt, 0.0)
            step(pool.iota(iotap_i[:, 0:1], pattern=[[0, 1]], base=0, channel_multiplier=1))
            step(pool.iota(iota16_i[:, 0:16], pattern=[[1, 16]], base=0, channel_multiplier=0))
            pool.sem_inc(sem("const_p"), 1)
            step(pool.memset(ident[:], 0.0))
            mask(ident[:], [[-1, 128]], 0, 1, ALU.not_equal, 1.0)
            step(pool.memset(ones[:], 1.0))
            step(pool.memset(after_b, 1.0))
            mask(after_b, [[-1, 16], [1, S]], 0, -16, ALU.is_ge, 0.0)
            pool.sem_inc(sem("const_a"), 1)
            step(pool.memset(lift[:], LIFT))
            step(pool.memset(causal[:], 1.0))
            mask(causal[:], [[1, 128]], 0, -1, ALU.is_ge, 0.0)
            step(pool.memset(blk16, 1.0))
            mask(blk16, [[-DK1, H1], [0, DK1]], 0, 1, ALU.is_ge, 0.0)
            mask(blk16, [[DK1, H1], [0, DK1]], DK1 - 1, -1, ALU.is_ge, 0.0)
            step(pool.memset(rank_t[:], 0.0))
            mask(rank_t[:], [[1, E2], [-1, E2]], 0, 0, ALU.is_gt, TINY)
            pool.wait_ge(sem("ld_a0"), ndma["ld_a0"])
            step(pool.tensor_copy(f_rep[0:DK1], bc(f_nat[0:DK1, :, :], 2, H1)))
            pool.sem_inc(sem("const_b"), 1)
            for e in range(E1):
                pool.wait_ge(sem("k1_hi"), e + 1)
                pool.tensor_tensor(kT1_lo[:, e, :], k32[e % 2], kT1_hi[:, e, :], ALU.subtract)\
                    .then_inc(sem("k1_lo"), 1)
            for i in range(B * E1):
                pool.wait_ge(sem("am_hi_ready"), i + 1)
                pool.tensor_tensor(am_lo[i % 4][:, 0:HP1, :], am[i % 3][:, 0:HP1, :], am_hi[i % 4][:, 0:HP1, :],
                                   ALU.subtract).then_inc(sem("am_lo_pool"), 1)
            pool.wait_ge(sem("x_ready"), 2)
            pool.wait_ge(sem("ld_x3"), ndma["ld_x3"])
            step(pool.tensor_copy(wk_hi, wk_nat))
            step(pool.tensor_tensor(wk_lo, wk_nat, wk_hi, ALU.subtract))
            pool.wait_ge(sem("ld_wv"), 16)
            step(pool.tensor_copy(wv_hi[:], wv_nat))
            step(pool.tensor_tensor(wv_lo[:], wv_nat, wv_hi[:], ALU.subtract))
            step(pool.tensor_tensor(wq_nk, wq_nat.rearrange("p (h d) -> p h d", h=H3), bc(nk_bc[:], 1, H3),
                                    ALU.mult))
            pool.sem_inc(sem("w3_split"), 1)
            for i in range(H3 // 2):
                pool.wait_ge(sem("tile_hi"), q_tile(i))
                pool.tensor_copy(q_hh[64:128, 2 * i, :], q_hh[0:64, 2 * i, :])
                step(pool.tensor_copy(q_hh[0:64, 2 * i + 1, :], q_hh[64:128, 2 * i + 1, :]))
                pool.sem_inc(sem("q_both"), 1)
            step(pool.memset(m16, 1.0))
            mask(m16, [[-DH4, H4], [0, S]], 0, 1, ALU.is_ge, 0.0)
            mask(m16, [[DH4, H4], [0, S]], DH4 - 1, -1, ALU.is_ge, 0.0)
            step(pool.memset(v4, 0.0))
            step(pool.memset(v4[:, :, :, DH4:DH4 + 1], 1.0))
            pool.sem_inc(sem("const_c"), 1)
            pool.wait_ge(sem("qk4_lo"), 1)
            for i in range(4 * B):
                b, g = divmod(i, 4)
                if i >= 3:
                    pool.wait_ge(sem("s4_ps"), i - 2)
                pool.tensor_tensor(kb_lo[i % 3], bc(k4_lo[:, b * S:(b + 1) * S], 1, 4),
                                   m16[:, 4 * g:4 * g + 4, :], ALU.mult).then_inc(sem("kb_lo_ready"), 1)
            for e in range(E5):
                pool.wait_ge(sem("wg_hi"), e + 1)
                pool.tensor_tensor(wg_lo[e % 4], wg5[e % 2], wg_hi[e % 4], ALU.subtract).then_inc(sem("wg_lo"), 1)

        @block.tensor
        def _(pe):
            def mm(o, lhsT, rhs, start=True, stop=True, **k):
                return pe.matmul(o, lhsT, rhs, start=start, stop=stop, **k)

            def tr(o, i, n=128):
                return pe.transpose(o, i, ident[0:n, 0:n])

            def turn_y(stage, b_ps):
                pe.wait_ge(sem("y_ready"), stage + 1)
                for b in range(B):
                    last = tr(bank(b_ps)[:, b * S:(b + 1) * S], y[:, b, :])
                last.then_inc(sem("yT_ps"), 1)

            pe.wait_ge(sem("scan_ready"), 1)
            mm(bank(1)[:, 0:12], strict, scan.rearrange("p (a c) -> p a c", c=NCH)[:, :, NCH - 1])\
                .then_inc(sem("prefix_ps"), 1)
            pe.wait_ge(sem("const_a"), 1)
            pe.wait_ge(sem("ld_s0"), ndma["ld_s0"])
            tr(bank(0)[:, 0:D], w_in).then_inc(sem("w_inT_ps"), 1)
            pe.wait_ge(sem("onehot_ready"), 1)
            for b in range(B):
                for c in range(NCH):
                    last = mm(bank(1)[0:8, 64 + 16 * b:80 + 16 * b], hi_oh[:, b * NCH + c, :],
                              lo_oh[:, b * NCH + c, :], start=(c == 0), stop=(c == NCH - 1))
            last.then_inc(sem("count_ps"), 1)
            pe.wait_ge(sem("bnd_ready"), 1)
            for b in range(B):
                for l in range(16):
                    last = mm(bank(2)[:, b * S:(b + 1) * S], bnd[0:8, b, l:l + 1].broadcast_to([8, 128]),
                              after_b[0:8, l, :], start=(l == 0), stop=(l == 15))
            last.then_inc(sem("plug_ps"), 1)
            turn_y(0, 3)
            pe.wait_ge(sem("const_b"), 1)
            pe.wait_ge(sem("ld_a0"), ndma["ld_a0"])
            for i in range(4):
                last = mm(bank(5)[:, i * 128:(i + 1) * 128], f_rep[0:DK1, i, :, :].rearrange("p a b -> p (a b)"),
                          bc(ident[0:DK1, 0:DK1], 1, H1))
            last.then_inc(sem("bd_ps"), 1)
            tr(bank(6)[:, 0:D], qo_nat[:, 1, :])
            tr(bank(6)[:, D:D + E1], gate_nat[0:E1, :], E1).then_inc(sem("og_ps"), 1)
            pe.wait_ge(sem("w0T_ready"), 1)
            pe.wait_ge(sem("r0T_ready"), 1)
            for b in range(B):
                o = bank(4)[:, b * D:(b + 1) * D]
                mm(o, r0T[:, b * S:(b + 1) * S], w_inT, stop=False)
                last = mm(o, ones[0:1, 0:S], rows[0:1, 0:D], start=False)
            last.then_inc(sem("s0_ps"), 1)
            pe.wait_ge(sem("wt0_ready"), 1)
            for b in range(B):
                last = mm(bank(2)[:, b * D:(b + 1) * D], wt0[:, b, :], u0[:, b, :])
            last.then_inc(sem("s0_ps"), 1)

            pe.wait_ge(sem("bd_ready"), 1)
            mm(bank(7)[:, 0:256], qo_nat[:, 0, :], bdT[:, 0:2, :].rearrange("p a b -> p (a b)")).then_inc(sem("mq_ps"), 1)
            for e in range(E1):
                if e % 2 == 0 and e >= 4:
                    pe.wait_ge(sem("mk_ready"), e // 2 - 1)
                if e == 2:
                    pe.wait_ge(sem("og_ready"), 1)
                last = mm(bank(5 + (e // 2) % 2)[:, (e % 2) * 256:(e % 2) * 256 + 256],
                          k_nat[:, e, :], bdT[:, 2:4, :].rearrange("p a b -> p (a b)"))
                if e % 2 == 1:
                    last.then_inc(sem("mk_ps"), 1)
            for g in range(2):
                pe.wait_ge(sem("mk_ready"), 3 + g)
                for e in range(4):
                    last = tr(bank(5 + g)[:, e * 128:(e + 1) * 128], v_nat[:, 4 * g + e, :])
                last.then_inc(sem("vw_ps"), 1)
            turn_y(1, 3)
            pe.wait_ge(sem("yT_ready"), 1)
            for b in range(B):
                last = mm(bank(0)[:, b * E1:(b + 1) * E1], yT[:, b * S:(b + 1) * S], gateT)
            last.then_inc(sem("logit_ps"), 1)
            pe.wait_ge(sem("mq_ready"), 1)
            mm(bank(1), mqT[:, 0, :], yT)
            mm(bank(2), mqT[:, 1, :], yT).then_inc(sem("qk_ps"), 1)
            pe.wait_ge(sem("mk_ready"), 4)
            pe.wait_ge(sem("vw_ready"), 2)
            for e in range(E1):
                lo = 4 + 2 * (e % 2)
                if e >= 2:
                    pe.wait_ge(sem("k1_ready"), e)
                mm(bank(lo), mkT[:, e, 0, :], yT)
                mm(bank(lo + 1), mkT[:, e, 1, :], yT).then_inc(sem("qk_ps"), 1)
                b, g = divmod(e, 2)
                pe.wait_ge(sem("k1_ready"), 1)
                if e >= 2:
                    pe.wait_ge(sem("v1_ready"), e - 1)
                mm(bank(1 + e % 2), yT[:, b * S:(b + 1) * S],
                   v_wT[:, 4 * g:4 * g + 4, :].rearrange("p a b -> p (a b)")).then_inc(sem("v1_ps"), 1)
                if e == 0:
                    pe.wait_ge(sem("w_ready"), 1)
                    for bb in range(B):
                        last = tr(bank(0)[0:E1, bb * S:(bb + 1) * S], wgt[:, bb, 0:E1])
                    last.then_inc(sem("rT_ps"), 1)
                    pe.wait_ge(sem("rT_ready"), 1)
                if e >= 2:
                    pe.wait_ge(sem("g_ready"), e - 1)
                mm(bank(0 if e % 2 else 3), ident[0:E1, e:e + 1].broadcast_to([E1, 128]), rT_sb[0:E1, :])\
                    .then_inc(sem("g_ps"), 1)
            pe.wait_ge(sem("g_ready"), E1)
            pe.wait_ge(sem("v1_ready"), 2 * B)
            pe.wait_ge(sem("k1_lo"), E1)
            pe.wait_ge(sem("qbd_ready"), 1)

            def scores1(i):
                b, e = divmod(i, E1)
                lo = (0, 2, 5)[i % 3]
                if i >= 3:
                    pe.wait_ge(sem("am_ready"), i - 2)
                if i == 0:
                    pe.wait_ge(sem("v1_ready"), 2 * B)
                kh, kl = kT1_hi[:, e, b * S:(b + 1) * S], kT1_lo[:, e, b * S:(b + 1) * S]
                for g in range(2):
                    qh, ql = (q[:, b, 4 * g:4 * g + 4, :].rearrange("p a b -> p (a b)") for q in (qbd_hi, qbd_lo))
                    mm(bank(lo + g), kh, qh, stop=False)
                    mm(bank(lo + g), kh, ql, start=False, stop=False)
                    last = mm(bank(lo + g), kl, qh, start=False)
                last.then_inc(sem("sc1_ps"), 1)

            def mix1(i):
                b, e = divmod(i, E1)
                pe.wait_ge(sem("am_lo_pool"), i + 1)
                pe.wait_ge(sem("am_lo_dve"), i + 1)
                for h in range(H1):
                    o = (b % 2) * 256 + h * 2 * DK1
                    bk = bank(4 + 3 * (b // 2))
                    mm(bk[:, o:o + 2 * DK1], am_hi[i % 4][:, h, :], v1[:, b, e, h, :],
                       start=(i % (2 * E1) == 0 and h == 0), stop=False, skip_group_check=True)
                    last = mm(bk[:, o:o + DK1], am_lo[i % 4][:, h, :], v1[:, b, e, h, 0:DK1], start=False,
                              stop=(e == E1 - 1), skip_group_check=True)
                last.then_inc(sem("o1_ps"), 1)

            for i in range(B * E1 + 3):
                if i < B * E1:
                    scores1(i)
                if i >= 3:
                    mix1(i - 3)
            pe.wait_ge(sem("z1_ready"), 1)
            for b in range(B):
                last = tr(bank(5)[:, b * S:(b + 1) * S], y[:, b, :])
            last.then_inc(sem("z1T_ps"), 1)
            pe.wait_ge(sem("z1T_ready"), 1)
            for b in range(B):
                last = mm(bank(6)[:, b * D:(b + 1) * D], yT[:, b * S:(b + 1) * S], o_wT)
            last.then_inc(sem("s1_ps"), 1)

            pe.wait_ge(sem("ld_f0"), ndma["ld_f0"])
            for t in range(FT2):
                tr(bank(7)[:, 64 + t * E2:64 + (t + 1) * E2], b1n[0:E2, t * 128:(t + 1) * 128], E2)
            pe.wait_ge(sem("kk_ready"), 1)
            for i in range(2):
                last = tr(bank(7)[:, i * E2:(i + 1) * E2], kk_nat[0:E2, i, :], E2)
            last.then_inc(sem("keysT_ps"), 1)

            def turn_w1(e):
                pe.wait_ge(sem(f"w0_{e % 2}"), 32 * (e // 2 + 1))
                if e >= 1:
                    pe.wait_ge(sem("w1T_ready"), e)
                for t in range(FT2):
                    last = tr(bank(4)[:, t * 128:(t + 1) * 128], w1n[e % 2][:, t, :])
                last.then_inc(sem("w1T_ps"), 1)

            def turn_w2(e):
                if e >= 1:
                    pe.wait_ge(sem("w2T_ready"), e)
                for t in range(FT2):
                    last = tr(bank(5)[:, t * 128:(t + 1) * 128], w2n[e % 2][:, t * 128:(t + 1) * 128])
                last.then_inc(sem("f0_turned"), 1)

            turn_w1(0)
            turn_w2(0)
            turn_y(2, 3)
            pe.wait_ge(sem("keysT_ready"), 1)
            o = bank(7)[:, 384:384 + E2]
            mm(o, ones[:, 0:S], keysT[:, 0, :], stop=False)
            mm(o, ones[0:1, 0:S], rows[0:1, 128:128 + E2], start=False)
            pe.wait_ge(sem("yT_ready"), 2)
            for b in range(B):
                o = bank(7)[:, 256 + b * E2:256 + (b + 1) * E2]
                last = mm(o, yT[:, b * S:(b + 1) * S], keysT[:, 1, :])
            last.then_inc(sem("logit_ps"), 1)

            def up0(e, t):
                k = FT2 * e + t
                if k >= 4:
                    pe.wait_ge(sem("gelu_done"), k - 3)
                wh, wl = (w[e % 2][:, t * 128:(t + 1) * 128] for w in (w1T_hi, w1T_lo))
                mm(bank(k % 4), wh, y2_hi, stop=False)
                mm(bank(k % 4), wh, y2_lo, start=False, stop=False)
                mm(bank(k % 4), wl, y2_hi, start=False).then_inc(sem("up0_ps"), 1)

            def down0(e):
                pe.wait_ge(sem("w2T_ready"), e + 1)
                if e == 1:
                    pe.wait_ge(sem("acc0_start"), 1)
                if e >= 2:
                    pe.wait_ge(sem("acc0_ready"), e - 1)
                for b in range(B):
                    o = bank(6 + e % 2)[:, b * D:(b + 1) * D]
                    for t in range(FT2):
                        if b == 0:
                            pe.wait_ge(sem("h2_ready"), FT2 * e + t + 1)
                        hh, hl = (h[e % 2][:, t, b * S:(b + 1) * S] for h in (h2_hi, h2_lo))
                        wh, wl = (w[e % 2][:, t * 128:(t + 1) * 128] for w in (w2T_hi, w2T_lo))
                        mm(o, hh, wh, start=(t == 0), stop=False)
                        mm(o, hh, wl, start=False, stop=False)
                        last = mm(o, hl, wh, start=False, stop=(t == FT2 - 1))
                last.then_inc(sem("down0_ps"), 1)

            pe.wait_ge(sem("y2_lo"), 1)
            for e in range(E2 + 1):
                if e + 1 < E2:
                    turn_w1(e + 1)
                if e < E2:
                    pe.wait_ge(sem("w1T_ready"), e + 1)
                    for t in range(FT2):
                        up0(e, t)
                if e == 1:
                    pe.wait_ge(sem("w_ready"), 2)
                    for b in range(B):
                        last = tr(bank(6)[0:E2, b * S:(b + 1) * S], wgt[:, b, :])
                    last.then_inc(sem("rT_ps"), 1)
                    pe.wait_ge(sem("rT_ready"), 2)
                    for b in range(B):
                        last = mm(bank(7)[:, b * D:(b + 1) * D], rT_sb[0:E2, b * S:(b + 1) * S], b2n[0:E2, :])
                    last.then_inc(sem("b2_ps"), 1)
                if e >= 1:
                    down0(e - 1)
                if e + 1 < E2:
                    turn_w2(e + 1)

            tiles = [0]
            last_in = {}

            def claim(bk):
                if bk in last_in:
                    name, value = last_in[bk]
                    pe.wait_ge(sem(name), value)

            def full(ins, bk):
                tiles[0] += 1
                last_in[bk] = "tile_lo", tiles[0]
                ins.then_inc(sem("tile_full"), 1)

            def ctx_turn(i, bk=6):
                if i == 0:
                    pe.wait_ge(sem("ld_ctx0"), ndma["ld_ctx0"])
                if i >= NCH // 2:
                    pe.wait_ge(sem(f"ctx_in{i % 2}"), 16 * ((i - NCH // 2) // 2 + 1))
                claim(bk)
                for c in range(2):
                    for t in range(CT):
                        last = tr(bank(bk)[:, (t * 2 + c) * 128:(t * 2 + c + 1) * 128],
                                  (ctx_nat[i % 2][:, c] if i >= NCH // 2 else ctx0[:, 2 * i + c])
                                  [:, t * 128:(t + 1) * 128])
                full(last, bk)
                assert tiles[0] == ctx_tile(i)

            def v_proj(n, bk):
                g, c = divmod(n, NCH)
                b = g // 2
                pe.wait_ge(sem("tile_lo"), ctx_tile(8 * b + c // 2))
                claim(bk)
                k, f = b % 2, (g % 2) * 512
                for t in range(CT):
                    ch, cl = cT_hi[k][:, t, c * 128:(c + 1) * 128], cT_lo[k][:, t, c * 128:(c + 1) * 128]
                    wh, wl = wv_hi[:, t, f:f + 512], wv_lo[:, t, f:f + 512]
                    mm(bank(bk), ch, wh, start=(t == 0), stop=False)
                    mm(bank(bk), ch, wl, start=False, stop=False)
                    last = mm(bank(bk), cl, wh, start=False, stop=(t == CT - 1))
                full(last, bk)

            def q_proj(i, bk):
                claim(bk)
                full(mm(bank(bk), wq_nat[:, i * 128:(i + 1) * 128], yT), bk)
                assert tiles[0] == q_tile(i)

            def k_proj(m, bk):
                p, j = divmod(m, 4)
                b, i = divmod(p, H3 // 2)
                k = b % 2
                if j == 0 and i == 0:
                    pe.wait_ge(sem("tile_lo"), ctx_tile(8 * b + 7))
                claim(bk)
                w = slice(i * 128, (i + 1) * 128)
                for t in range(CT):
                    ch, cl = cT_hi[k][:, t, j * 512:(j + 1) * 512], cT_lo[k][:, t, j * 512:(j + 1) * 512]
                    mm(bank(bk), wk_hi[:, t, w], ch, start=(t == 0), stop=False)
                    mm(bank(bk), wk_hi[:, t, w], cl, start=False, stop=False)
                    last = mm(bank(bk), wk_lo[:, t, w], ch, start=False, stop=(t == CT - 1))
                full(last, bk)
                k_no[p % 2, j] = tiles[0]

            k_no = {}

            def scores3(u, j):
                b, h = divmod(u, H3)
                claim(j)
                if u == 0 and j == 3:
                    pe.wait_ge(sem("sim0_ready"), 1)
                if j == 0:
                    if u >= 1:
                        pe.wait_ge(sem("exp_done"), u)
                    if u < H3 and h % 2 == 0:
                        pe.wait_ge(sem("q_both"), h // 2 + 1)
                        pe.wait_ge(sem("tile_lo"), q_tile(h // 2))
                if h % 2 == 0:
                    pe.wait_ge(sem("tile_lo"), k_no[(u // 2) % 2, j])
                k = k3[(u // 2) % 2][:, h % 2, j * 512:(j + 1) * 512]
                half = slice(64 * (h % 2), 64 * (h % 2) + 64)
                mm(bank(j), q_hh[:, h, b * S:(b + 1) * S], k, start=True, stop=False)
                last = mm(bank(j), q_lo[half, h // 2, b * S:(b + 1) * S], k[half, :], start=False, stop=True)
                if j % 2:
                    last.then_inc(sem("s3_ps"), 1)

            def p_turn(u, g):
                bk = t_bank(u, g)
                if g == 0:
                    pe.wait_ge(sem("exp_done"), u + 1)
                claim(bk)
                for j in range(4):
                    c = 4 * g + j
                    last = tr(bank(bk)[:, j * 128:(j + 1) * 128], p3[u % 2][:, c * 128:(c + 1) * 128])
                full(last, bk)
                pT_no[g] = tiles[0]

            pT_no = {}

            def pv(u):
                claim(7)
                hh = (u % H3) % 8
                v = v3[(u // 8) % 2]
                for c in range(NCH):
                    if c % 4 == 0:
                        pe.wait_ge(sem("tile_lo"), pT_no[c // 4])
                    mm(bank(7)[:, 0:2 * DH3], pT_hi[:, c, :], v[:, c, hh, :], start=(c == 0), stop=False,
                       skip_group_check=True)
                    last = mm(bank(7)[:, 0:DH3], pT_lo[:, c, :], v[:, c, hh, 0:DH3], start=False,
                              stop=(c == NCH - 1), skip_group_check=True)
                last.then_inc(sem("pv_ps"), 1)
                last_in[7] = "o_head", u + 1

            def heads_turn(b, i):
                if i == 0:
                    pe.wait_ge(sem("z3_ready"), b + 1)
                claim(6 - i)
                for j in range(4):
                    f = 4 * i + j
                    last = tr(bank(6 - i)[:, j * 128:(j + 1) * 128], zat[:, f * 128:(f + 1) * 128])
                last.then_inc(sem("oT_ps"), 1)
                last_in[6 - i] = "oT_ready", 2 * b + i + 1

            def out_proj3(b):
                pe.wait_ge(sem("oT_ready"), 2 * (b + 1))
                claim(7)
                for f in range(8):
                    last = mm(bank(7)[:, 0:D], oT3[:, f, :], wout_sb[:, f, :], start=(f == 0), stop=(f == 7))
                last.then_inc(sem("o3_ps"), 1)
                last_in[7] = "o3_ready", b + 1

            pe.wait_ge(sem("w3_split"), 1)
            for i in range(8):
                if i == 5:
                    pe.wait_ge(sem("acc0_ready"), E2)
                ctx_turn(i, pro_bank(i))
            for n in range(4):
                v_proj(n, pro_bank(8 + n))
            turn_y(3, 3)
            pe.wait_ge(sem("yT_ready"), 3)
            q_proj(0, pro_bank(12))
            pe.wait_ge(sem("wn_ready"), 1)
            for b in range(B):
                last = mm(bank(3)[:, b * H3:(b + 1) * H3], yT[:, b * S:(b + 1) * S], wn[:])
            last.then_inc(sem("sim0_ps"), 1)
            for j in range(4):
                k_proj(j, pro_bank(13 + j))
            for i in range(1, H3 // 2):
                v_proj(3 + i, pro_bank(15 + 2 * i))
                q_proj(i, pro_bank(16 + 2 * i))
            for n in range(11, NCH):
                v_proj(n, pro_bank(20 + n))
            for n in (0, 1, 2):
                claim(n)
            NU = B * H3
            for u in range(NU + 1):
                b, h = divmod(u, H3)
                new, old = u < NU, u >= 1
                done = b - 1 if h == 1 and b >= 1 else None
                if done is not None:
                    heads_turn(done, 0)
                    heads_turn(done, 1)
                if new and done is not None:
                    for j in range(4):
                        scores3(u, j)
                if old:
                    p_turn(u - 1, 0)
                    p_turn(u - 1, 1)
                if new and done is None:
                    for j in range(4):
                        scores3(u, j)
                if done is not None:
                    out_proj3(done)
                if old:
                    p_turn(u - 1, 2)
                    p_turn(u - 1, 3)
                n = 4 + 2 * u
                more_k = n < 4 * B * H3 // 2
                a, c = swing(u)
                if more_k:
                    k_proj(n, c)
                m = NCH + 2 * u
                more_v = m < 2 * B * NCH
                if more_k and not more_v:
                    k_proj(n + 1, 5)
                late = u % 8 == 0
                if more_v and not late:
                    v_proj(m, 5)
                if old:
                    pv(u - 1)
                if more_v and late:
                    v_proj(m, 5)
                if more_k and more_v:
                    k_proj(n + 1, a)
                if more_v:
                    v_proj(m + 1, 7)
                if new and b + 1 < B and h < 8:
                    pe.wait_ge(sem("exp_done"), u + 1)
                    ctx_turn(8 * (b + 1) + h, 3)
            heads_turn(B - 1, 0)
            heads_turn(B - 1, 1)
            out_proj3(B - 1)

            turn_y(4, 3)
            pe.wait_ge(sem("ld_a1"), ndma["ld_a1"])
            pe.wait_ge(sem("yT_ready"), 4)
            mm(bank(0), wqkv_sb[:, 0:D], yT)
            mm(bank(1), wqkv_sb[:, D:2 * D], yT).then_inc(sem("qk4_ps"), 1)
            for b in range(B):
                o = bank(2)[:, b * D:(b + 1) * D]
                mm(o, yT[:, b * S:(b + 1) * S], wqkv_sb[:, 2 * D:3 * D], stop=False)
                last = mm(o, ones[0:1, 0:S], rows4[0:1, 0:D], start=False)
            last.then_inc(sem("v4_ps"), 1)

            def scores4(i):
                b, g = divmod(i, 4)
                pe.wait_ge(sem("kb_hi_ready"), i + 1)
                if i >= 3:
                    pe.wait_ge(sem("p4_ready"), i - 2)
                bk, o = (0, 1, 3)[i % 3], slice(b * S, (b + 1) * S)
                kh, kl = (k[i % 3].rearrange("p a b -> p (a b)") for k in (kb_hi, kb_lo))
                mm(bank(bk), q4_hi[:, o], kh, stop=False)
                mm(bank(bk), q4_lo[:, o], kh, start=False, stop=False)
                pe.wait_ge(sem("kb_lo_ready"), i + 1)
                mm(bank(bk), q4_hi[:, o], kl, start=False).then_inc(sem("s4_ps"), 1)

            def p_turn4(i):
                pe.wait_ge(sem("p4_ready"), i + 1)
                if i >= 2:
                    pe.wait_ge(sem("t4_lo"), i - 1)
                for j in range(4):
                    last = tr(bank(4 + i % 2)[:, j * 128:(j + 1) * 128], p4[i % 3][:, j, :])
                last.then_inc(sem("t4_full"), 1)

            W4 = 2 * (DH4 + 1)

            def mix4(i):
                b, g = divmod(i, 4)
                pe.wait_ge(sem("t4_lo"), i + 1)
                if i == 0:
                    pe.wait_ge(sem("v4_ready"), 1)
                if b >= 2 and g == 0:
                    pe.wait_ge(sem("z4_ready"), b - 1)
                bk = (6, 2)[b % 2]
                for j in range(4):
                    h = 4 * g + j
                    o = h * W4
                    mm(bank(bk)[:, o:o + W4], pT4_hi[i % 3][:, j, :], v4[:, b, h, :], start=(h == 0), stop=False,
                       skip_group_check=True)
                    last = mm(bank(bk)[:, o:o + DH4 + 1], pT4_lo[i % 3][:, j, :], v4[:, b, h, 0:DH4 + 1],
                              start=False, skip_group_check=True)
                last.then_inc(sem("o4_ps"), 1)

            def z_turn4(b):
                pe.wait_ge(sem("z4_ready"), b + 1)
                if b >= 1:
                    pe.wait_ge(sem("s4_out"), b)
                tr(bank(7)[:, 0:128], z4).then_inc(sem("zT4_ps"), 1)

            def proj4(b):
                o = bank(7)[:, 128:256]
                pe.wait_ge(sem("zT4_ready"), b + 1)
                mm(o, zT4, wproj_sb, stop=False)
                mm(o, ones[0:1, 0:S], rows4[0:1, D:2 * D], start=False).then_inc(sem("s4o_ps"), 1)

            for i in range(4 * B + 8):
                if i < 4 * B:
                    scores4(i)
                if 2 <= i < 4 * B + 2:
                    p_turn4(i - 2)
                if 4 <= i < 4 * B + 4:
                    mix4(i - 4)
                if i >= 9 and i % 4 == 1:
                    z_turn4(i // 4 - 2)
                if i >= 9 and i % 4 == 2:
                    proj4(i // 4 - 2)

            turn_y(5, 3)
            pe.wait_ge(sem("ld_a1"), ndma["ld_a1"])
            pe.wait_ge(sem("yT_ready"), 5)
            for b in range(B):
                last = mm(bank(0)[:, b * E5:(b + 1) * E5], yT[:, b * S:(b + 1) * S], f1g)
            last.then_inc(sem("logit_ps"), 1)
            pe.wait_ge(sem("l5_ready"), 1)

            pe.wait_ge(sem("y5_lo"), 1)

            def up5(e, t):
                k = FT5 * e + t
                lo = 2 * (k % 3)
                if k >= 3:
                    pe.wait_ge(sem("h5_product"), k - 2)
                if t == 0:
                    pe.wait_ge(sem("wg_lo"), e + 1)
                for i in range(2):
                    o = slice(i * F5 + t * 128, i * F5 + (t + 1) * 128)
                    mm(bank(lo + i), wg_hi[e % 4][:, o], y5_hi, stop=False)
                    mm(bank(lo + i), wg_hi[e % 4][:, o], y5_lo, start=False, stop=False)
                    last = mm(bank(lo + i), wg_lo[e % 4][:, o], y5_hi, start=False)
                last.then_inc(sem("up5_ps"), 1)

            def down5(e):
                if e >= 2:
                    pe.wait_ge(sem("acc5_ready"), e - 1)
                for b in range(B):
                    o = bank(6 + e % 2)[:, b * D:(b + 1) * D]
                    for t in range(FT5):
                        if b == 0:
                            pe.wait_ge(sem("h5_ready"), FT5 * e + t + 1)
                        hh, hl = (h[e % 2][:, t, b * S:(b + 1) * S] for h in (h5_hi, h5_lo))
                        wh, wl = (w[e % 4][:, 2 * F5 + t * 128:2 * F5 + (t + 1) * 128] for w in (wg_hi, wg_lo))
                        mm(o, hh, wh, start=(t == 0), stop=False)
                        mm(o, hh, wl, start=False, stop=False)
                        last = mm(o, hl, wh, start=False, stop=(t == FT5 - 1))
                last.then_inc(sem("f1_used"), 1)

            for e in range(E5 + 1):
                for t in range(FT5):
                    if e < E5:
                        up5(e, t)
                    if t == 2 and e >= 1:
                        down5(e - 1)

        @block.vector
        def _(dve):
            n = [0]

            def step(ins):
                n[0] += 1
                ins.then_inc(sem("dve_step"), 1)
                dve.wait_ge(sem("dve_step"), n[0])

            def tt(o, a, b, op):
                return dve.tensor_tensor(o, a, b, op)

            def ts(o, a, s1, op0, s2=None, op1=None):
                if s2 is None:
                    return dve.tensor_scalar(o, a, s1, None, op0)
                return dve.tensor_scalar(o, a, s1, s2, op0, op1)

            def stt(o, a, s, b, op0, op1):
                return dve.scalar_tensor_tensor(out=o, in0=a, scalar=s, in1=b, op0=op0, op1=op1)

            def rsqrt(o, v, t):
                step(dve.tensor_scalar(t.bitcast(I32), v.bitcast(I32), 1, None, ALU.logical_shift_right))
                step(ts(o.bitcast(I32), t.bitcast(I32), -1.0, ALU.mult, MAGIC, ALU.add))
                for _ in range(3):
                    step(stt(t, o, -0.5, o, ALU.mult, ALU.mult))
                    step(tt(t, t, v, ALU.mult))
                    step(stt(o, t, 1.5, o, ALU.add, ALU.mult))

            def moments(src):
                for b in range(B):
                    ins = dve.bn_stats(stats[:, b, :], src[:, b, :])
                step(ins)
                for b in range(B):
                    ins = dve.bn_aggr(mv[:, b, :], stats[:, b, :])
                step(ins)

            mean, var = (lambda b: mv[:, b, 0:1]), mv[:, :, 1]

            def layernorm(stage):
                src = xs[stage % 3]
                moments(src)
                v, r, t = small[:, 0, 0:B], small[:, 1, 0:B], small[:, 2, 0:B]
                step(ts(v, var, LN_EPS, ALU.add))
                rsqrt(r, v, t)
                if stage == 2:
                    q = small[:, 3, 0:B]
                    step(tt(q, r, r, ALU.mult))
                    step(stt(q, q, float(D), var, ALU.mult, ALU.mult))
                for b in range(B):
                    ins = ts(y[:, b, :], src[:, b, :], mean(b), ALU.subtract, r[:, b:b + 1], ALU.mult)
                ins.then_inc(sem("y_ready"), 1)

            def yT_copy(stage):
                dve.wait_ge(sem("yT_ps"), stage + 1)
                dve.tensor_copy(yT, bank(3)).then_inc(sem("yT_ready"), 1)

            def route(stage, k, E, logits, by_prob, cmp_t, meanwhile=None):
                K = {1: 1, 2: 2, 5: 3}[stage]
                mx, d, ex = route_s[:, 0, 0:B], route_s[:, 1, 0:B * E].rearrange("p (b e) -> p b e", b=B), \
                    route_s[:, 2, 0:B * E].rearrange("p (b e) -> p b e", b=B)
                rank = route_s[:, 3, 0:B * E].rearrange("p (b e) -> p b e", b=B)
                den = route_s[:, 4, 0:B]
                step(dve.tensor_reduce(mx, logits, AX.X, ALU.max))
                tt(d, logits, bc(mx, 2, E), ALU.subtract).then_inc(sem("route_d"), 1)
                if meanwhile:
                    meanwhile()
                dve.wait_ge(sem("route_e"), K)
                by = ex if by_prob else logits
                step(tt(cmp_t, bc(by, 2, E), bc(by, 3, E), ALU.subtract))
                step(tt(cmp_t, cmp_t, bc(rank_t[:, 0:E, 0:E], 1, B), ALU.is_ge))
                step(dve.tensor_reduce(rank, cmp_t, AX.X, ALU.add))
                step(ts(rank, rank, float(k), ALU.is_lt))
                step(tt(ex, ex, rank, ALU.mult))
                step(dve.tensor_reduce(den, ex, AX.X, ALU.add))
                step(dve.reciprocal(den, den))
                tt(wgt[:, :, 0:E], ex, bc(den, 2, E), ALU.mult).then_inc(sem("w_ready"), 1)
                return rank

            dve.wait_ge(sem("ld_patch"), 16)
            pl = patch_i.rearrange("p b c -> p (b c)")
            ts(parts_i[:, 0, :], pl, 2047, ALU.bitwise_and)
            ts(parts_i[:, 1, :], pl, 11, ALU.logical_shift_right, 2047, ALU.bitwise_and)
            step(ts(parts_i[:, 2, :], pl, 22, ALU.logical_shift_right, 1023, ALU.bitwise_and))
            step(dve.tensor_copy(parts_f, parts_i.rearrange("p a b -> p (a b)")))
            dve.wait_ge(sem("const_p"), 1)
            dve.tensor_tensor_scan(scan, reset, parts_f, 0.0, ALU.mult, ALU.add).then_inc(sem("scan_ready"), 1)
            ts(iotap[:, 1:2], iotap_i[:, 0:1], 1.0, ALU.add)
            dve.tensor_copy(iota8, iota16_i[:, 0:8])
            ts(iota16, iota16_i[:, 0:16], 1.0, ALU.add)
            dve.wait_ge(sem("prefix_ps"), 1)
            dve.wait_ge(sem("scan_ready"), 1)
            step(tt(cum_i.rearrange("p a (b c) -> p (a b) c", c=NCH), scan.rearrange("p (a c) -> p a c", c=NCH),
                    bc(bank(1)[:, 0:12], 2, NCH), ALU.add))
            P = [pint[:, i, :] for i in range(12)]
            step(ts(P[0], cum_i[:, 0, :], 2047.0, ALU.add))
            step(ts(P[1], P[0], 11, ALU.logical_shift_right))
            step(stt(P[2], cum_i[:, 1, :], 2047.0, P[1], ALU.add, ALU.add))
            step(ts(P[3], P[2], 11, ALU.logical_shift_right))
            step(stt(P[4], cum_i[:, 2, :], 1023.0, P[3], ALU.add, ALU.add))
            ts(P[5], P[0], 1920, ALU.bitwise_and)
            ts(P[6], P[2], 2047, ALU.bitwise_and)
            ts(P[7], P[4], 1023, ALU.bitwise_and)
            ts(P[8], P[0], 15, ALU.bitwise_and)
            step(ts(P[9], P[0], 4, ALU.logical_shift_right, 7, ALU.bitwise_and))
            step(tt(pflt[:, 0, :], P[5], P[6], ALU.add))
            step(tt(pflt[:, 0, :], pflt[:, 0, :], P[7], ALU.add))
            step(ts(pflt[:, 1, :], pflt[:, 0, :], 0.0, ALU.is_equal))
            step(stt(pflt[:, 1, :], pflt[:, 0, :], float(1920 + 2047 + 1023), pflt[:, 1, :], ALU.is_equal, ALU.add))
            step(stt(pflt[:, 2, :], P[8], 1.0, pflt[:, 1, :], ALU.add, ALU.mult))
            step(dve.tensor_copy(pflt[:, 3, :], P[9]))
            tt(lo_oh, bc(pflt[:, 2, :], 2, 16), bc(iota16, 1, 64), ALU.is_equal)
            tt(hi_oh, bc(pflt[:, 3, :], 2, 8), bc(iota8, 1, 64), ALU.is_equal).then_inc(sem("onehot_ready"), 1)
            dve.wait_ge(sem("count_ps"), 1)
            ts(bnd[0:8], bank(1)[0:8, 64:128].rearrange("p (b l) -> p b l", b=B), 1.0, ALU.min)\
                .then_inc(sem("bnd_ready"), 1)
            dve.wait_ge(sem("ld_x"), 16)
            moments(xs[0])
            v, r, t = small[:, 0, 0:B], small[:, 1, 0:B], small[:, 2, 0:B]
            v2, r2 = small[:, 3, 0:B], small[:, 4, 0:B]
            step(ts(v, var, LN_EPS, ALU.add))
            rsqrt(r, v, t)
            step(tt(v2, var, r, ALU.mult))
            step(tt(v2, v2, r, ALU.mult))
            step(ts(v2, v2, RMS_EPS, ALU.add))
            rsqrt(r2, v2, t)
            step(tt(r2, r2, r, ALU.mult))
            for b in range(B):
                ins = ts(y[:, b, :], xs[0][:, b, :], mean(b), ALU.subtract, r2[:, b:b + 1], ALU.mult)
            ins.then_inc(sem("y_ready"), 1)
            dve.wait_ge(sem("w_inT_ps"), 1)
            ts(w_inT, bank(0)[:, 0:D], biases[:, 0:1], ALU.mult).then_inc(sem("w0T_ready"), 1)
            dve.wait_ge(sem("ssq_ready"), 1)
            dve.wait_ge(sem("ld_s0"), ndma["ld_s0"])
            v5, r5 = small[:, 5, 0:B], small[:, 6, 0:B]
            step(ts(v5, small[:, 7, 0:B], 1.0 / DC, ALU.mult, RMS_EPS, ALU.add))
            rsqrt(r5, v5, t)
            step(ts(r5, r5, BCOEF, ALU.mult))
            for b in range(B):
                ins = stt(u0[:, b, :], c0[:, b, 0:D], r5[:, b:b + 1], ginit_bc, ALU.mult, ALU.mult)
            step(ins)
            dve.wait_ge(sem("bd_ps"), 1)
            dve.wait_ge(sem("const_b"), 1)
            tt(bdT, bank(5).rearrange("p (a b) -> p a b", a=4),
               bc(blk16.rearrange("p a b -> p (a b)"), 1, 4), ALU.mult).then_inc(sem("bd_ready"), 1)
            dve.wait_ge(sem("yT_ps"), 1)
            dve.tensor_copy(r0T, bank(3)).then_inc(sem("r0T_ready"), 1)
            x01 = xs[1][:].rearrange("p b d -> p (b d)")
            dve.wait_ge(sem("plug_ps"), 1)
            fl = lambda a: a.rearrange("p b s -> p (b s)")
            step(ts(fl(t0), bank(2), 1.0, ALU.max, iotap[:, 1:2], ALU.subtract))
            ts(fl(e0), fl(t0), 0.0, ALU.max).then_inc(sem("plug_ready"), 1)
            dve.wait_ge(sem("pw_ready"), 1)
            stt(fl(wt0), fl(t0), 0.0, fl(e0), ALU.is_ge, ALU.mult).then_inc(sem("wt0_ready"), 1)
            dve.wait_ge(sem("s0_ps"), 1)
            step(tt(x01, xs[0][:].rearrange("p b d -> p (b d)"), bank(4), ALU.add))
            dve.wait_ge(sem("s0_ps"), 2)
            tt(x01, x01, bank(2), ALU.add).then_inc(sem("x_ready"), 1)

            dve.wait_ge(sem("x_ready"), 1)
            layernorm(1)
            yT_copy(1)
            dve.wait_ge(sem("logit_ps"), 1)
            lg = route_s[:, 5, 0:B * E1].rearrange("p (b e) -> p b e", b=B)
            step(dve.tensor_copy(lg, bank(0)[:, 0:B * E1].rearrange("p (b e) -> p b e", b=B)))
            rank1 = route(1, TOPK1, E1, lg, True, cmp[:, :, 0:E1, 0:E1].rearrange("p b e f -> p b e f"))
            dve.wait_ge(sem("qk1_sb"), 1)
            tt(q1, q1, bank(2), ALU.mult).then_inc(sem("k1_ready"), 1)

            def k1_product(e):
                dve.wait_ge(sem("qk1_sb"), e + 2)
                tt(k32[e % 2], k32[e % 2], bank(5 + 2 * (e % 2)), ALU.mult).then_inc(sem("k1_ready"), 1)

            for e in range(E1):
                k1_product(e)
                if e == 0:
                    dve.wait_ge(sem("rT_ps"), 1)
                    dve.tensor_copy(rT_sb[0:E1, :], bank(0)[0:E1, :]).then_inc(sem("rT_ready"), 1)
                b, g = divmod(e, 2)
                dve.wait_ge(sem("v1_hi"), e + 1)
                vals = v1[:, b, 4 * g:4 * g + 4, :, :].rearrange("p e h v -> p (e h) v")
                tt(vals[:, :, DK1:2 * DK1], bank(1 + e % 2).rearrange("p (a v) -> p a v", v=DK1), vals[:, :, 0:DK1],
                   ALU.subtract).then_inc(sem("v1_ready"), 1)
                dve.wait_ge(sem("g_ps"), e + 1)
                for b in range(B):
                    ins = stt(gmask[:, e, b, :], bank(0 if e % 2 else 3)[:, b * S:(b + 1) * S], rank1[:, b, e:e + 1],
                              causal[:], ALU.mult, ALU.mult)
                ins.then_inc(sem("g_ready"), 1)
                if e == 1:
                    dve.wait_ge(sem("q1_hi"), 1)
                    tt(q1_lo, q1, q1_hi, ALU.subtract).then_inc(sem("q1_lo"), 1)
                if e == 2:
                    dve.wait_ge(sem("q1_lo"), 1)
                    for src, dst in ((q1_hi, qbd_hi), (q1_lo, qbd_lo)):
                        for h in range(H1):
                            ins = ts(dst[:, :, h, :], src.rearrange("p (b s) -> p b s", b=B), blk16[:, h, 0:1],
                                     ALU.mult)
                    ins.then_inc(sem("qbd_ready"), 1)
            dve.wait_ge(sem("g_ready"), E1)

            def am_product(i):
                b, e = divmod(i, E1)
                lo = (0, 2, 5)[i % 3]
                dve.wait_ge(sem("sc1_ps"), i + 1)
                if i >= 3:
                    dve.wait_ge(sem("am_lo_pool"), i - 2)
                    dve.wait_ge(sem("am_lo_dve"), i - 2)
                tt(am[i % 3], ps[:, lo:lo + 2, :].rearrange("p a (h s) -> p (a h) s", h=4),
                   bc(gmask[:, e, b, :], 1, H1), ALU.mult).then_inc(sem("am_ready"), 1)

            def am_rest(i):
                dve.wait_ge(sem("am_hi_ready"), i + 1)
                tt(am_lo[i % 4][:, HP1:, :], am[i % 3][:, HP1:, :], am_hi[i % 4][:, HP1:, :], ALU.subtract)\
                    .then_inc(sem("am_lo_dve"), 1)

            am_product(0)
            for i in range(B * E1):
                if i + 1 < B * E1:
                    am_product(i + 1)
                am_rest(i)
            dve.wait_ge(sem("o1_ps"), B * E1)
            o1v = o1.rearrange("p (a h v) -> p a h v", a=B, v=DK1)
            for i in range(2):
                dve.wait_ge(sem("o1_lo"), i + 1)
                src = bank(4 + 3 * i).rearrange("p (a h v) -> p a h v", a=2, v=2 * DK1)
                ins = tt(o1v[:, 2 * i:2 * i + 2], src[:, :, :, 0:DK1], o1v[:, 2 * i:2 * i + 2], ALU.add)
            step(ins)
            step(tt(q1, o1, o1, ALU.mult))
            hs, hr, ht = small[:, 5, 0:B * H1], small[:, 6, 0:B * H1], small[:, 7, 0:B * H1]
            step(dve.tensor_reduce(hs, q1.rearrange("p (h v) -> p h v", v=DK1), AX.X, ALU.add))
            step(ts(hs, hs, 1.0 / DK1, ALU.mult, LN_EPS, ALU.add))
            rsqrt(hr, hs, ht)
            tt(y.rearrange("p b d -> p (b d)").rearrange("p (h v) -> p h v", v=DK1),
               o1.rearrange("p (h v) -> p h v", v=DK1), bc(hr, 2, DK1), ALU.mult).then_inc(sem("z1_ready"), 1)
            dve.wait_ge(sem("z1T_ps"), 1)
            dve.tensor_copy(yT, bank(5)).then_inc(sem("z1T_ready"), 1)
            dve.wait_ge(sem("ld_f0"), ndma["ld_f0"])
            stt(kk_nat[0:E2, 1, :], kk_nat[0:E2, 0, :], 2.0, kk_nat[0:E2, 1, :], ALU.mult, ALU.add)\
                .then_inc(sem("kk_ready"), 1)
            dve.wait_ge(sem("s1_ps"), 1)
            tt(xs[2][:].rearrange("p b d -> p (b d)"), xs[1][:].rearrange("p b d -> p (b d)"), bank(6), ALU.add)\
                .then_inc(sem("x_ready"), 1)

            dve.wait_ge(sem("x_ready"), 2)
            layernorm(2)
            dve.wait_ge(sem("keysT_ps"), 1)
            step(dve.tensor_copy(keysT, bank(7)[:, 0:2 * E2].rearrange("p (a e) -> p a e", a=2)))
            dve.tensor_copy(b1T, bank(7)[:, 64:64 + FT2 * E2].rearrange("p (a e) -> p a e", a=FT2))
            step(stt(keysT[:, 0, :], keysT[:, 0, :], -1.0, keysT[:, 0, :], ALU.mult, ALU.mult))
            dve.sem_inc(sem("keysT_ready"), 1)
            def w1T_rest(e):
                dve.wait_ge(sem("w1T_hi"), e + 1)
                tt(w1T_lo[e % 2], bank(4), w1T_hi[e % 2], ALU.subtract).then_inc(sem("w1T_ready"), 1)

            def w2T_rest(e):
                dve.wait_ge(sem("w2T_hi"), e + 1)
                tt(w2T_lo[e % 2], bank(5), w2T_hi[e % 2], ALU.subtract).then_inc(sem("w2T_ready"), 1)

            w1T_rest(0)
            w2T_rest(0)
            yT_copy(2)
            dve.wait_ge(sem("y2_hi"), 1)
            dve.wait_ge(sem("yT_ready"), 2)
            tt(y2_lo, yT, y2_hi, ALU.subtract).then_inc(sem("y2_lo"), 1)
            dve.wait_ge(sem("logit_ps"), 2)
            lg = route_s[:, 5, 0:B * E2].rearrange("p (b e) -> p b e", b=B)
            step(tt(lg, bank(7)[:, 256:256 + B * E2].rearrange("p (b e) -> p b e", b=B), bc(small[:, 3, 0:B], 2, E2),
                    ALU.subtract))
            step(tt(lg, lg, bc(bank(7)[:, 384:384 + E2], 1, B), ALU.add))
            route(2, TOPK2, E2, lg, False, cmp, lambda: w1T_rest(1))
            dve.wait_ge(sem("rT_ps"), 2)
            dve.tensor_copy(rT_sb[0:E2, :], bank(6)[0:E2, :]).then_inc(sem("rT_ready"), 1)
            dve.wait_ge(sem("b2_ps"), 1)
            acc = xs[0]
            tt(acc[:].rearrange("p b d -> p (b d)"), xs[2][:].rearrange("p b d -> p (b d)"), bank(7), ALU.add)\
                .then_inc(sem("acc0_start"), 1)

            def gather_expert(acc, w, bk):
                for b in range(B):
                    ins = stt(acc[:, b, :], bank(bk)[:, b * D:(b + 1) * D], w[:, b, :], acc[:, b, :],
                              ALU.mult, ALU.add)
                return ins

            dve.wait_ge(sem("acc0_start"), 1)
            for e in range(E2 + 1):
                if e == 8:
                    dve.wait_ge(sem("w3_split"), 1)
                    step(dve.tensor_reduce(wn[:], wq_nk, AX.X, ALU.add))
                    ts(wn[:], wn[:], DH3 ** -0.5, ALU.mult).then_inc(sem("wn_ready"), 1)
                if 1 <= e < E2 - 1:
                    w1T_rest(e + 1)
                if e < E2:
                    for t_ in range(FT2):
                        k = FT2 * e + t_
                        dve.wait_ge(sem("h2_hi"), k + 1)
                        tt(h2_lo[e % 2][:, t_, :], h2_32[k % 4], h2_hi[e % 2][:, t_, :], ALU.subtract)\
                            .then_inc(sem("h2_ready"), 1)
                if e >= 1:
                    dve.wait_ge(sem("down0_ps"), e)
                    if e >= 2:
                        dve.wait_ge(sem("acc0_ready"), e - 1)
                    gather_expert(acc, wgt[:, :, e - 1:e], 6 + (e - 1) % 2).then_inc(sem("acc0_ready"), 1)
                if e + 1 < E2:
                    w2T_rest(e + 1)
            dve.wait_ge(sem("acc0_ready"), E2)
            dve.sem_inc(sem("x_ready"), 1)

            layernorm(3)
            tiles = [0]

            def split_lo(dst, bk, hi):
                tiles[0] += 1
                dve.wait_ge(sem("tile_hi"), tiles[0])
                tt(dst, bk, hi, ALU.subtract).then_inc(sem("tile_lo"), 1)

            def ctx_lo(i, bk=6):
                b, c = divmod(2 * i, NCH)
                o = (slice(None), slice(None), slice(c * 128, (c + 2) * 128))
                split_lo(cT_lo[b % 2][o], bank(bk).rearrange("p (t s) -> p t s", t=CT), cT_hi[b % 2][o])

            def v_lo(n, bk):
                g, c = divmod(n, NCH)
                v = v3[g % 2][:, c, :, :]
                split_lo(v[:, :, DH3:2 * DH3], bank(bk).rearrange("p (h d) -> p h d", h=8), v[:, :, 0:DH3])

            def q_lo_(i, bk):
                tiles[0] += 1
                dve.wait_ge(sem("tile_hi"), tiles[0])
                stt(q_lo[0:64, i, :], bank(bk)[0:64, :], DH3 ** -0.5, q_hh[0:64, 2 * i, :], ALU.mult, ALU.subtract)
                stt(q_lo[64:128, i, :], bank(bk)[64:128, :], DH3 ** -0.5, q_hh[64:128, 2 * i + 1, :], ALU.mult,
                    ALU.subtract).then_inc(sem("tile_lo"), 1)

            def k_lo(m, bk):
                p, j = divmod(m, 4)
                tiles[0] += 1
                dve.wait_ge(sem("tile_hi"), tiles[0])
                k = k3[p % 2][:, :, j * 512:(j + 1) * 512]
                tt(k[64:128, 0, :], bank(bk)[0:64, :], k[0:64, 0, :], ALU.subtract)
                tt(k[0:64, 1, :], bank(bk)[64:128, :], k[64:128, 1, :], ALU.subtract).then_inc(sem("tile_lo"), 1)

            def pT_lo_(u, g):
                split_lo(pT_lo[:, 4 * g:4 * g + 4, :].rearrange("p a b -> p (a b)"), bank(t_bank(u, g)),
                         pT_hi[:, 4 * g:4 * g + 4, :].rearrange("p a b -> p (a b)"))

            us = lambda u, i: unit_s[:, u % 2, i:i + 1]

            def max_a(u):
                dve.wait_ge(sem("s3_ps"), 2 * u + 1)
                dve.tensor_reduce(us(u, 0), ps[:, 0:2, :], AX.XY, ALU.max, negate=True).then_inc(sem("max_part"), 1)

            def max_b(u):
                b, h = divmod(u, H3)
                dve.wait_ge(sem("max_part"), 2 * u + 1)
                step(tt(us(u, 0), us(u, 0), nsim0[:, b, h:h + 1], ALU.min))
                dve.wait_ge(sem("s3_ps"), 2 * u + 2)
                dve.tensor_reduce(us(u, 1), ps[:, 2:4, :], AX.XY, ALU.max, negate=True).then_inc(sem("max_part"), 1)
                dve.wait_ge(sem("max_part"), 2 * u + 2)
                stt(us(u, 2), us(u, 1), us(u, 0), lift[:], ALU.min, ALU.add).then_inc(sem("nmax_ready"), 1)

            def head_out(u):
                b, h = divmod(u, H3)
                dve.wait_ge(sem("p0_ready"), u + 1)
                dve.wait_ge(sem("pv_ps"), u + 1)
                if h == 0 and b >= 1:
                    dve.wait_ge(sem("oT_ps"), 2 * b)
                z = zat[:, h * DH3:(h + 1) * DH3]
                step(stt(z, nv_bc[:], p03[:, b % 2, h:h + 1], bank(7)[:, 0:DH3], ALU.mult, ALU.add))
                tt(z, z, bank(7)[:, DH3:2 * DH3], ALU.add).then_inc(sem("o_head"), 1)

            def heads_norm(b):
                dve.wait_ge(sem("o_head"), H3 * (b + 1))
                sums = sums3[:, b % 2, :]
                step(tt(sums, sums, p03[:, b % 2, :], ALU.add))
                step(dve.reciprocal(sums, sums))
                zv = zat[:].rearrange("p (h d) -> p h d", h=H3)
                tt(zv, zv, bc(sums, 2, DH3), ALU.mult).then_inc(sem("z3_ready"), 1)

            def out3(b):
                dve.wait_ge(sem("o3_ps"), b + 1)
                dve.tensor_copy(xs[1][:, b, :], bank(7)[:, 0:D]).then_inc(sem("o3_ready"), 1)

            for i in range(8):
                ctx_lo(i, pro_bank(i))
            for m in range(4):
                v_lo(m, pro_bank(8 + m))
            yT_copy(3)
            q_lo_(0, pro_bank(12))
            dve.wait_ge(sem("sim0_ps"), 1)
            s0v = bank(3)[:, 0:B * H3].rearrange("p (b h) -> p b h", b=B)
            dve.tensor_copy(sim0[:], s0v)
            ts(nsim0[:], s0v, -1.0, ALU.mult).then_inc(sem("sim0_ready"), 1)
            for j in range(4):
                k_lo(j, pro_bank(13 + j))
            for i in range(1, H3 // 2):
                v_lo(3 + i, pro_bank(15 + 2 * i))
                q_lo_(i, pro_bank(16 + 2 * i))
            for m in range(11, NCH):
                v_lo(m, pro_bank(20 + m))
            NU = B * H3
            for u in range(NU + 1):
                b, h = divmod(u, H3)
                new, old = u < NU, u >= 1
                if old:
                    pT_lo_(u - 1, 0)
                    pT_lo_(u - 1, 1)
                if new:
                    max_a(u)
                if h == 1 and b >= 1:
                    out3(b - 1)
                if old:
                    pT_lo_(u - 1, 2)
                if new:
                    max_b(u)
                if old:
                    pT_lo_(u - 1, 3)
                n_k = 4 + 2 * u
                more_k = n_k < 4 * B * H3 // 2
                sa, sc = swing(u)
                if more_k:
                    k_lo(n_k, sc)
                n_v = NCH + 2 * u
                more_v = n_v < 2 * B * NCH
                if more_k and not more_v:
                    k_lo(n_k + 1, 5)
                if old:
                    head_out(u - 1)
                    if h == 0:
                        heads_norm(b - 1)
                if more_v:
                    v_lo(n_v, 5)
                if more_k and more_v:
                    k_lo(n_k + 1, sa)
                if more_v:
                    v_lo(n_v + 1, 7)
                if new and b + 1 < B and h < 8:
                    ctx_lo(8 * (b + 1) + h, 3)
            out3(B - 1)
            dve.wait_ge(sem("o3_ready"), B)
            o3 = xs[1]
            moments(o3)
            step(ts(v, var, XLN_EPS, ALU.add))
            rsqrt(r, v, t)
            for b in range(B):
                ins = ts(o3[:, b, :], o3[:, b, :], mean(b), ALU.subtract, r[:, b:b + 1], ALU.mult)
            step(ins)
            step(tt(o3[:], o3[:], bc(lns_bc[:, 0, :], 1, B), ALU.mult))
            step(tt(o3[:], o3[:], bc(lns_bc[:, 1, :], 1, B), ALU.add))
            tt(o3[:], o3[:], xs[0][:], ALU.add).then_inc(sem("x_ready"), 1)

            dve.wait_ge(sem("x_ready"), 4)
            layernorm(4)
            yT_copy(4)
            dve.wait_ge(sem("qk4_ps"), 1)
            ts(qT4, bank(0), biases[:, 2:3], ALU.add, DH4 ** -0.5, ALU.mult)
            ts(kT4, bank(1), biases[:, 3:4], ALU.add).then_inc(sem("qk4_sb"), 1)
            dve.wait_ge(sem("qk4_hi"), 1)
            dve.wait_ge(sem("qk4_sb"), 1)
            tt(k4_lo, kT4, k4_hi, ALU.subtract)
            tt(q4_lo, qT4, q4_hi, ALU.subtract).then_inc(sem("qk4_lo"), 1)
            dve.wait_ge(sem("const_c"), 1)

            def kb4(i):
                b, g = divmod(i, 4)
                if i >= 3:
                    dve.wait_ge(sem("s4_ps"), i - 2)
                tt(kb_hi[i % 3], bc(k4_hi[:, b * S:(b + 1) * S], 1, 4), m16[:, 4 * g:4 * g + 4, :], ALU.mult)\
                    .then_inc(sem("kb_hi_ready"), 1)

            def max4(i):
                dve.wait_ge(sem("s4_ps"), i + 1)
                if i >= 3:
                    dve.wait_ge(sem("p4_ready"), i - 2)
                step(dve.tensor_reduce(nm4[:, i % 3, :], bank((0, 1, 3)[i % 3]).rearrange("p (h s) -> p h s", h=4),
                                       AX.X, ALU.max, negate=True))
                ts(nm4[:, i % 3, :], nm4[:, i % 3, :], LIFT, ALU.add).then_inc(sem("nm4_ready"), 1)

            def p_lo4(i):
                dve.wait_ge(sem("t4_hi"), i + 1)
                fl = lambda a: a.rearrange("p a b -> p (a b)")
                tt(fl(pT4_lo[i % 3]), bank(4 + i % 2), fl(pT4_hi[i % 3]), ALU.subtract).then_inc(sem("t4_lo"), 1)

            def heads4(b):
                dve.wait_ge(sem("o4_ps"), 4 * b + 4)
                if b >= 1:
                    dve.wait_ge(sem("zT4_ps"), b)
                o4 = bank((6, 2)[b % 2])[:, 0:H4 * 18].rearrange("p (h v) -> p h v", h=H4)
                z = z4.rearrange("p (h v) -> p h v", h=H4)
                step(dve.reciprocal(rs4, o4[:, :, DH4]))
                step(tt(z, o4[:, :, 0:DH4], bc(rs4, 2, DH4), ALU.mult))
                step(tt(zl4.rearrange("p (h v) -> p h v", h=H4), o4[:, :, DH4 + 1:2 * DH4 + 1], bc(rs4, 2, DH4),
                        ALU.mult))
                tt(z4, z4, zl4, ALU.add).then_inc(sem("z4_ready"), 1)

            def out4(b):
                dve.wait_ge(sem("s4o_ps"), b + 1)
                tt(xs[2][:, b, :], bank(7)[:, 128:256], xs[1][:, b, :], ALU.add).then_inc(sem("s4_out"), 1)

            kb4(0)
            for i in range(4 * B + 8):
                if i + 1 < 4 * B:
                    kb4(i + 1)
                if i < 4 * B:
                    max4(i)
                if i == 1:
                    dve.wait_ge(sem("v4_hi"), 1)
                    tt(v4[:, :, :, DH4 + 1:2 * DH4 + 1], bank(2).rearrange("p (b h v) -> p b h v", b=B, h=H4),
                       v4[:, :, :, 0:DH4], ALU.subtract).then_inc(sem("v4_ready"), 1)
                if 3 <= i < 4 * B + 3:
                    p_lo4(i - 3)
                if i >= 8 and i % 4 == 0:
                    heads4(i // 4 - 2)
                if i >= 11 and i % 4 == 3:
                    out4(i // 4 - 2)
            dve.wait_ge(sem("s4_out"), B)
            dve.sem_inc(sem("x_ready"), 1)

            layernorm(5)
            yT_copy(5)
            dve.wait_ge(sem("y5_hi"), 1)
            dve.wait_ge(sem("yT_ready"), 5)
            tt(y5_lo, yT, y5_hi, ALU.subtract).then_inc(sem("y5_lo"), 1)
            dve.wait_ge(sem("logit_ps"), 3)
            lg = route_s[:, 5, 0:B * E5].rearrange("p (b e) -> p b e", b=B)
            step(dve.tensor_copy(lg, bank(0)[:, 0:B * E5].rearrange("p (b e) -> p b e", b=B)))
            dve.sem_inc(sem("l5_ready"), 1)
            route(5, TOPK5, E5, lg, True, cmp5)
            acc = xs[0]
            step(dve.tensor_copy(acc[:], xs[2][:]))
            for e in range(E5 + 1):
                for t_ in range(FT5):
                    k = FT5 * e + t_
                    if e < E5:
                        dve.wait_ge(sem("silu_done"), k + 1)
                        if k >= 4:
                            dve.wait_ge(sem("h5_ready"), k - 3)
                        tt(h5_32[k % 4], sg[k % 2], bank(2 * (k % 3) + 1), ALU.mult).then_inc(sem("h5_product"), 1)
                    if 1 <= k <= E5 * FT5:
                        e_, q_ = divmod(k - 1, FT5)
                        dve.wait_ge(sem("h5_hi"), k)
                        tt(h5_lo[e_ % 2][:, q_, :], h5_32[(k - 1) % 4], h5_hi[e_ % 2][:, q_, :], ALU.subtract)\
                            .then_inc(sem("h5_ready"), 1)
                    if e >= 1 and t_ == 3:
                        dve.wait_ge(sem("f1_used"), e)
                        if e >= 2:
                            dve.wait_ge(sem("acc5_ready"), e - 1)
                        if e == 1:
                            dve.wait_ge(sem("w_ready"), 3)
                        gather_expert(acc, wgt[:, :, e - 1:e], 6 + (e - 1) % 2).then_inc(sem("acc5_ready"), 1)
            dve.wait_ge(sem("acc5_ready"), E5)
            dve.sem_inc(sem("x_ready"), 1)

        @block.scalar
        def _(act):
            def copy(o, i, scale=1.0):
                return act.activation(o, i, ACT.Copy, scale=scale)

            act.wait_ge(sem("ld_c0"), 16)
            for b in range(B):
                if b:
                    act.wait_ge(sem("ssq_b"), b)
                ins = act.activation(sq_junk, c0[:, b, :], ACT.Square, accum_out=small[:, 7, b:b + 1])
                ins.then_inc(sem("ssq_b") if b < B - 1 else sem("ssq_ready"), 1)
            act.wait_ge(sem("plug_ready"), 1)
            e0f = e0.rearrange("p b s -> p (b s)")
            act.activation(e0f, e0f, ACT.Exp, scale=-DT).then_inc(sem("pw_ready"), 1)
            act.wait_ge(sem("og_ps"), 1)
            act.activation(o_wT, bank(6)[:, 0:D], ACT.Copy, scale=biases[:, 1:2])
            copy(gateT, bank(6)[:, D:D + E1]).then_inc(sem("og_ready"), 1)
            act.wait_ge(sem("mq_ps"), 1)
            act.activation(mqT[:, 0, :], bank(7)[:, 0:D], ACT.Copy, scale=DK1 ** -0.5)
            copy(mqT[:, 1, :], bank(7)[:, D:2 * D]).then_inc(sem("mq_ready"), 1)
            for i in range(4):
                act.wait_ge(sem("mk_ps"), i + 1)
                copy(mkT[:, 2 * i:2 * i + 2, :, :].rearrange("p a b c -> p (a b c)"), bank(5 + i % 2))\
                    .then_inc(sem("mk_ready"), 1)
            for g in range(2):
                act.wait_ge(sem("vw_ps"), g + 1)
                copy(v_wT[:, 4 * g:4 * g + 4, :].rearrange("p a b -> p (a b)"), bank(5 + g)).then_inc(sem("vw_ready"), 1)

            def route_exp(k, E):
                act.wait_ge(sem("route_d"), k)
                act.activation(route_s[:, 2, 0:B * E], route_s[:, 1, 0:B * E], ACT.Exp).then_inc(sem("route_e"), 1)

            route_exp(1, E1)
            act.wait_ge(sem("qk_ps"), 1)
            copy(q1, bank(1)).then_inc(sem("qk1_sb"), 1)

            def k1_hi(e):
                act.wait_ge(sem("k1_ready"), e + 2)
                copy(kT1_hi[:, e, :], k32[e % 2]).then_inc(sem("k1_hi"), 1)

            for e in range(E1):
                act.wait_ge(sem("qk_ps"), e + 2)
                if e >= 2:
                    act.wait_ge(sem("k1_lo"), e - 1)
                copy(k32[e % 2], bank(4 + 2 * (e % 2))).then_inc(sem("qk1_sb"), 1)
                if e == 0:
                    act.wait_ge(sem("k1_ready"), 1)
                    copy(q1_hi, q1).then_inc(sem("q1_hi"), 1)
                b, g = divmod(e, 2)
                act.wait_ge(sem("v1_ps"), e + 1)
                copy(v1[:, b, 4 * g:4 * g + 4, :, 0:DK1].rearrange("p e h v -> p (e h) v"),
                     bank(1 + e % 2).rearrange("p (a v) -> p a v", v=DK1)).then_inc(sem("v1_hi"), 1)
                k1_hi(e)
            for i in range(B * E1):
                act.wait_ge(sem("am_ready"), i + 1)
                if i >= 4:
                    act.wait_ge(sem("o1_ps"), i - 3)
                copy(am_hi[i % 4], am[i % 3]).then_inc(sem("am_hi_ready"), 1)
            o1v = o1.rearrange("p (a h v) -> p a h v", a=B, v=DK1)
            for i in range(2):
                act.wait_ge(sem("o1_ps"), (i + 1) * 2 * E1)
                copy(o1v[:, 2 * i:2 * i + 2], bank(4 + 3 * i).rearrange("p (a h v) -> p a h v", a=2, v=2 * DK1)
                     [:, :, :, DK1:]).then_inc(sem("o1_lo"), 1)

            def w1T_high(e):
                act.wait_ge(sem("w1T_ps"), e + 1)
                copy(w1T_hi[e % 2], bank(4)).then_inc(sem("w1T_hi"), 1)

            def w2T_high(e):
                act.wait_ge(sem("f0_turned"), e + 1)
                copy(w2T_hi[e % 2], bank(5)).then_inc(sem("w2T_hi"), 1)

            def h2_high(k):
                e, t = divmod(k, FT2)
                act.wait_ge(sem("gelu_done"), k + 1)
                copy(h2_hi[e % 2][:, t, :], h2_32[k % 4]).then_inc(sem("h2_hi"), 1)

            w1T_high(0)
            w2T_high(0)
            act.wait_ge(sem("yT_ready"), 2)
            copy(y2_hi, yT).then_inc(sem("y2_hi"), 1)
            for e in range(E2):
                if e + 1 < E2:
                    w1T_high(e + 1)
                if e == 0:
                    route_exp(2, E2)
                for t in range(FT2):
                    k = FT2 * e + t
                    act.wait_ge(sem("up0_ps"), k + 1)
                    if k >= 4:
                        act.wait_ge(sem("h2_ready"), k - 3)
                    if t == 0 and e >= 2:
                        act.wait_ge(sem("down0_ps"), e - 1)
                    act.activation(h2_32[k % 4], bank(k % 4), ACT.Gelu, bias=b1T[:, t, e:e + 1])\
                        .then_inc(sem("gelu_done"), 1)
                    if t >= 1:
                        h2_high(k - 1)
                h2_high(k)
                if e + 1 < E2:
                    w2T_high(e + 1)

            tiles = [0]

            def split_hi(dst, bk):
                tiles[0] += 1
                act.wait_ge(sem("tile_full"), tiles[0])
                copy(dst, bk).then_inc(sem("tile_hi"), 1)

            def ctx_hi(i, bk=6):
                b, c = divmod(2 * i, NCH)
                split_hi(cT_hi[b % 2][:, :, c * 128:(c + 2) * 128], bank(bk).rearrange("p (t s) -> p t s", t=CT))

            def v_hi(n, bk):
                g, c = divmod(n, NCH)
                split_hi(v3[g % 2][:, c, :, 0:DH3], bank(bk).rearrange("p (h d) -> p h d", h=8))

            def q_hi(i, bk):
                tiles[0] += 1
                act.wait_ge(sem("tile_full"), tiles[0])
                copy(q_hh[0:64, 2 * i, :], bank(bk)[0:64, :], DH3 ** -0.5)
                copy(q_hh[64:128, 2 * i + 1, :], bank(bk)[64:128, :], DH3 ** -0.5).then_inc(sem("tile_hi"), 1)

            def k_hi(m, bk):
                p, j = divmod(m, 4)
                tiles[0] += 1
                act.wait_ge(sem("tile_full"), tiles[0])
                k = k3[p % 2][:, :, j * 512:(j + 1) * 512]
                copy(k[0:64, 0, :], bank(bk)[0:64, :])
                copy(k[64:128, 1, :], bank(bk)[64:128, :]).then_inc(sem("tile_hi"), 1)

            def pT_hi_(u, g):
                split_hi(pT_hi[:, 4 * g:4 * g + 4, :].rearrange("p a b -> p (a b)"), bank(t_bank(u, g)))

            us = lambda u, i: unit_s[:, u % 2, i:i + 1]

            def exps(u):
                b, h = divmod(u, H3)
                act.wait_ge(sem("nmax_ready"), u + 1)
                act.activation(p3[u % 2], ps[:, 0:4, :].rearrange("p a b -> p (a b)"), ACT.Exp, bias=us(u, 2),
                               accum_out=sums3[:, b % 2, h:h + 1]).then_inc(sem("exp_done"), 1)
                act.activation(p03[:, b % 2, h:h + 1], sim0[:, b, h:h + 1], ACT.Exp, bias=us(u, 2))\
                    .then_inc(sem("p0_ready"), 1)

            def heads_copy(b, i):
                act.wait_ge(sem("oT_ps"), 2 * b + i + 1)
                copy(oT3[:, 4 * i:4 * i + 4, :].rearrange("p a b -> p (a b)"), bank(6 - i))\
                    .then_inc(sem("oT_ready"), 1)

            for i in range(8):
                ctx_hi(i, pro_bank(i))
            for m in range(4):
                v_hi(m, pro_bank(8 + m))
            q_hi(0, pro_bank(12))
            for j in range(4):
                k_hi(j, pro_bank(13 + j))
            for i in range(1, H3 // 2):
                v_hi(3 + i, pro_bank(15 + 2 * i))
                q_hi(i, pro_bank(16 + 2 * i))
            for m in range(11, NCH):
                v_hi(m, pro_bank(20 + m))
            NU = B * H3
            for u in range(NU + 1):
                b, h = divmod(u, H3)
                new, old = u < NU, u >= 1
                if h == 1 and b >= 1:
                    heads_copy(b - 1, 0)
                    heads_copy(b - 1, 1)
                if old:
                    pT_hi_(u - 1, 0)
                    pT_hi_(u - 1, 1)
                    pT_hi_(u - 1, 2)
                    pT_hi_(u - 1, 3)
                n_k = 4 + 2 * u
                more_k = n_k < 4 * B * H3 // 2
                sa, sc = swing(u)
                n_v = NCH + 2 * u
                more_v = n_v < 2 * B * NCH
                if more_k:
                    k_hi(n_k, sc)
                if more_k and not more_v:
                    k_hi(n_k + 1, 5)
                if new:
                    exps(u)
                if more_v:
                    v_hi(n_v, 5)
                if more_k and more_v:
                    k_hi(n_k + 1, sa)
                if more_v:
                    v_hi(n_v + 1, 7)
                if new and b + 1 < B and h < 8:
                    ctx_hi(8 * (b + 1) + h, 3)
            for i in range(2):
                heads_copy(B - 1, i)

            act.wait_ge(sem("qk4_sb"), 1)
            copy(k4_hi, kT4)
            copy(q4_hi, qT4).then_inc(sem("qk4_hi"), 1)
            act.wait_ge(sem("v4_ps"), 1)
            act.wait_ge(sem("const_c"), 1)
            copy(v4[:, :, :, 0:DH4], bank(2).rearrange("p (b h v) -> p b h v", b=B, h=H4)).then_inc(sem("v4_hi"), 1)

            def exp4(i):
                act.wait_ge(sem("nm4_ready"), i + 1)
                if i >= 3:
                    act.wait_ge(sem("t4_full"), i - 2)
                for j in range(4):
                    ins = act.activation(p4[i % 3][:, j, :], bank((0, 1, 3)[i % 3])[:, j * S:(j + 1) * S], ACT.Exp,
                                         bias=nm4[:, i % 3, j:j + 1])
                ins.then_inc(sem("p4_ready"), 1)

            def p_hi4(i):
                act.wait_ge(sem("t4_full"), i + 1)
                if i >= 3:
                    act.wait_ge(sem("o4_ps"), i - 2)
                copy(pT4_hi[i % 3].rearrange("p a b -> p (a b)"), bank(4 + i % 2)).then_inc(sem("t4_hi"), 1)

            for i in range(4 * B + 6):
                if 2 <= i < 4 * B + 2:
                    p_hi4(i - 2)
                if i < 4 * B:
                    exp4(i)
                if i >= 9 and i % 4 == 1:
                    b = i // 4 - 2
                    act.wait_ge(sem("zT4_ps"), b + 1)
                    if b >= 1:
                        act.wait_ge(sem("s4o_ps"), b)
                    copy(zT4, bank(7)[:, 0:128]).then_inc(sem("zT4_ready"), 1)

            def wg_high(e):
                act.wait_ge(sem(f"w5_{e % 2}"), 48 * (e // 2 + 1))
                if e >= 4:
                    act.wait_ge(sem("f1_used"), e - 3)
                copy(wg_hi[e % 4], wg5[e % 2]).then_inc(sem("wg_hi"), 1)

            wg_high(0)
            wg_high(1)
            act.wait_ge(sem("yT_ready"), 5)
            copy(y5_hi, yT).then_inc(sem("y5_hi"), 1)
            route_exp(3, E5)
            for k in range(E5 * FT5 + 1):
                e, t = divmod(k, FT5)
                if k < E5 * FT5:
                    act.wait_ge(sem("up5_ps"), k + 1)
                    if k >= 2:
                        act.wait_ge(sem("h5_product"), k - 1)
                    act.activation(sg[k % 2], bank(2 * (k % 3)), ACT.Silu).then_inc(sem("silu_done"), 1)
                if t == 2 and e + 2 < E5:
                    wg_high(e + 2)
                if k >= 1:
                    e, t = divmod(k - 1, FT5)
                    act.wait_ge(sem("h5_product"), k)
                    if t == 0 and e >= 2:
                        act.wait_ge(sem("f1_used"), e - 1)
                    copy(h5_hi[e % 2][:, t, :], h5_32[(k - 1) % 4]).then_inc(sem("h5_hi"), 1)


_INS = ['x', 'ctx_2048', 'mask_BxS2_if0', 'L0_xattn_W_in', 'L0_xattn_b_in', 'L0_xattn_g_res', 'L0_xattn_g_init',
        'L0_attn_gate_w', 'L0_attn_q_w', 'L0_attn_k_w', 'L0_attn_v_w', 'L0_attn_fmq1_w', 'L0_attn_fmq2_w',
        'L0_attn_fmk1_w', 'L0_attn_fmk2_w', 'L0_attn_norm_w', 'L0_attn_o_w',
        'L0_ffn_keys', 'L0_ffn_w1', 'L0_ffn_b1', 'L0_ffn_w2', 'L0_ffn_b2', 'L0_ffn_rw', 'L0_ffn_rb',
        'L1_xattn_Wq', 'L1_xattn_Wkv', 'L1_xattn_null_kv', 'L1_xattn_Wout', 'L1_xattn_ln_scale', 'L1_xattn_ln_bias',
        'L1_attn_w_qkv', 'L1_attn_b_qkv', 'L1_attn_w_proj', 'L1_attn_b_proj',
        'L1_ffn_gate_w', 'L1_ffn_w1', 'L1_ffn_w3', 'L1_ffn_w2']
_OUTS = [((4, 128, 128), 'float32')]


def kernel(**inputs):
    import numpy as _np
    import concourse.bacc as _bacc
    from concourse import mybir as _mybir
    from concourse.bass_utils import run_bass_kernel_spmd as _run

    nc = _bacc.Bacc("TRN2", target_bir_lowering=False, num_devices=1, dynamic_dma_scratch_size=1024)
    arrays, args = {}, []
    for name in _INS:
        a = _np.ascontiguousarray(inputs[name])
        arrays[f"in_{name}_dram"] = a
        args.append(nc.dram_tensor(f"in_{name}_dram", a.shape, _mybir.dt.from_np(a.dtype), kind="ExternalInput").ap())
    for i, (shape, dtype) in enumerate(_OUTS):
        dt = _mybir.dt.from_np(_np.dtype(dtype))
        args.append(nc.dram_tensor(f"out_{i}_dram", shape, dt, kind="ExternalOutput").ap())
    perceiver_kernel(nc, *args)
    r = _run(nc, [arrays], core_ids=[0])
    return r.results[0]["out_0_dram"]
```
